# Optimizing a Trainium2 kernel written in Bass

```python
import numpy as np
import jax
import jax.numpy as jnp

def _softmax(x, axis=-1):
    return jax.nn.softmax(x, axis=axis)

def _gelu(x):
    return jax.nn.gelu(x, approximate=True)

def _silu(x):
    return jax.nn.silu(x)

def _sigmoid(x):
    return jax.nn.sigmoid(x)

def _layernorm(x, axis=-1, eps=1e-05):
    m = jnp.mean(x, axis=axis, keepdims=True)
    v = jnp.var(x, axis=axis, keepdims=True)
    return (x - m) / jnp.sqrt(v + eps)

def _scatter_add(tgt, idx, src, axis=0):
    return tgt.at[idx].add(src)

def _segment_sum(src, seg, n):
    return jax.ops.segment_sum(src, seg, n)
kernel_name = 'mk_hybrid_d2_jaxref_r4_c214ca'

def setup_inputs(seed: int=0):
    np.random.seed(seed)
    _w = jnp.asarray

    def _L0_attn_a_setup():
        import jax, jax.numpy as jnp
        import numpy as np
        DIM, D_STATE, D_CONV, EXPAND = (256, 16, 4, 2)
        D_INNER = EXPAND * DIM
        DT_RANK = (DIM + 15) // 16
        B_SZ, L_SEQ = (2, 256)
        EPS = 1e-05

        def _mamba_block(x, norm_w, in_proj_w, conv_w, conv_b, x_proj_w, dt_proj_w, dt_proj_b, A_log, D_param, out_proj_w):
            xn = x * jax.lax.rsqrt(jnp.mean(x * x, axis=-1, keepdims=True) + EPS) * norm_w
            xz = jnp.einsum('bld,ed->ble', xn, in_proj_w)
            xi, z = jnp.split(xz, 2, axis=-1)
            xc = jax.lax.conv_general_dilated(xi.transpose(0, 2, 1), conv_w, window_strides=(1,), padding=[(D_CONV - 1, 0)], dimension_numbers=('NCH', 'OIH', 'NCH'), feature_group_count=D_INNER) + conv_b[None, :, None]
            u = jax.nn.silu(xc.transpose(0, 2, 1))
            x_dbl = jnp.einsum('bld,ed->ble', u, x_proj_w)
            dt, Bm, Cm = jnp.split(x_dbl, [DT_RANK, DT_RANK + D_STATE], axis=-1)
            delta = jax.nn.softplus(jnp.einsum('blr,dr->bld', dt, dt_proj_w) + dt_proj_b)
            A = -jnp.exp(A_log)

            def step(h, inp):
                delta_t, B_t, C_t, u_t = inp
                dA = jnp.exp(delta_t[..., None] * A)
                dBu = (delta_t * u_t)[..., None] * B_t[:, None, :]
                h = dA * h + dBu
                y = jnp.einsum('bds,bs->bd', h, C_t)
                return (h, y)
            h0 = jnp.zeros((x.shape[0], D_INNER, D_STATE), x.dtype)
            inputs = (delta.swapaxes(0, 1), Bm.swapaxes(0, 1), Cm.swapaxes(0, 1), u.swapaxes(0, 1))
            _, ys = jax.lax.scan(step, h0, inputs)
            y = ys.swapaxes(0, 1) + u * D_param
            y = y * jax.nn.silu(z)
            out = jnp.einsum('ble,de->bld', y, out_proj_w)
            return x + out
        key = jax.random.key(seed)
        ks = jax.random.split(key, 10)
        s_in = 1.0 / np.sqrt(DIM)
        s_xp = 1.0 / np.sqrt(D_INNER)
        s_dt = 1.0 / np.sqrt(DT_RANK)
        return {'x': jax.random.normal(ks[0], (B_SZ, L_SEQ, DIM), jnp.float32), 'norm_w': jnp.ones((DIM,), jnp.float32), 'in_proj_w': jax.random.normal(ks[1], (2 * D_INNER, DIM), jnp.float32) * s_in, 'conv_w': jax.random.normal(ks[2], (D_INNER, 1, D_CONV), jnp.float32) * 0.5, 'conv_b': jnp.zeros((D_INNER,), jnp.float32), 'x_proj_w': jax.random.normal(ks[3], (DT_RANK + 2 * D_STATE, D_INNER), jnp.float32) * s_xp, 'dt_proj_w': jax.random.normal(ks[4], (D_INNER, DT_RANK), jnp.float32) * s_dt, 'dt_proj_b': jax.random.uniform(ks[5], (D_INNER,), jnp.float32, -4.0, -1.0), 'A_log': jnp.log(jnp.tile(jnp.arange(1, D_STATE + 1, dtype=jnp.float32), (D_INNER, 1))), 'D_param': jnp.ones((D_INNER,), jnp.float32), 'out_proj_w': jax.random.normal(ks[6], (DIM, D_INNER), jnp.float32) * s_xp}
    _L0_attn_a_in = _L0_attn_a_setup()

    def _L0_attn_b_setup():
        import jax, jax.numpy as jnp
        import numpy as np
        NUM_HEADS = 16
        LORA_SCALE = 32.0 / 8.0
        ROPE_BASE = 10000.0

        def make_sincos(seq_len, dim):
            pos = jnp.arange(seq_len, dtype=jnp.float32)
            i = jnp.arange(0, dim, 2, dtype=jnp.float32) / dim
            theta = pos[:, None] / ROPE_BASE ** i[None, :]
            return (jnp.sin(theta), jnp.cos(theta))

        def apply_rope(x, sin, cos):
            x_even = x[..., 0::2]
            x_odd = x[..., 1::2]
            rot_even = x_even * cos - x_odd * sin
            rot_odd = x_even * sin + x_odd * cos
            return jnp.stack([rot_even, rot_odd], axis=-1).reshape(x.shape)
        key = jax.random.key(seed)
        ks = jax.random.split(key, 9)
        B, T, D, R = (4, 512, 256, 8)
        s = 1.0 / np.sqrt(D)
        return {'query': jax.random.normal(ks[0], (B, T, D), dtype=jnp.float32), 'wq': jax.random.normal(ks[1], (D, D), dtype=jnp.float32) * s, 'wk': jax.random.normal(ks[2], (D, D), dtype=jnp.float32) * s, 'wv': jax.random.normal(ks[3], (D, D), dtype=jnp.float32) * s, 'wo': jax.random.normal(ks[4], (D, D), dtype=jnp.float32) * s, 'Aq': jax.random.normal(ks[5], (D, R), dtype=jnp.float32) * s, 'Bq': jax.random.normal(ks[6], (R, D), dtype=jnp.float32) * 0.01, 'Av': jax.random.normal(ks[7], (D, R), dtype=jnp.float32) * s, 'Bv': jax.random.normal(ks[8], (R, D), dtype=jnp.float32) * 0.01}
    _L0_attn_b_in = _L0_attn_b_setup()

    def _L0_ffn_setup():
        import jax, jax.numpy as jnp
        import numpy as np

        def _bitlinear(x, w_latent):
            scale = jax.lax.stop_gradient(jnp.clip(jnp.mean(jnp.abs(w_latent), axis=1, keepdims=True), 1e-05, None))
            tern = jnp.clip(jnp.round(w_latent / scale), -1.0, 1.0)
            w = w_latent + jax.lax.stop_gradient(tern - w_latent)
            return x @ (w * scale).T
        key = jax.random.key(seed)
        ks = jax.random.split(key, 6)
        dim, hidden, rank = (256, 1024, 16)
        B, S = (4, 1024)
        x = jax.random.normal(ks[0], (B, S, dim), dtype=jnp.float32)
        w_fc = 0.02 * jax.random.normal(ks[1], (hidden, dim), dtype=jnp.float32)
        w_proj = 0.02 * jax.random.normal(ks[2], (dim, hidden), dtype=jnp.float32)
        u = 0.02 * jax.random.normal(ks[3], (hidden, rank), dtype=jnp.float32)
        v = 0.02 * jax.random.normal(ks[4], (rank, dim), dtype=jnp.float32)
        fast_b = jax.random.normal(ks[5], (rank, rank), dtype=jnp.float32)
        gate = jnp.float32(0.05)
        return {'x': x, 'fast_b': fast_b, 'w_fc': w_fc, 'w_proj': w_proj, 'u': u, 'v': v, 'gate': gate}
    _L0_ffn_in = _L0_ffn_setup()

    def _L1_attn_a_setup():
        import jax, jax.numpy as jnp
        import numpy as np
        S, B, H = (512, 2, 256)
        NH = 16
        HD = H // NH
        key = jax.random.key(seed)
        k1, k2 = jax.random.split(key)
        hidden_states = jax.random.normal(k1, (S, B, H), dtype=jnp.float32)
        W_qkv = jax.random.normal(k2, (3 * H, H), dtype=jnp.float32) * H ** (-0.5)
        b_qkv = jnp.zeros((3 * H,), dtype=jnp.float32)
        return {'hidden_states': hidden_states, 'W_qkv': W_qkv, 'b_qkv': b_qkv}
    _L1_attn_a_in = _L1_attn_a_setup()

    def _L1_attn_b_setup():
        import jax, jax.numpy as jnp
        import numpy as np
        EPS = 1e-05

        def layer_norm(x, w, b):
            mu = jnp.mean(x, axis=-1, keepdims=True)
            var = jnp.var(x, axis=-1, keepdims=True)
            return (x - mu) / jnp.sqrt(var + EPS) * w + b
        key = jax.random.key(seed)
        B, N, C = (4, 1024, 256)
        H = 16
        MW = 4 * C
        ks = jax.random.split(key, 8)
        s = 0.02
        return {'x': jax.random.normal(ks[0], (B, N, C), dtype=jnp.float32), 'ln1_w': jnp.ones((C,), jnp.float32), 'ln1_b': jnp.zeros((C,), jnp.float32), 'q_w': jax.random.normal(ks[1], (C, C), jnp.float32) * s, 'q_b': jnp.zeros((C,), jnp.float32), 'k_w': jax.random.normal(ks[2], (C, C), jnp.float32) * s, 'k_b': jnp.zeros((C,), jnp.float32), 'v_w': jax.random.normal(ks[3], (C, C), jnp.float32) * s, 'v_b': jnp.zeros((C,), jnp.float32), 'o_w': jax.random.normal(ks[4], (C, C), jnp.float32) * s, 'o_b': jnp.zeros((C,), jnp.float32), 'ln2_w': jnp.ones((C,), jnp.float32), 'ln2_b': jnp.zeros((C,), jnp.float32), 'fc_w': jax.random.normal(ks[5], (MW, C), jnp.float32) * s, 'fc_b': jnp.zeros((MW,), jnp.float32), 'proj_w': jax.random.normal(ks[6], (C, MW), jnp.float32) * s, 'proj_b': jnp.zeros((C,), jnp.float32)}
    _L1_attn_b_in = _L1_attn_b_setup()

    def _L1_ffn_setup():
        import jax, jax.numpy as jnp
        import numpy as np
        TOP_K = 2
        N_GROUP = 4
        TOPK_GROUP = 2
        ROUTED_SCALE = 2.5

        def _gate(xf, gate_w, gate_bias):
            logits = xf.astype(jnp.float32) @ gate_w.astype(jnp.float32)
            scores = jax.nn.sigmoid(logits)
            sfc = scores + gate_bias.astype(jnp.float32)[None]
            T, E = sfc.shape
            e_g = E // N_GROUP
            group_feat = sfc.reshape(T, N_GROUP, e_g)
            group_scores = jax.lax.top_k(group_feat, 2)[0].sum(axis=-1)
            _, group_idx = jax.lax.top_k(group_scores, TOPK_GROUP)
            group_mask = jax.nn.one_hot(group_idx, N_GROUP, dtype=sfc.dtype).sum(axis=1)
            score_mask = jnp.broadcast_to(group_mask[..., None], (T, N_GROUP, e_g)).reshape(T, E)
            tmp_scores = jnp.where(score_mask > 0, sfc, 0.0)
            _, topk_idx = jax.lax.top_k(tmp_scores, TOP_K)
            topk_w = jnp.take_along_axis(sfc, topk_idx, axis=-1)
            topk_w = topk_w / (topk_w.sum(axis=-1, keepdims=True) + 1e-20)
            return (topk_idx, topk_w * ROUTED_SCALE)
        key = jax.random.key(seed)
        ks = jax.random.split(key, 9)
        B, N, H, I, E, SH_I = (2, 256, 256, 128, 8, 256)
        s = lambda k, shape, scale: jax.random.normal(k, shape, jnp.float32) * scale
        return {'x': s(ks[0], (B, N, H), 1.0), 'gate_w': s(ks[1], (H, E), 0.02), 'gate_bias': s(ks[2], (E,), 0.02), 'w_gate': s(ks[3], (E, H, I), 0.02), 'w_up': s(ks[4], (E, H, I), 0.02), 'w_down': s(ks[5], (E, I, H), 0.02), 'sw_gate': s(ks[6], (H, SH_I), 0.02), 'sw_up': s(ks[7], (H, SH_I), 0.02), 'sw_down': s(ks[8], (SH_I, H), 0.02)}
    _L1_ffn_in = _L1_ffn_setup()
    _d = {'L0_attn_a_x': _L0_attn_a_in['x'], 'L0_attn_a_norm_w': _L0_attn_a_in['norm_w'], 'L0_attn_a_in_proj_w': _L0_attn_a_in['in_proj_w'], 'L0_attn_a_conv_w': _L0_attn_a_in['conv_w'], 'L0_attn_a_conv_b': _L0_attn_a_in['conv_b'], 'L0_attn_a_x_proj_w': _L0_attn_a_in['x_proj_w'], 'L0_attn_a_dt_proj_w': _L0_attn_a_in['dt_proj_w'], 'L0_attn_a_dt_proj_b': _L0_attn_a_in['dt_proj_b'], 'L0_attn_a_A_log': _L0_attn_a_in['A_log'], 'L0_attn_a_D_param': _L0_attn_a_in['D_param'], 'L0_attn_a_out_proj_w': _L0_attn_a_in['out_proj_w'], 'L0_attn_b_wq': _L0_attn_b_in['wq'], 'L0_attn_b_wk': _L0_attn_b_in['wk'], 'L0_attn_b_wv': _L0_attn_b_in['wv'], 'L0_attn_b_wo': _L0_attn_b_in['wo'], 'L0_attn_b_Aq': _L0_attn_b_in['Aq'], 'L0_attn_b_Bq': _L0_attn_b_in['Bq'], 'L0_attn_b_Av': _L0_attn_b_in['Av'], 'L0_attn_b_Bv': _L0_attn_b_in['Bv'], 'L0_ffn_fast_b': _L0_ffn_in['fast_b'], 'L0_ffn_w_fc': _L0_ffn_in['w_fc'], 'L0_ffn_w_proj': _L0_ffn_in['w_proj'], 'L0_ffn_u': _L0_ffn_in['u'], 'L0_ffn_v': _L0_ffn_in['v'], 'L0_ffn_gate': _L0_ffn_in['gate'], 'L1_attn_a_W_qkv': _L1_attn_a_in['W_qkv'], 'L1_attn_a_b_qkv': _L1_attn_a_in['b_qkv'], 'L1_attn_b_ln1_w': _L1_attn_b_in['ln1_w'], 'L1_attn_b_ln1_b': _L1_attn_b_in['ln1_b'], 'L1_attn_b_q_w': _L1_attn_b_in['q_w'], 'L1_attn_b_q_b': _L1_attn_b_in['q_b'], 'L1_attn_b_k_w': _L1_attn_b_in['k_w'], 'L1_attn_b_k_b': _L1_attn_b_in['k_b'], 'L1_attn_b_v_w': _L1_attn_b_in['v_w'], 'L1_attn_b_v_b': _L1_attn_b_in['v_b'], 'L1_attn_b_o_w': _L1_attn_b_in['o_w'], 'L1_attn_b_o_b': _L1_attn_b_in['o_b'], 'L1_attn_b_ln2_w': _L1_attn_b_in['ln2_w'], 'L1_attn_b_ln2_b': _L1_attn_b_in['ln2_b'], 'L1_attn_b_fc_w': _L1_attn_b_in['fc_w'], 'L1_attn_b_fc_b': _L1_attn_b_in['fc_b'], 'L1_attn_b_proj_w': _L1_attn_b_in['proj_w'], 'L1_attn_b_proj_b': _L1_attn_b_in['proj_b'], 'L1_ffn_gate_w': _L1_ffn_in['gate_w'], 'L1_ffn_gate_bias': _L1_ffn_in['gate_bias'], 'L1_ffn_w_gate': _L1_ffn_in['w_gate'], 'L1_ffn_w_up': _L1_ffn_in['w_up'], 'L1_ffn_w_down': _L1_ffn_in['w_down'], 'L1_ffn_sw_gate': _L1_ffn_in['sw_gate'], 'L1_ffn_sw_up': _L1_ffn_in['sw_up'], 'L1_ffn_sw_down': _L1_ffn_in['sw_down']}
    _x0 = _d['L0_attn_a_x']
    _d['L0_attn_a_x'] = jax.random.normal(jax.random.fold_in(jax.random.key(seed), 1), (4, 1024, 256), dtype=_x0.dtype)
    del _x0
    return _d

def reference(L0_attn_a_x, L0_attn_a_norm_w, L0_attn_a_in_proj_w, L0_attn_a_conv_w, L0_attn_a_conv_b, L0_attn_a_x_proj_w, L0_attn_a_dt_proj_w, L0_attn_a_dt_proj_b, L0_attn_a_A_log, L0_attn_a_D_param, L0_attn_a_out_proj_w, L0_attn_b_wq, L0_attn_b_wk, L0_attn_b_wv, L0_attn_b_wo, L0_attn_b_Aq, L0_attn_b_Bq, L0_attn_b_Av, L0_attn_b_Bv, L0_ffn_fast_b, L0_ffn_w_fc, L0_ffn_w_proj, L0_ffn_u, L0_ffn_v, L0_ffn_gate, L1_attn_a_W_qkv, L1_attn_a_b_qkv, L1_attn_b_ln1_w, L1_attn_b_ln1_b, L1_attn_b_q_w, L1_attn_b_q_b, L1_attn_b_k_w, L1_attn_b_k_b, L1_attn_b_v_w, L1_attn_b_v_b, L1_attn_b_o_w, L1_attn_b_o_b, L1_attn_b_ln2_w, L1_attn_b_ln2_b, L1_attn_b_fc_w, L1_attn_b_fc_b, L1_attn_b_proj_w, L1_attn_b_proj_b, L1_ffn_gate_w, L1_ffn_gate_bias, L1_ffn_w_gate, L1_ffn_w_up, L1_ffn_w_down, L1_ffn_sw_gate, L1_ffn_sw_up, L1_ffn_sw_down):

    def _L0_attn_a_ref(x, norm_w, in_proj_w, conv_w, conv_b, x_proj_w, dt_proj_w, dt_proj_b, A_log, D_param, out_proj_w):
        import jax, jax.numpy as jnp
        import numpy as np
        DIM, D_STATE, D_CONV, EXPAND = (256, 16, 4, 2)
        D_INNER = EXPAND * DIM
        DT_RANK = (DIM + 15) // 16
        B_SZ, L_SEQ = (2, 256)
        EPS = 1e-05

        def _mamba_block(x, norm_w, in_proj_w, conv_w, conv_b, x_proj_w, dt_proj_w, dt_proj_b, A_log, D_param, out_proj_w):
            xn = x * jax.lax.rsqrt(jnp.mean(x * x, axis=-1, keepdims=True) + EPS) * norm_w
            xz = jnp.einsum('bld,ed->ble', xn, in_proj_w)
            xi, z = jnp.split(xz, 2, axis=-1)
            xc = jax.lax.conv_general_dilated(xi.transpose(0, 2, 1), conv_w, window_strides=(1,), padding=[(D_CONV - 1, 0)], dimension_numbers=('NCH', 'OIH', 'NCH'), feature_group_count=D_INNER) + conv_b[None, :, None]
            u = jax.nn.silu(xc.transpose(0, 2, 1))
            x_dbl = jnp.einsum('bld,ed->ble', u, x_proj_w)
            dt, Bm, Cm = jnp.split(x_dbl, [DT_RANK, DT_RANK + D_STATE], axis=-1)
            delta = jax.nn.softplus(jnp.einsum('blr,dr->bld', dt, dt_proj_w) + dt_proj_b)
            A = -jnp.exp(A_log)

            def step(h, inp):
                delta_t, B_t, C_t, u_t = inp
                dA = jnp.exp(delta_t[..., None] * A)
                dBu = (delta_t * u_t)[..., None] * B_t[:, None, :]
                h = dA * h + dBu
                y = jnp.einsum('bds,bs->bd', h, C_t)
                return (h, y)
            h0 = jnp.zeros((x.shape[0], D_INNER, D_STATE), x.dtype)
            inputs = (delta.swapaxes(0, 1), Bm.swapaxes(0, 1), Cm.swapaxes(0, 1), u.swapaxes(0, 1))
            _, ys = jax.lax.scan(step, h0, inputs)
            y = ys.swapaxes(0, 1) + u * D_param
            y = y * jax.nn.silu(z)
            out = jnp.einsum('ble,de->bld', y, out_proj_w)
            return x + out
        return _mamba_block(x, norm_w, in_proj_w, conv_w, conv_b, x_proj_w, dt_proj_w, dt_proj_b, A_log, D_param, out_proj_w)

    def _L0_attn_b_ref(query, wq, wk, wv, wo, Aq, Bq, Av, Bv):
        import jax, jax.numpy as jnp
        import numpy as np
        NUM_HEADS = 16
        LORA_SCALE = 32.0 / 8.0
        ROPE_BASE = 10000.0

        def make_sincos(seq_len, dim):
            pos = jnp.arange(seq_len, dtype=jnp.float32)
            i = jnp.arange(0, dim, 2, dtype=jnp.float32) / dim
            theta = pos[:, None] / ROPE_BASE ** i[None, :]
            return (jnp.sin(theta), jnp.cos(theta))

        def apply_rope(x, sin, cos):
            x_even = x[..., 0::2]
            x_odd = x[..., 1::2]
            rot_even = x_even * cos - x_odd * sin
            rot_odd = x_even * sin + x_odd * cos
            return jnp.stack([rot_even, rot_odd], axis=-1).reshape(x.shape)
        B, T, D = query.shape
        H = NUM_HEADS
        dh = D // H
        q = query @ wq + query @ Aq @ Bq * LORA_SCALE
        k = query @ wk
        v = query @ wv + query @ Av @ Bv * LORA_SCALE

        def split(x):
            return x.reshape(B, T, H, dh).transpose(0, 2, 1, 3)
        q, k, v = (split(q), split(k), split(v))
        sin, cos = make_sincos(T, dh)
        q = apply_rope(q, sin, cos)
        k = apply_rope(k, sin, cos)
        scores = jnp.einsum('bhqd,bhkd->bhqk', q, k) / jnp.sqrt(jnp.float32(dh))
        causal = jnp.triu(jnp.ones((T, T), dtype=bool), k=1)
        scores = jnp.where(causal[None, None], jnp.float32(-1000000000.0), scores)
        attn = jax.nn.softmax(scores, axis=-1)
        out = jnp.einsum('bhqk,bhkd->bhqd', attn, v)
        out = out.transpose(0, 2, 1, 3).reshape(B, T, D)
        return out @ wo

    def _L0_ffn_ref(x, fast_b, w_fc, w_proj, u, v, gate):
        import jax, jax.numpy as jnp
        import numpy as np

        def _bitlinear(x, w_latent):
            scale = jax.lax.stop_gradient(jnp.clip(jnp.mean(jnp.abs(w_latent), axis=1, keepdims=True), 1e-05, None))
            tern = jnp.clip(jnp.round(w_latent / scale), -1.0, 1.0)
            w = w_latent + jax.lax.stop_gradient(tern - w_latent)
            return x @ (w * scale).T
        h = _bitlinear(x, w_fc) + gate * (x @ v.T @ fast_b.T @ u.T)
        r = jnp.maximum(h, 0.0)
        return _bitlinear(r * r, w_proj)

    def _L1_attn_a_ref(hidden_states, W_qkv, b_qkv):
        import jax, jax.numpy as jnp
        import numpy as np
        S, B, H = (512, 2, 256)
        NH = 16
        HD = H // NH
        s, b, h = hidden_states.shape
        qkv = hidden_states @ W_qkv.T + b_qkv
        qkv = qkv.reshape(s, b, NH, 3 * HD)
        q, k, v = jnp.split(qkv, 3, axis=-1)
        norm_factor = HD ** (-0.5)
        scores = jnp.einsum('sbhd,tbhd->bhst', q, k) * norm_factor
        probs = jnp.cumsum(scores.astype(jnp.float32), axis=-1) * s ** (-0.5)
        probs = probs.astype(hidden_states.dtype)
        ctx = jnp.einsum('bhst,tbhd->sbhd', probs, v)
        return ctx.reshape(s, b, h)

    def _L1_attn_b_ref(x, ln1_w, ln1_b, q_w, q_b, k_w, k_b, v_w, v_b, o_w, o_b, ln2_w, ln2_b, fc_w, fc_b, proj_w, proj_b):
        import jax, jax.numpy as jnp
        import numpy as np
        EPS = 1e-05

        def layer_norm(x, w, b):
            mu = jnp.mean(x, axis=-1, keepdims=True)
            var = jnp.var(x, axis=-1, keepdims=True)
            return (x - mu) / jnp.sqrt(var + EPS) * w + b
        B, N, C = x.shape
        H = 16
        D = C // H
        xn = layer_norm(x, ln1_w, ln1_b)
        q = (xn @ q_w.T + q_b).reshape(B, N, H, D).transpose(0, 2, 1, 3)
        k = (xn @ k_w.T + k_b).reshape(B, N, H, D).transpose(0, 2, 1, 3)
        v = (xn @ v_w.T + v_b).reshape(B, N, H, D).transpose(0, 2, 1, 3)
        q = jax.nn.elu(q) + 1.0
        k = jax.nn.elu(k) + 1.0
        kv = jnp.einsum('bhnd,bhne->bnde', k, v)
        qkv = jnp.einsum('bhnd,bnde->bhne', q, kv)
        k_sum = k.sum(axis=1)
        qk = jnp.einsum('bhnd,bnd->bhn', q, k_sum)
        attn = qkv / qk[..., None]
        attn = attn.transpose(0, 2, 1, 3).reshape(B, N, C)
        attn = attn @ o_w.T + o_b
        x = x + attn
        xn2 = layer_norm(x, ln2_w, ln2_b)
        h = jax.nn.gelu(xn2 @ fc_w.T + fc_b, approximate=False)
        x = x + (h @ proj_w.T + proj_b)
        return x

    def _L1_ffn_ref(x, gate_w, gate_bias, w_gate, w_up, w_down, sw_gate, sw_up, sw_down):
        import jax, jax.numpy as jnp
        import numpy as np
        TOP_K = 2
        N_GROUP = 4
        TOPK_GROUP = 2
        ROUTED_SCALE = 2.5

        def _gate(xf, gate_w, gate_bias):
            logits = xf.astype(jnp.float32) @ gate_w.astype(jnp.float32)
            scores = jax.nn.sigmoid(logits)
            sfc = scores + gate_bias.astype(jnp.float32)[None]
            T, E = sfc.shape
            e_g = E // N_GROUP
            group_feat = sfc.reshape(T, N_GROUP, e_g)
            group_scores = jax.lax.top_k(group_feat, 2)[0].sum(axis=-1)
            _, group_idx = jax.lax.top_k(group_scores, TOPK_GROUP)
            group_mask = jax.nn.one_hot(group_idx, N_GROUP, dtype=sfc.dtype).sum(axis=1)
            score_mask = jnp.broadcast_to(group_mask[..., None], (T, N_GROUP, e_g)).reshape(T, E)
            tmp_scores = jnp.where(score_mask > 0, sfc, 0.0)
            _, topk_idx = jax.lax.top_k(tmp_scores, TOP_K)
            topk_w = jnp.take_along_axis(sfc, topk_idx, axis=-1)
            topk_w = topk_w / (topk_w.sum(axis=-1, keepdims=True) + 1e-20)
            return (topk_idx, topk_w * ROUTED_SCALE)
        B, N, H = x.shape
        xf = x.reshape(-1, H)
        topk_idx, topk_w = _gate(xf, gate_w, gate_bias)
        g = jax.nn.silu(jnp.einsum('th,ehi->tei', xf, w_gate))
        u = jnp.einsum('th,ehi->tei', xf, w_up)
        experts_y = jnp.einsum('tei,eih->teh', g * u, w_down)
        masked_y = jnp.take_along_axis(experts_y, topk_idx[:, :, None], axis=1)
        y = jnp.einsum('tkh,tk->th', masked_y, topk_w.astype(x.dtype)).reshape(B, N, H)
        shared = jax.nn.silu(x @ sw_gate) * (x @ sw_up) @ sw_down
        return y + shared
    x = L0_attn_a_x
    x = x + _L0_attn_a_ref(_layernorm(x, axis=-1), L0_attn_a_norm_w, L0_attn_a_in_proj_w, L0_attn_a_conv_w, L0_attn_a_conv_b, L0_attn_a_x_proj_w, L0_attn_a_dt_proj_w, L0_attn_a_dt_proj_b, L0_attn_a_A_log, L0_attn_a_D_param, L0_attn_a_out_proj_w)
    x = x + _L0_ffn_ref(_layernorm(x, axis=-1), L0_ffn_fast_b, L0_ffn_w_fc, L0_ffn_w_proj, L0_ffn_u, L0_ffn_v, L0_ffn_gate)
    x = x + _L0_attn_b_ref(_layernorm(x, axis=-1), L0_attn_b_wq, L0_attn_b_wk, L0_attn_b_wv, L0_attn_b_wo, L0_attn_b_Aq, L0_attn_b_Bq, L0_attn_b_Av, L0_attn_b_Bv)
    x = x + _L0_ffn_ref(_layernorm(x, axis=-1), L0_ffn_fast_b, L0_ffn_w_fc, L0_ffn_w_proj, L0_ffn_u, L0_ffn_v, L0_ffn_gate)
    x = x + _L1_attn_a_ref(_layernorm(x, axis=-1), L1_attn_a_W_qkv, L1_attn_a_b_qkv)
    x = x + _L1_ffn_ref(_layernorm(x, axis=-1), L1_ffn_gate_w, L1_ffn_gate_bias, L1_ffn_w_gate, L1_ffn_w_up, L1_ffn_w_down, L1_ffn_sw_gate, L1_ffn_sw_up, L1_ffn_sw_down)
    x = x + _L1_attn_b_ref(_layernorm(x, axis=-1), L1_attn_b_ln1_w, L1_attn_b_ln1_b, L1_attn_b_q_w, L1_attn_b_q_b, L1_attn_b_k_w, L1_attn_b_k_b, L1_attn_b_v_w, L1_attn_b_v_b, L1_attn_b_o_w, L1_attn_b_o_b, L1_attn_b_ln2_w, L1_attn_b_ln2_b, L1_attn_b_fc_w, L1_attn_b_fc_b, L1_attn_b_proj_w, L1_attn_b_proj_b)
    x = x + _L1_ffn_ref(_layernorm(x, axis=-1), L1_ffn_gate_w, L1_ffn_gate_bias, L1_ffn_w_gate, L1_ffn_w_up, L1_ffn_w_down, L1_ffn_sw_gate, L1_ffn_sw_up, L1_ffn_sw_down)
    return x

_drawn_inputs = setup_inputs


def setup_inputs(seed=0):
    import zlib

    import numpy as np

    out = dict(_drawn_inputs(seed))
    spreads = {'L0_attn_a_norm_w': (1.0, 0.2),
     'L0_attn_a_conv_b': (0.0, 0.1),
     'L0_attn_a_D_param': (1.0, 0.2),
     'L1_attn_a_b_qkv': (0.0, 0.1),
     'L1_attn_b_ln1_w': (1.0, 0.6),
     'L1_attn_b_ln1_b': (0.0, 0.8),
     'L1_attn_b_q_b': (0.0, 2.0),
     'L1_attn_b_k_b': (0.0, 2.0),
     'L1_attn_b_v_b': (0.0, 0.8),
     'L1_attn_b_o_b': (0.0, 0.779),
     'L1_attn_b_ln2_w': (1.0, 0.6),
     'L1_attn_b_ln2_b': (0.0, 2.0),
     'L1_attn_b_fc_b': (0.0, 0.8),
     'L1_attn_b_proj_b': (0.0, 0.303)}
    factors = {'L0_attn_b_Aq': 6.565,
     'L0_attn_b_Bq': 6.623,
     'L0_attn_b_Av': 6.237,
     'L0_attn_b_Bv': 6.096,
     'L0_ffn_fast_b': 8.0,
     'L0_ffn_u': 8.0,
     'L0_ffn_v': 8.0,
     'L1_attn_b_q_w': 8.0,
     'L1_attn_b_k_w': 8.0,
     'L1_attn_b_v_w': 8.0,
     'L1_attn_b_o_w': 7.558,
     'L1_ffn_gate_w': 4.984,
     'L1_ffn_gate_bias': 8.0,
     'L1_ffn_w_gate': 4.275,
     'L1_ffn_w_up': 4.24,
     'L1_ffn_w_down': 4.229,
     'L1_ffn_sw_gate': 5.354,
     'L1_ffn_sw_up': 5.301,
     'L1_ffn_sw_down': 5.296}
    for name, (base, spread) in spreads.items():
        noise = np.random.default_rng([zlib.crc32(name.encode()), seed]).standard_normal(out[name].shape)
        drawn = base * np.exp(spread * noise) if base else spread * noise
        out[name] = jnp.asarray(drawn.astype(out[name].dtype))
    for name, factor in factors.items():
        out[name] = (out[name] * factor).astype(out[name].dtype)
    return out
```

```python
from contextlib import ExitStack

import numpy as np

import concourse.bass as bass
from concourse import mybir
from concourse.alu_op_type import AluOpType as ALU

F32 = mybir.dt.float32
BF16 = mybir.dt.bfloat16
ACT = mybir.ActivationFunctionType
AX = mybir.AxisListType

P = 128
B, L, D = 4, 1024, 256
T = B * L
TILES = T // P
GT = 4
G = TILES // GT
GN = GT * P
KD = D // P
EPS = 1e-5
HID = 1024
HB = HID // P


class Ctx:

    def __init__(self, nc, ins, stack):
        self.nc, self.ins, self.stack, self.stage = nc, ins, stack, ""
        self.x = self.keep("x", [P, TILES * D])
        self.ident = self.keep("ident", [P, P])
        self.prepared = {}

    def keep(self, name, shape, dt=F32):
        return self.stack.enter_context(self.nc.sbuf_tensor(name, shape, dt))

    def x_tile(self, t):
        return self.x[:, bass.ds(t * D, D)]

    def x_pair(self, t):
        return self.x[:, bass.ds(t * 2 * D, 2 * D)]


class Local:

    def __init__(self, c, stage):
        self.c, self.nc, self.stage = c, c.nc, stage

    def __enter__(self):
        self.stack = ExitStack().__enter__()
        self.sems = []
        return self

    def __exit__(self, *why):
        if why[0] is None:
            self.nc.clear_and_free_semaphores(self.sems)
            self.nc.all_engine_barrier()
        return self.stack.__exit__(*why)

    def sb(self, name, shape, dt=F32):
        return self.stack.enter_context(self.nc.sbuf_tensor(f"{self.stage}_{name}", shape, dt))

    def ps(self, name, shape, dt=F32):
        return self.stack.enter_context(self.nc.psum_tensor(f"{self.stage}_{name}", shape, dt))

    def sem(self, name):
        self.sems.append(self.nc.alloc_semaphore(f"{self.stage}_{name}"))
        return self.sems[-1]


class Norm:

    def __init__(self, c, s, tile=lambda g, j: g * GT + j, trp=None):
        self.c, self.nc, self.tile = c, c.nc, tile
        self.st = s.sb("bn_stats", [P, GT, 6])
        self.mv = s.sb("moments", [P, GT, 2])
        self.ve = s.sb("var_eps", [P, GT])
        self.rstd = s.sb("rstd", [P, GT])
        self.half = s.sb("minus_half", [P, GT])
        self.eps = s.sb("eps", [P, GT])
        self.xn = s.sb("xn", [P, GT, D])
        self.xT = s.sb("xT", [P, KD, GN])
        self.trp = s.ps("trp", [P, KD, GN]) if trp is None else trp
        self.stats_ready = s.sem("stats_ready")
        self.stats_seen = s.sem("stats_seen")
        self.moments_ready = s.sem("moments_ready")
        self.half_ready = s.sem("half_ready")
        self.eps_added = s.sem("eps_added")
        self.rstd_ready = s.sem("rstd_ready")
        self.xn_ready = s.sem("xn_ready")
        self.xn_used = s.sem("xn_used")
        self.xT_ready = s.sem("xT_ready")

    def moments(self, dve, g):
        for j in range(GT):
            dve.bn_stats(self.st[:, j, :], self.c.x_tile(self.tile(g, j))).then_inc(self.stats_ready, 1)
        dve.wait_ge(self.stats_ready, g * GT + GT)
        dve.sem_inc(self.stats_seen, 1)
        for j in range(GT):
            dve.bn_aggr(self.mv[:, j, :], self.st[:, j, :]).then_inc(self.moments_ready, 1)

    def pool_prologue(self, pool):
        pool.memset(self.half[:, :], -0.5).then_inc(self.half_ready, 1)
        pool.memset(self.eps[:, :], EPS).then_inc(self.half_ready, 1)
        pool.wait_ge(self.half_ready, 2)

    def power(self, pool, g):
        pool.wait_ge(self.moments_ready, g * GT + GT)
        pool.tensor_tensor(self.ve[:, :], self.mv[:, :, 1], self.eps[:, :], ALU.add).then_inc(self.eps_added, 1)
        pool.wait_ge(self.eps_added, g + 1)
        pool.tensor_tensor(self.rstd[:, :], self.ve[:, :], self.half[:, :], ALU.pow).then_inc(self.rstd_ready, 1)

    def normalise(self, dve, g, first=False):
        dve.wait_ge(self.rstd_ready, g + 1)
        if not first:
            dve.wait_ge(self.xn_used, g)
        for j in range(GT):
            dve.tensor_scalar(self.xn[:, j, :], self.c.x_tile(self.tile(g, j)), self.mv[:, j, 0:1],
                              self.rstd[:, j:j + 1], ALU.subtract, ALU.mult).then_inc(self.xn_ready, 1)

    def transposes(self, pe, g, first=False):
        pe.wait_ge(self.xn_ready, g * GT + GT)
        if not first:
            pe.wait_ge(self.xT_ready, g * KD)
        for k in range(KD):
            for j in range(GT):
                mm = pe.transpose(self.trp[:, k, j * P:(j + 1) * P], self.xn[:, j, k * P:(k + 1) * P],
                                  self.c.ident[:, :])
        mm.then_inc(self.xn_used, 1)

    def copy_out(self, act, g, gemms_done=None, count=None):
        act.wait_ge(self.xn_used, g + 1)
        if gemms_done is not None:
            act.wait_ge(gemms_done, count)
        for k in range(KD):
            act.copy(self.xT[:, k, :], self.trp[:, k, :]).then_inc(self.xT_ready, 1)


class TwiceNorm(Norm):

    def __init__(self, c, s, tile=lambda g, j: g * GT + j, trp=None):
        super().__init__(c, s, tile, trp)
        self.v2 = s.sb("var_z", [P, GT])
        self.v2e = s.sb("var_z_eps", [P, GT])
        self.r2 = s.sb("rstd_z", [P, GT])
        self.v1 = s.sb("std_share", [P, GT])
        self.pool_step = s.sem("pool_step")
        self.r2_ready = s.sem("r2_ready")
        self.z_ready = s.sem("z_ready")

    def power(self, pool, g):
        super().power(pool, g)
        pool.wait_ge(self.rstd_ready, g + 1)
        pool.tensor_tensor(self.v1[:, :], self.mv[:, :, 1], self.rstd[:, :], ALU.mult).then_inc(self.pool_step, 1)
        pool.wait_ge(self.pool_step, g * 3 + 1)
        pool.tensor_tensor(self.v2[:, :], self.v1[:, :], self.rstd[:, :], ALU.mult).then_inc(self.pool_step, 1)
        pool.wait_ge(self.pool_step, g * 3 + 2)
        pool.tensor_tensor(self.v2e[:, :], self.v2[:, :], self.eps[:, :], ALU.add).then_inc(self.pool_step, 1)
        pool.wait_ge(self.pool_step, g * 3 + 3)
        pool.tensor_tensor(self.r2[:, :], self.v2e[:, :], self.half[:, :], ALU.pow).then_inc(self.r2_ready, 1)

    def normalise(self, dve, g, z_of, first=False):
        dve.wait_ge(self.rstd_ready, g + 1)
        for j in range(GT):
            dve.tensor_scalar(z_of(j), self.c.x_tile(self.tile(g, j)), self.mv[:, j, 0:1],
                              self.rstd[:, j:j + 1], ALU.subtract, ALU.mult).then_inc(self.z_ready, 1)
        dve.wait_ge(self.r2_ready, g + 1)
        if not first:
            dve.wait_ge(self.xn_used, g)
        for j in range(GT):
            dve.wait_ge(self.z_ready, g * GT + j + 1)
            dve.tensor_scalar(self.xn[:, j, :], z_of(j), self.r2[:, j:j + 1], None, ALU.mult).then_inc(self.xn_ready, 1)


CB = 4
NS = 16
DTR = 16
XD = DTR + 2 * NS
TAPS = 4
PAD = TAPS - 1


def stage_mamba(c):
    nc = c.nc
    bc = nc.dram_tensor("mamba_bc", (2 * NS, T), F32, kind="Internal").ap()
    with Local(c, "mamba") as s:
        banks = s.ps("banks", [P, 8, 512])
        norm = TwiceNorm(c, s, trp=banks[:, 0:2, :])
        zt = s.sb("z", [P, GT, D])
        win = s.sb("win", [P, KD, 2 * CB * P])
        nw = s.sb("nw", [P, KD])
        chan = s.sb("chan", [P, CB, 7])
        a_log = s.sb("a_log", [P, CB, NS])
        a_neg = s.sb("a_neg", [P, CB, NS])
        wxp = s.sb("wxp", [P, CB, XD])
        wdt = s.sb("wdt", [P, CB * P])
        wout = s.sb("wout", [P, CB, D])
        xi = s.sb("xi", [P, CB, PAD + L])
        hc = s.sb("hc", [P, 2, L])
        xc, ab = (hc[:, i, :].rearrange("p (a n) -> p a n", a=2) for i in range(2))
        u = s.sb("u", [P, CB, L])
        sz = s.sb("sz", [P, CB, L])
        xd = s.sb("xd", [P, L])
        ex = s.sb("ex", [P, 2, GN])
        relu = s.sb("relu", [P, 2, GN])
        delta = s.sb("delta", [P, CB, L])
        du = s.sb("du", [P, CB, L])
        bcs = s.sb("bcs", [P, 2, 2, L])
        dA = s.sb("dA", [P, 2, L])
        dBu = s.sb("dBu", [P, 2, L])
        h = s.sb("h", [P, 2, L])
        names = ("loaded consts w_ready a_ready z_added hp_filled hp_used conv_step xc_ready u_ready xp_filled xd_ready bc_stored "
                 "dt_filled abs_ready exp_ready ln_ready relu_ready delta_ready du_ready bc_loaded0 bc_loaded1 dA_ready dBu_ready h_ready "
                 "hc_ready hc_used du_seen skip_ready yg_ready out_filled out_used")
        S = {n: s.sem(n) for n in names.split()}
        START = {"z_added": 1, "u_ready": 2, "exp_ready": 2, "h_ready": 2, "hc_ready": 2, "hc_used": 2, "out_used": 1,
                 "delta_ready": 2}

        def sem(n):
            return S[n]

        with nc.Block() as block:
            @block.sync
            def _(sp):
                for dst, src in ((win[:, :, :], c.ins["mb_inT"].rearrange("(k p) n -> p k n", p=P)),
                                 (nw[:, :], c.ins["mb_norm"]), (chan[:, :, :], c.ins["mb_chan"]),
                                 (a_log[:, :, :], c.ins["mb_alog"]),
                                 (wxp[:, :, :], c.ins["mb_xpT"].rearrange("(c p) n -> p c n", p=P)),
                                 (wout[:, :, :], c.ins["mb_outT"].rearrange("(c p) n -> p c n", p=P))):
                    sp.dma_start(dst, src).then_inc(sem("loaded"), 16)
                sp.wait_ge(sem("consts"), 1)
                sp.dma_start(wdt[0:DTR, :], c.ins["mb_dtT"]).then_inc(sem("loaded"), 16)

                def load(b, st, slot):
                    src = bc.rearrange("(k s) t -> s k t", k=2)[bass.ds(st, 1), :, bass.ds(b * L, L)]
                    sp.dma_start(bcs[:, slot, :, :], src.to_broadcast((P, 2, L))).then_inc(sem(f"bc_loaded{slot}"), 16)

                with sp.Fori(0, B) as b:
                    for v in range(2):
                        sp.wait_ge(sem("xd_ready"), b * 2 + v + 1)
                        sp.dma_start(bc[:, bass.ds(b * L + v * GN, GN)], xd[DTR:XD, v * GN:(v + 1) * GN]).then_inc(sem("bc_stored"), 16)
                    sp.wait_ge(sem("bc_stored"), b * 32 + 32)
                    load(b, 0, 0)
                    load(b, 1, 1)
                    with sp.Fori(1, NS // 2) as m:
                        for slot in range(2):
                            sp.wait_ge(sem("hc_ready"), b * (NS * CB) + m * (2 * CB) + slot * CB - CB + START["hc_ready"])
                            load(b, m * 2 + slot, slot)

            @block.tensor
            def _(pe):
                def project(g, v):
                    pe.wait_ge(norm.xT_ready, g * KD + KD)
                    for i in range(2 * CB):
                        if i >= 4:
                            pe.wait_ge(sem("hp_used"), g * 8 + i - 3)
                        elif v == 1:
                            pe.wait_ge(sem("abs_ready"), g * CB)
                            pe.wait_ge(sem("relu_ready"), g * CB)
                        for k in range(KD):
                            mm = pe.matmul(banks[:, 2 + i % 4, :], win[:, k, i * P:(i + 1) * P], norm.xT[:, k, :],
                                           start=(k == 0), stop=(k == KD - 1))
                        mm.then_inc(sem("hp_filled"), 1)

                def x_proj(g, v):
                    pe.wait_ge(sem("u_ready"), g * CB + CB + START["u_ready"])
                    if v == 1:
                        pe.wait_ge(sem("xd_ready"), g)
                    for k in range(CB):
                        mm = pe.matmul(banks[0:XD, 6, :], wxp[:, k, :], u[:, k, v * GN:(v + 1) * GN],
                                       start=(k == 0), stop=(k == CB - 1))
                    mm.then_inc(sem("xp_filled"), 1)
                    pe.wait_ge(sem("xd_ready"), g + 1)
                    pe.wait_ge(sem("hp_used"), g * 8 + 8)
                    for k in range(CB):
                        pe.matmul(banks[:, 2 + k, :], wdt[:, k * P:(k + 1) * P], xd[:, v * GN:(v + 1) * GN],
                                  start=True, stop=True).then_inc(sem("dt_filled"), 1)

                def sums(b, st, first=False):
                    for k in range(CB):
                        n = b * (NS * CB) + st * CB + k
                        pe.wait_ge(sem("hc_ready"), n + 1 + START["hc_ready"])
                        for i in range(2):
                            mm = pe.matmul(banks[:, 2 * k + i, :], c.ident[:, :], hc[:, k % 2, i * 512:(i + 1) * 512],
                                           start=first, stop=True, skip_group_check=True)
                        mm.then_inc(sem("hc_used"), 1)

                pe.wait_ge(sem("w_ready"), KD)
                pe.wait_ge(sem("loaded"), 16 * 7)
                pe.wait_ge(sem("consts"), 3)
                with pe.Fori(0, B) as b:
                    for v in range(2):
                        g = b * 2 + v
                        if v == 0:
                            pe.wait_ge(sem("out_used"), b * 4 + 1)
                        else:
                            pe.wait_ge(norm.xT_ready, g * KD)
                        norm.transposes(pe, g, first=True)
                        project(g, v)
                        x_proj(g, v)
                    pe.wait_ge(sem("abs_ready"), b * (2 * CB) + 2 * CB)
                    pe.wait_ge(sem("relu_ready"), b * (2 * CB) + 2 * CB)
                    sums(b, 0, first=True)
                    with pe.Fori(1, NS) as st:
                        sums(b, st)
                    pe.wait_ge(sem("yg_ready"), b * CB + CB)
                    for t in range(8):
                        for k in range(CB):
                            mm = pe.matmul(banks[:, t // 2, (t % 2) * D:(t % 2 + 1) * D], delta[:, k, t * P:(t + 1) * P],
                                           wout[:, k, :], start=(k == 0), stop=(k == CB - 1))
                        if t % 2 == 1:
                            mm.then_inc(sem("out_filled"), 1)

            @block.gpsimd
            def _(pool):
                norm.pool_prologue(pool)

                def inputs(b, m, slot):
                    st = m * 2 + slot
                    for k in range(CB):
                        n = b * (NS * CB) + st * CB + k
                        if k == 0:
                            pool.wait_ge(sem(f"bc_loaded{slot}"), b * (NS * 8) + m * 16 + 16)
                        pool.wait_ge(sem("h_ready"), n + 1)
                        pool.tensor_tensor(dBu[:, k % 2, :], du[:, k, :], bcs[:, slot, 0, :], ALU.mult).then_inc(sem("dBu_ready"), 1)

                with pool.Fori(0, B) as b:
                    norm.power(pool, b * 2)
                    norm.power(pool, b * 2 + 1)
                    pool.wait_ge(sem("du_ready"), b * (2 * CB) + 2 * CB)
                    pool.sem_inc(sem("du_seen"), 1)
                    with pool.Fori(0, NS // 2) as m:
                        inputs(b, m, 0)
                        inputs(b, m, 1)

            @block.scalar
            def _(act):
                def group(g, v):
                    norm.copy_out(act, g, *((None, None) if v == 0 else (sem("hp_filled"), g * 8)))
                    for i in range(2 * CB):
                        act.wait_ge(sem("hp_filled"), g * 8 + i + 1)
                        if i < CB:
                            act.copy(xi[:, i, PAD + v * GN:PAD + (v + 1) * GN], banks[:, 2 + i % 4, :]).then_inc(sem("hp_used"), 1)
                        else:
                            act.activation(sz[:, i - CB, v * GN:(v + 1) * GN], banks[:, 2 + i % 4, :], ACT.Silu)\
                               .then_inc(sem("hp_used"), 1)
                    for k in range(CB):
                        act.wait_ge(sem("xc_ready"), g * CB + k + 1)
                        act.activation(u[:, k, v * GN:(v + 1) * GN], xc[:, k % 2, :], ACT.Silu,
                                       bias=chan[:, k, 4:5]).then_inc(sem("u_ready"), 1)
                    act.wait_ge(sem("xp_filled"), g + 1)
                    act.copy(xd[0:XD, v * GN:(v + 1) * GN], banks[0:XD, 6, :]).then_inc(sem("xd_ready"), 1)
                    for k in range(CB):
                        act.wait_ge(sem("dt_filled"), g * CB + k + 1)
                        act.wait_ge(sem("delta_ready"), g * CB + k + 1)
                        act.activation(ab[:, k % 2, :], banks[:, 2 + k, :], ACT.Abs, bias=chan[:, k, 5:6])\
                           .then_inc(sem("abs_ready"), 1)
                        act.activation(relu[:, k % 2, :], banks[:, 2 + k, :], ACT.Relu, bias=chan[:, k, 5:6])\
                           .then_inc(sem("relu_ready"), 1)
                        act.wait_ge(sem("abs_ready"), g * CB + k + 1)
                        act.activation(ex[:, k % 2, :], ab[:, k % 2, :], ACT.Exp, scale=-1.0).then_inc(sem("exp_ready"), 1)
                        act.wait_ge(sem("exp_ready"), g * CB + k + 1 + START["exp_ready"])
                        act.activation(ex[:, k % 2, :], ex[:, k % 2, :], ACT.Ln, bias=1.0).then_inc(sem("ln_ready"), 1)

                def decays(b, st):
                    for k in range(CB):
                        n = b * (NS * CB) + st * CB + k
                        act.wait_ge(sem("h_ready"), n + 1)
                        act.activation(dA[:, k % 2, :], delta[:, k, :], ACT.Exp, scale=a_neg[:, k, bass.ds(st, 1)])\
                           .then_inc(sem("dA_ready"), 1)

                act.sem_inc(sem("exp_ready"), START["exp_ready"])
                act.sem_inc(sem("u_ready"), START["u_ready"])
                act.wait_ge(sem("loaded"), 16 * 7)
                act.activation(a_log[:, :, :], a_log[:, :, :], ACT.Exp).then_inc(sem("a_ready"), 1)
                act.wait_ge(sem("a_ready"), 2)
                with act.Fori(0, B) as b:
                    group(b * 2, 0)
                    group(b * 2 + 1, 1)
                    act.wait_ge(sem("delta_ready"), b * (2 * CB) + 2 * CB + START["delta_ready"])
                    with act.Fori(0, NS) as st:
                        decays(b, st)

            @block.vector
            def _(dve):
                STEPS = TAPS - 1

                def norm_group(g, v):
                    norm.moments(dve, g)
                    dve.wait_ge(sem("z_added"), g + 1)
                    norm.normalise(dve, g, lambda j: zt[:, j, :], first=(v == 0))
                    xg = c.x[:, bass.ds(g * GT * D, GT * D)]
                    dve.tensor_tensor(xg, xg, zt[:, :, :].rearrange("p j d -> p (j d)"), ALU.add).then_inc(sem("z_added"), 1)

                def conv(g, v):
                    for k in range(CB):
                        dve.wait_ge(sem("hp_used"), g * 8 + k + 1)
                        dve.wait_ge(sem("u_ready"), g * CB + k + 1)
                        for j in range(TAPS):
                            src = xi[:, k, v * GN + j:v * GN + j + GN]
                            if j == 0:
                                ins = dve.tensor_scalar(xc[:, k % 2, :], src, chan[:, k, 0:1], None, ALU.mult)
                            else:
                                dve.wait_ge(sem("conv_step"), (g * CB + k) * STEPS + j)
                                ins = dve.scalar_tensor_tensor(xc[:, k % 2, :], src, chan[:, k, j:j + 1], xc[:, k % 2, :],
                                                               ALU.mult, ALU.add)
                            ins.then_inc(sem("conv_step" if j < TAPS - 1 else "xc_ready"), 1)

                def softplus(g, v):
                    at = slice(v * GN, (v + 1) * GN)
                    for k in range(CB):
                        dve.wait_ge(sem("ln_ready"), g * CB + k + 1)
                        dve.tensor_tensor(delta[:, k, at], relu[:, k % 2, :], ex[:, k % 2, :], ALU.add).then_inc(sem("delta_ready"), 1)
                        dve.wait_ge(sem("delta_ready"), g * CB + k + 1 + START["delta_ready"])
                        dve.tensor_tensor(du[:, k, at], delta[:, k, at], u[:, k, at], ALU.mult).then_inc(sem("du_ready"), 1)

                def scan(b, st, k):
                    n = b * (NS * CB) + st * CB + k
                    dve.wait_ge(sem("dA_ready"), n + 1)
                    dve.wait_ge(sem("dBu_ready"), n + 1)
                    dve.wait_ge(sem("hc_ready"), n + 1)
                    dve.tensor_tensor_scan(h[:, k % 2, :], dA[:, k % 2, :], dBu[:, k % 2, :], 0.0, ALU.mult,
                                           ALU.add).then_inc(sem("h_ready"), 1)

                def times_c(b, st, k, slot):
                    n = b * (NS * CB) + st * CB + k
                    dve.wait_ge(sem("h_ready"), n + 1 + START["h_ready"])
                    dve.wait_ge(sem("hc_used"), n + 1)
                    dve.tensor_tensor(hc[:, k % 2, :], h[:, k % 2, :], bcs[:, slot, 1, :], ALU.mult).then_inc(sem("hc_ready"), 1)

                def gate(b):
                    dve.wait_ge(sem("hc_used"), b * (NS * CB) + NS * CB + START["hc_used"])
                    for k in range(CB):
                        dve.scalar_tensor_tensor(du[:, k, :], u[:, k, :], chan[:, k, 6:7],
                                                 banks[:, 2 * k:2 * k + 2, :].rearrange("p a n -> p (a n)"), ALU.mult,
                                                 ALU.add).then_inc(sem("skip_ready"), 1)
                    for k in range(CB):
                        dve.wait_ge(sem("skip_ready"), b * CB + k + 1)
                        dve.tensor_tensor(delta[:, k, :], du[:, k, :], sz[:, k, :], ALU.mult).then_inc(sem("yg_ready"), 1)

                def add(b):
                    for i in range(4):
                        dve.wait_ge(sem("out_filled"), b * 4 + i + 1)
                        at = c.x_pair(b * 4 + i)
                        dve.tensor_tensor(at, banks[:, i, :], at, ALU.add).then_inc(sem("out_used"), 1)

                for n in ("z_added", "h_ready", "hc_ready", "out_used", "delta_ready"):
                    dve.sem_inc(sem(n), START[n])
                dve.sem_inc(sem("hc_used"), START["hc_used"])
                dve.memset(wdt[:, :], 0.0).then_inc(sem("consts"), 1)
                dve.memset(xd[:, :], 0.0).then_inc(sem("consts"), 1)
                dve.memset(xi[:, :, 0:PAD], 0.0).then_inc(sem("consts"), 1)
                dve.wait_ge(sem("loaded"), 16 * 7)
                for k in range(KD):
                    dve.tensor_scalar(win[:, k, :], win[:, k, :], nw[:, k:k + 1], None, ALU.mult).then_inc(sem("w_ready"), 1)
                dve.wait_ge(sem("a_ready"), 1)
                dve.tensor_scalar(a_neg[:, :, :], a_log[:, :, :], -1.0, None, ALU.mult).then_inc(sem("a_ready"), 1)
                with dve.Fori(0, B) as b:
                    norm_group(b * 2, 0)
                    norm_group(b * 2 + 1, 1)
                    for v in range(2):
                        conv(b * 2 + v, v)
                        softplus(b * 2 + v, v)
                    scan(b, 0, 0)
                    with dve.Fori(0, NS // 2 - 1) as m:
                        for slot in range(2):
                            for k in range(CB):
                                st = m * 2 + slot
                                scan(b, *((st, k + 1) if k + 1 < CB else (st + 1, 0)))
                                times_c(b, st, k, slot)
                    for st in (NS - 2, NS - 1):
                        for k in range(CB):
                            if (st, k) != (NS - 1, CB - 1):
                                scan(b, *((st, k + 1) if k + 1 < CB else (st + 1, 0)))
                            times_c(b, st, k, st % 2)
                    gate(b)
                    add(b)


RANK = 16


def prepare_ffn(c):
    nc = c.nc
    w1T = c.keep("ffn_w1T", [P, KD, HID])
    w2T = c.keep("ffn_w2T", [P, HB, D])
    c.prepared["ffn"] = (w1T, w2T)
    with Local(c, "ffnprep") as s:
        wfc = s.sb("wfc", [P, HB, D])
        wpr = s.sb("wpr", [P, KD, HID])
        scale = s.sb("scale", [P, HB + KD])
        half = s.sb("half", [P, HB + KD])
        nhalf = s.sb("nhalf", [P, HB + KD])
        hi = s.sb("hi", [P, (HB + KD), HID])
        uT = s.sb("uT", [RANK, HID])
        fb = s.sb("fb", [RANK, RANK])
        v = s.sb("v", [RANK, D])
        gate = s.sb("gate", [RANK, 1])
        ufT = s.sb("ufT", [RANK, HID])
        pu = s.ps("pu", [RANK, 2, 512])
        pw = s.ps("pw", [P, 4, 512])
        loaded, small_loaded = s.sem("loaded"), s.sem("small_loaded")
        step, uf_ready, uf_scaled = s.sem("step"), s.sem("uf_ready"), s.sem("uf_scaled")
        tern_ready, tr_ready, tr_used = s.sem("tern_ready"), s.sem("tr_ready"), s.sem("tr_used")
        rows = [(wfc[:, b, :], hi[:, b, 0:D], D) for b in range(HB)] + \
               [(wpr[:, b, :], hi[:, HB + b, :], HID) for b in range(KD)]
        with nc.Block() as block:
            @block.sync
            def _(sp):
                sp.dma_start(wfc[:, :, :], c.ins["w_fc"].rearrange("(b p) d -> p b d", p=P)).then_inc(loaded, 16)
                sp.dma_start(wpr[:, :, :], c.ins["w_proj"].rearrange("(b p) d -> p b d", p=P)).then_inc(loaded, 16)
                sp.dma_start(uT[:, :], c.ins["uT"]).then_inc(small_loaded, 16)
                sp.dma_start(fb[:, :], c.ins["fast_b"]).then_inc(small_loaded, 16)
                sp.dma_start(v[:, :], c.ins["v"]).then_inc(small_loaded, 16)
                sp.dma_start(gate[:, :], c.ins["gate"].to_broadcast((RANK, 1))).then_inc(small_loaded, 16)

            @block.vector
            def _(dve):
                dve.wait_ge(loaded, 32)
                for i, (w, _, n) in enumerate(rows):
                    dve.tensor_reduce(scale[:, i:i + 1], w, AX.X, ALU.add, apply_absolute_value=True).then_inc(step, 1)
                dve.wait_ge(step, 10)
                dve.tensor_scalar(scale[:, 0:HB], scale[:, 0:HB], 1.0 / D, EPS, ALU.mult, ALU.max).then_inc(step, 1)
                dve.tensor_scalar(scale[:, HB:], scale[:, HB:], 1.0 / HID, EPS, ALU.mult, ALU.max).then_inc(step, 1)
                dve.wait_ge(step, 12)
                dve.tensor_scalar(half[:, :], scale[:, :], 0.5, None, ALU.mult).then_inc(step, 1)
                dve.tensor_scalar(nhalf[:, :], scale[:, :], -0.5, None, ALU.mult).then_inc(step, 1)
                dve.wait_ge(step, 14)
                for i, (w, up, n) in enumerate(rows):
                    dve.tensor_scalar(up, w, half[:, i:i + 1], scale[:, i:i + 1], ALU.is_gt, ALU.mult).then_inc(step, 1)
                    dve.wait_ge(step, 15 + 2 * i)
                    dve.tensor_scalar(w, w, nhalf[:, i:i + 1], scale[:, i:i + 1], ALU.is_lt, ALU.mult).then_inc(step, 1)
                    dve.wait_ge(step, 16 + 2 * i)
                    dve.tensor_tensor(w, up, w, ALU.subtract).then_inc(tern_ready, 1)
                dve.wait_ge(uf_ready, 1)
                dve.wait_ge(small_loaded, 64)
                dve.tensor_scalar(ufT[:, :], pu[:, :, :].rearrange("p a n -> p (a n)"), gate[:, 0:1], None,
                                  ALU.mult).then_inc(uf_scaled, 1)

            @block.tensor
            def _(pe):
                pe.wait_ge(small_loaded, 64)
                for n in range(2):
                    mm = pe.matmul(pu[:, n, :], fb[:, :], uT[:, n * 512:(n + 1) * 512], start=True, stop=True)
                mm.then_inc(uf_ready, 1)
                pe.wait_ge(uf_scaled, 1)
                pe.wait_ge(tern_ready, HB + KD)
                for k in range(KD):
                    for n in range(2):
                        for b in range(4):
                            pe.matmul(pw[:, 2 * k + n, b * P:(b + 1) * P], wfc[:, 4 * n + b, k * P:(k + 1) * P],
                                      c.ident[:, :], start=(b == 0), stop=False, skip_group_check=True)
                        mm = pe.matmul(pw[:, 2 * k + n, :], v[:, k * P:(k + 1) * P], ufT[:, n * 512:(n + 1) * 512],
                                       start=False, stop=True, skip_group_check=True)
                        mm.then_inc(tr_ready, 1)
                for b in range(0, HB, 2):
                    pe.wait_ge(tr_used, b // 2 + 1)
                    for i in range(2):
                        for k in range(KD):
                            mm = pe.transpose(pw[:, b // 2, i * D + k * P:i * D + (k + 1) * P],
                                              wpr[:, k, (b + i) * P:(b + i + 1) * P], c.ident[:, :])
                    mm.then_inc(tr_ready, 1)

            @block.scalar
            def _(act):
                for i in range(4):
                    act.wait_ge(tr_ready, i + 1)
                    act.copy(w1T[:, i // 2, (i % 2) * 512:(i % 2 + 1) * 512], pw[:, i, :]).then_inc(tr_used, 1)
                for i in range(4):
                    act.wait_ge(tr_ready, 5 + i)
                    act.copy(w2T[:, 2 * i:2 * i + 2, :].rearrange("p a n -> p (a n)"), pw[:, i, :]).then_inc(tr_used, 1)


def stage_ffn(c, name):
    nc = c.nc
    w1T, w2T = c.prepared["ffn"]
    with Local(c, name) as s:
        norm = Norm(c, s)
        r = s.sb("relu", [P, 2, GN])
        h = s.sb("h", [P, HB, GN])
        hp = s.ps("hp", [P, 4, GN])
        yp = s.ps("yp", [P, GT, D])
        h_filled, relu_ready, h_ready = s.sem("h_filled"), s.sem("relu_ready"), s.sem("h_ready")
        y_ready, y_used = s.sem("y_ready"), s.sem("y_used")
        with nc.Block() as block:
            @block.tensor
            def _(pe):
                def up(g, first=False):
                    pe.wait_ge(norm.xT_ready, g * KD + KD)
                    for b in range(HB):
                        if not (first and b < 4):
                            pe.wait_ge(h_ready, g * HB + b - 3)
                        for k in range(KD):
                            mm = pe.matmul(hp[:, b % 4, :], w1T[:, k, b * P:(b + 1) * P], norm.xT[:, k, :],
                                           start=(k == 0), stop=(k == KD - 1))
                        mm.then_inc(h_filled, 1)

                def down(g, first=False):
                    pe.wait_ge(h_ready, g * HB + HB)
                    for j in range(GT):
                        if j % 2 == 0 and not first:
                            pe.wait_ge(y_used, g * 2 - 1 + j // 2)
                        for b in range(HB):
                            mm = pe.matmul(yp[:, j, :], h[:, b, j * P:(j + 1) * P], w2T[:, b, :],
                                           start=(b == 0), stop=(b == HB - 1))
                        if j % 2 == 1:
                            mm.then_inc(y_ready, 1)

                norm.transposes(pe, 0, first=True)
                up(0, first=True)
                norm.transposes(pe, 1)
                down(0, first=True)
                up(1)
                with pe.Fori(2, G) as g:
                    norm.transposes(pe, g)
                    down(g - 1)
                    up(g)
                down(G - 1)

            @block.gpsimd
            def _(pool):
                norm.pool_prologue(pool)
                norm.power(pool, 0)
                with pool.Fori(1, G) as g:
                    norm.power(pool, g)

            @block.scalar
            def _(act):
                def relu(g, first=False):
                    for b in range(HB):
                        act.wait_ge(h_filled, g * HB + b + 1)
                        if not (first and b < 2):
                            act.wait_ge(h_ready, g * HB + b - 1)
                        act.activation(r[:, b % 2, :], hp[:, b % 4, :], ACT.Relu).then_inc(relu_ready, 1)

                norm.copy_out(act, 0)
                relu(0, first=True)
                with act.Fori(1, G) as g:
                    norm.copy_out(act, g, h_filled, g * HB)
                    relu(g)

            @block.vector
            def _(dve):
                def square(g, first=False):
                    for b in range(HB):
                        dve.wait_ge(relu_ready, g * HB + b + 1)
                        if b == 0 and not first:
                            dve.wait_ge(y_ready, g * 2)
                        dve.tensor_tensor(h[:, b, :], r[:, b % 2, :], r[:, b % 2, :], ALU.mult).then_inc(h_ready, 1)

                def add(g):
                    for i in range(2):
                        dve.wait_ge(y_ready, g * 2 + i + 1)
                        pair = c.x_pair(g * 2 + i)
                        dve.tensor_tensor(pair, yp[:, 2 * i:2 * i + 2, :].rearrange("p a n -> p (a n)"), pair,
                                          ALU.add).then_inc(y_used, 1)

                norm.moments(dve, 0)
                norm.normalise(dve, 0, first=True)
                norm.moments(dve, 1)
                norm.normalise(dve, 1)
                square(0, first=True)
                with dve.Fori(1, G - 1) as g:
                    norm.moments(dve, g + 1)
                    add(g - 1)
                    norm.normalise(dve, g + 1)
                    square(g)
                add(G - 2)
                square(G - 1)
                add(G - 1)


AH, AD = 16, 16
PARTS = 6
KS = PARTS * AD
KM = KS + 2
Q_TILES = L // P
CHUNKS = 12
HG = 4
VP = 32
ST = 3
LORA_SCALE = 4.0
LORA_R = 8


def stage_attn(c):
    nc = c.nc
    with Local(c, "attn") as s:
        banks = s.ps("banks", [P, 8, 512])
        norm = Norm(c, s, trp=banks[:, 0:2, :])
        w = s.sb("w", [P, KD, 3 * D])
        wo = s.sb("wo", [P, KD, D])
        loraA = s.sb("loraA", [LORA_R, 2, D])
        loraB = s.sb("loraB", [LORA_R, 2, D])
        rope = s.sb("rope", [P, Q_TILES, 2, AD])
        causal32 = s.sb("causal32", [P, 3, P])
        causal = s.sb("causal", [P, 3, P], BF16)
        ra = s.sb("ra", [P, 2, 2 * AH, AD])
        rb = s.sb("rb", [P, 2, 2 * AH, AD])
        r = s.sb("r", [P, 2, 2 * AH, AD])
        r1 = s.sb("r1", [P, 2, 2 * AH, AD])
        stk = s.sb("stk", [P, 4, 2 * AH, KM], BF16)
        qT = s.sb("qT", [KM, AH, L], BF16)
        kT = s.sb("kT", [KM, AH, L], BF16)
        v = s.sb("v", [P, Q_TILES, AH, AD])
        vh = s.sb("vh", [P, HG, Q_TILES, VP])
        mp = s.sb("mp", [P, 2, Q_TILES, 2])
        nm = s.sb("nm", [P, 2, Q_TILES])
        nmb = s.sb("nmb", [P, 2, 2, Q_TILES], BF16)
        nmT = s.sb("nmT", [2 * Q_TILES, P], BF16)
        probs = s.sb("probs", [P, ST, 512])
        ov = ra[:, :, :, :].rearrange("p a h d -> p (a h d)")
        rec = s.sb("rec", [P, 2, GT, HG])
        o = s.sb("o", [P, Q_TILES, D])
        oT = s.sb("oT", [P, KD, GN])
        names = ("loaded lora_filled w_ready qkv_filled qp_used roped r_ready p1_ready r1_ready p2_ready p3_ready dup_ready "
                 "stT_filled evac_act evac_dve sa_filled sa_used max_ready part_ready m_ready mt_filled mt_copied "
                 "m_loaded st_filled exp_ready pv_done vh_ready ov_ready ot_filled rec_ready o_used oT_filled oT_ready y_ready y_used consts zeroed parts_seen")
        S = {n: s.sem(n) for n in names.split()}

        def sem(n):
            return S[n]

        START = {"qp_used": 2, "p3_ready": 2, "r_ready": 2, "r1_ready": 2, "evac_act": 1, "evac_dve": 1, "sa_used": 2,
                 "exp_ready": ST + 2 * CHUNKS, "pv_done": ST + HG * CHUNKS, "vh_ready": 1, "ov_ready": 2, "ot_filled": 2,
                 "mt_copied": 1, "m_loaded": 16, "o_used": 1, "oT_ready": 1, "y_used": 1}
        bf = [banks[:, i, :].bitcast(BF16).rearrange("p (h n) -> p h n", n=P) for i in range(8)]
        LAST = Q_TILES + 2

        def chunks(qt):
            return [(0, 512), (512, (qt + 1) * P - 512)] if qt >= 4 else [(0, (qt + 1) * P)]

        STEPS = [(kt, half, max(kt * P, half * 512), (half + 1) * 512 - max(kt * P, half * 512))
                 for kt in range(Q_TILES) for half in range(kt // GT, 2)]
        A_CHUNKS = [(qt, half, at, size) for qt in reversed(range(Q_TILES)) for half, (at, size) in enumerate(chunks(qt))]

        def head_loop(engine, body):
            body(0, 0, 0)
            with engine.Fori(0, HG - 1) as hh:
                for j in range(1, HG):
                    body(hh * HG + j, hh, j)
                body(hh * HG + HG, hh + 1, 0)
            for h in range(AH - HG + 1, AH):
                body(h, h // HG, h % HG)

        with nc.Block() as block:
            @block.sync
            def _(sp):
                sp.sem_inc(sem("m_loaded"), START["m_loaded"])
                for i, n in enumerate(("attn_wq", "attn_wk", "attn_wv")):
                    sp.dma_start(w[:, :, i * D:(i + 1) * D], c.ins[n].rearrange("(k p) n -> p k n", p=P)).then_inc(sem("loaded"), 16)
                sp.dma_start(wo[:, :, :], c.ins["attn_wo"].rearrange("(k p) n -> p k n", p=P)).then_inc(sem("loaded"), 16)
                for i, n in enumerate("qv"):
                    sp.dma_start(loraA[:, i, :], c.ins[f"attn_A{n}T"]).then_inc(sem("loaded"), 16)
                    sp.dma_start(loraB[:, i, :], c.ins[f"attn_B{n}"]).then_inc(sem("loaded"), 16)
                sp.dma_start(rope[:, :, :, :].rearrange("p t a d -> p t (a d)"), c.ins["rope"]).then_inc(sem("loaded"), 16)
                sp.dma_start(causal32[:, :, :], c.ins["causal"]).then_inc(sem("loaded"), 16)
                with sp.Fori(0, B) as b:
                    with sp.Fori(0, AH) as h:
                        sp.wait_ge(sem("mt_copied"), b * AH + h + 2)
                        sp.dma_start(qT[KS:KM, bass.ds(h, 1), :], nmT[:, :]).then_inc(sem("m_loaded"), 16)

            @block.tensor
            def _(pe):
                def project(b, t):
                    at, j = 2 + 2 * (t % 2), t % GT
                    pe.wait_ge(sem("qp_used"), b * Q_TILES + t + 1)
                    for n, size, bank in ((0, 512, at), (512, 256, at + 1)):
                        for k in range(KD):
                            mm = pe.matmul(banks[:, bank, 0:size], norm.xT[:, k, j * P:(j + 1) * P], w[:, k, n:n + size],
                                           start=(k == 0), stop=(k == KD - 1))
                    mm.then_inc(sem("qkv_filled"), 1)

                def stack_transposes(b, t):
                    T0 = b * Q_TILES + t
                    pe.wait_ge(sem("p3_ready"), T0 + 3)
                    pe.wait_ge(sem("dup_ready"), T0 + 1)
                    for i in range(4):
                        if i == 0:
                            pe.wait_ge(sem("evac_act"), T0 * 3 + 1)
                        if i == 2:
                            pe.wait_ge(sem("evac_act"), T0 * 3 + 2)
                        if i == 3:
                            pe.wait_ge(sem("evac_dve"), T0 + 2)
                        for n in range(8):
                            mm = pe.transpose(bf[6 + i % 2][0:KM, n, :], stk[:, t % 4, i * 8 + n, :], causal[:, 2, :])
                        mm.then_inc(sem("stT_filled"), 1)

                def scores_q(b, h, i):
                    qt, half, at, size = A_CHUNKS[i]
                    pe.wait_ge(sem("sa_used"), (b * AH + h) * CHUNKS + i + 1)
                    diag = at + size == (qt + 1) * P
                    mm = pe.matmul(banks[:, i % 2, 0:size], qT[0:KS, bass.ds(h, 1), qt * P:(qt + 1) * P],
                                   kT[0:KS, bass.ds(h, 1), at:at + size], start=True, stop=not diag, skip_group_check=True)
                    if diag:
                        mm = pe.matmul(banks[:, i % 2, size - P:size], causal[:, 2, :], causal[:, 0, :],
                                       start=False, stop=True, skip_group_check=True)
                    mm.then_inc(sem("sa_filled"), 1)

                def scores_k(b, h, i):
                    H = b * AH + h
                    kt, _, at, size = STEPS[i]
                    if i == 0:
                        pe.wait_ge(sem("m_loaded"), H * 16 + 32)
                    pe.wait_ge(sem("exp_ready"), (H + 2) * CHUNKS + i + 1)
                    diag = at == kt * P
                    mm = pe.matmul(banks[:, 2 + i % ST, 0:size], kT[:, bass.ds(h, 1), kt * P:(kt + 1) * P],
                                   qT[:, bass.ds(h, 1), at:at + size], start=True, stop=not diag, skip_group_check=True)
                    if diag:
                        mm = pe.matmul(banks[:, 2 + i % ST, 0:P], causal[:, 2, :], causal[:, 1, :],
                                       start=False, stop=True, skip_group_check=True)
                    mm.then_inc(sem("st_filled"), 1)

                def values(b, h, hg, j, i, before=0):
                    kt, half, at, size = STEPS[i]
                    H = b * AH + h - before
                    pe.wait_ge(sem("exp_ready"), (H + 2) * CHUNKS + i + 1 + ST)
                    if i == 0:
                        pe.wait_ge(sem("vh_ready"), H + 2)
                    if kt == 0 and j == 0:
                        pe.wait_ge(sem("ov_ready"), b * (2 * AH // HG) + hg * 2 + half + 1)
                    pe.matmul(banks[j * VP:(j + 1) * VP, 6 + half, at - half * 512:at - half * 512 + size], vh[:, j, kt, :],
                              probs[:, i % ST, 0:size], start=(kt == 0), stop=(at == kt * P and (kt + 1) % GT == 0),
                              skip_group_check=True).then_inc(sem("pv_done"), 1)

                def max_transpose(b, h, slot):
                    H = b * AH + h
                    pe.wait_ge(sem("m_ready"), H + 1)
                    pe.wait_ge(sem("mt_copied"), H + 1)
                    pe.transpose(bf[5][0:2 * Q_TILES, 0, :], nmb[:, slot, :, :].rearrange("p a q -> p (a q)"),
                                 causal[:, 2, :]).then_inc(sem("mt_filled"), 1)

                def turn(b, hg, u, copied):
                    R = b * (2 * AH // HG) + hg * 2 + u
                    pe.wait_ge(sem("ov_ready"), b * (2 * AH // HG) + hg * 2 + u + 3)
                    pe.wait_ge(sem("o_used"), R + 1)
                    pe.wait_ge(sem("mt_copied"), copied)
                    for n in range(GT):
                        mm = pe.transpose(banks[:, 5, n * P:(n + 1) * P], ov[:, (u * GT + n) * P:(u * GT + n + 1) * P],
                                          c.ident[:, :])
                    mm.then_inc(sem("ot_filled"), 1)

                def body(b, h, hg, j):
                    peeled = isinstance(h, int)
                    for i in range(CHUNKS):
                        scores_k(b, h, i)
                        if not (peeled and h >= AH - 2):
                            scores_q(b, h + 2, i)
                        if i >= 2:
                            values(b, h, hg, j, i - 2)
                        elif not (peeled and h == 0):
                            values(b, h, hg, (j - 1) % HG, CHUNKS - 2 + i, before=1)
                        if i == 3 and not (peeled and h == AH - 1):
                            if not (peeled and h == 0):
                                pe.wait_ge(sem("o_used"), b * (2 * AH // HG) + (hg if j else hg - 1) * 2 + 1)
                            max_transpose(b, h + 1, (j + 1) % 2)
                        if j == 0 and not (peeled and h == 0) and i in (6, 10):
                            turn(b, hg - 1, (i - 6) // 4, b * AH + h + 3)

                pe.sem_inc(sem("pv_done"), START["pv_done"])
                pe.sem_inc(sem("ot_filled"), START["ot_filled"])
                pe.wait_ge(sem("loaded"), 16 * 10)
                for i in range(2):
                    for k in range(KD):
                        mm = pe.matmul(banks[:, i, k * D:(k + 1) * D], loraA[:, i, k * P:(k + 1) * P], loraB[:, i, :],
                                       start=True, stop=True)
                mm.then_inc(sem("lora_filled"), 1)
                pe.wait_ge(sem("w_ready"), 2 * KD)
                pe.wait_ge(sem("consts"), 3)
                with pe.Fori(0, B) as b:
                    pe.wait_ge(sem("sa_used"), b * (AH * CHUNKS) + START["sa_used"])
                    pe.wait_ge(sem("ov_ready"), b * (2 * AH // HG) + START["ov_ready"])
                    pe.wait_ge(sem("mt_copied"), b * AH + 1)
                    pe.wait_ge(sem("y_used"), b * 2 + 1)
                    for t in range(-1, LAST):
                        if t + 1 < Q_TILES:
                            if (t + 1) % GT == 0:
                                g = b * 2 + (t + 1) // GT
                                if t + 1 == 0:
                                    pe.wait_ge(sem("oT_ready"), b * (2 * KD) + 1)
                                else:
                                    pe.wait_ge(norm.xT_ready, g * KD)
                                norm.transposes(pe, g, first=True)
                                pe.wait_ge(norm.xT_ready, g * KD + KD)
                            project(b, t + 1)
                        if t >= 2:
                            stack_transposes(b, t - 2)
                    pe.wait_ge(sem("qp_used"), b * Q_TILES + Q_TILES + START["qp_used"])
                    pe.wait_ge(sem("evac_act"), (b * Q_TILES + Q_TILES) * 3 + 1)
                    pe.wait_ge(sem("evac_dve"), b * Q_TILES + Q_TILES + 1)
                    for i in range(CHUNKS):
                        scores_q(b, 0, i)
                    for i in range(CHUNKS):
                        scores_q(b, 1, i)
                        if i == 5:
                            max_transpose(b, 0, 0)
                    head_loop(pe, lambda h, hg, j: body(b, h, hg, j))
                    for i in (CHUNKS - 2, CHUNKS - 1):
                        values(b, AH, 0, HG - 1, i, before=1)
                    for u in range(2):
                        turn(b, AH // HG - 1, u, b * AH + AH + 1)
                    pe.wait_ge(sem("o_used"), (b + 1) * (2 * AH // HG) + 1)
                    for u in range(2):
                        pe.wait_ge(sem("oT_ready"), (b * 2 + u) * KD + 1)
                        for k in range(KD):
                            for j in range(GT):
                                mm = pe.transpose(banks[:, k, j * P:(j + 1) * P], o[:, u * GT + j, k * P:(k + 1) * P],
                                                  c.ident[:, :])
                        mm.then_inc(sem("oT_filled"), 1)
                        pe.wait_ge(sem("oT_ready"), (b * 2 + u) * KD + KD + 1)
                        if u > 0:
                            pe.wait_ge(sem("y_used"), b * 2 + u + 1)
                        for j in range(GT):
                            for k in range(KD):
                                mm = pe.matmul(banks[:, 2 + j // 2, (j % 2) * D:(j % 2 + 1) * D], oT[:, k, j * P:(j + 1) * P],
                                               wo[:, k, :], start=(k == 0), stop=(k == KD - 1))
                        mm.then_inc(sem("y_ready"), 1)

            @block.gpsimd
            def _(pool):
                norm.pool_prologue(pool)
                pool.sem_inc(sem("r_ready"), START["r_ready"])
                pool.sem_inc(sem("vh_ready"), START["vh_ready"])
                with pool.Fori(0, B) as b:
                    norm.power(pool, b * 2)
                    norm.power(pool, b * 2 + 1)
                    for t in range(Q_TILES + 1):
                        if t < Q_TILES:
                            T0 = b * Q_TILES + t
                            pool.wait_ge(sem("roped"), T0 + 1)
                            pool.wait_ge(sem("r1_ready"), T0 + 1)
                            pool.tensor_tensor(r[:, t % 2], ra[:, t % 2], rb[:, t % 2], ALU.add).then_inc(sem("r_ready"), 1)
                        if t >= 1:
                            m = t - 1
                            st = stk[:, m % 4, :, 0:KS].rearrange("p h (a d) -> p h a d", d=AD)
                            pool.wait_ge(sem("p1_ready"), b * Q_TILES + m + 1)
                            pool.sem_inc(sem("parts_seen"), 1)
                            pool.tensor_copy(st[:, 0:AH, 1, :], st[:, 0:AH, 0, :])
                            pool.tensor_copy(st[:, 0:AH, 2, :], st[:, 0:AH, 0, :])
                            pool.tensor_copy(st[:, AH:, 3, :], st[:, AH:, 0, :]).then_inc(sem("dup_ready"), 1)
                    pool.wait_ge(sem("qp_used"), b * Q_TILES + Q_TILES + START["qp_used"])
                    pool.sem_inc(sem("parts_seen"), 1)
                    with pool.Fori(0, AH // HG) as hg:
                        for j in range(HG):
                            H = b * AH + hg * HG + j
                            pool.wait_ge(sem("pv_done"), H * CHUNKS + ST + CHUNKS)
                            pool.sem_inc(sem("parts_seen"), 1)
                            pool.tensor_copy(vh[:, j, :, 0:AD], v[:, :, bass.ds(hg * HG + j, 1), :].rearrange("p t h d -> p t (h d)"))\
                                .then_inc(sem("vh_ready"), 1)

            @block.scalar
            def _(act):
                def evac(b, t, i):
                    act.wait_ge(sem("stT_filled"), (b * Q_TILES + t) * 4 + i + 1)
                    rows = KS if i < 2 else KM
                    dst = (qT if i < 2 else kT)[0:rows, (i % 2) * 8:(i % 2) * 8 + 8, t * P:(t + 1) * P]
                    act.copy(dst, bf[6 + i % 2][0:rows, :, :]).then_inc(sem("evac_act"), 1)

                def first_part(b, t):
                    T0 = b * Q_TILES + t
                    act.wait_ge(sem("r_ready"), T0 + 3)
                    if t >= 4:
                        act.wait_ge(sem("stT_filled"), b * (Q_TILES * 4) + (t - 3) * 4)
                    act.copy(stk[:, t % 4, :, 0:AD], r[:, t % 2]).then_inc(sem("p1_ready"), 1)

                def second_part(b, t):
                    act.wait_ge(sem("r1_ready"), b * Q_TILES + t + 3)
                    act.copy(stk[:, t % 4, :, 4 * AD:5 * AD], r1[:, t % 2]).then_inc(sem("p2_ready"), 1)

                def exps(b, h, i):
                    H = b * AH + h
                    size = STEPS[i][3]
                    act.wait_ge(sem("st_filled"), H * CHUNKS + i + 1)
                    act.wait_ge(sem("pv_done"), H * CHUNKS + i + 1 + HG * CHUNKS)
                    act.activation(probs[:, i % ST, 0:size], banks[:, 2 + i % ST, 0:size], ACT.Exp, scale=AD ** -0.5)\
                       .then_inc(sem("exp_ready"), 1)

                def copy_max(b, h):
                    H = b * AH + h
                    act.wait_ge(sem("mt_filled"), H + 1)
                    act.wait_ge(sem("m_loaded"), H * 16 + 16)
                    act.copy(nmT[:, :], bf[5][0:2 * Q_TILES, 0, :]).then_inc(sem("mt_copied"), 1)

                def copy_sums(b, hg, u):
                    H = b * AH + hg * HG + HG - 1
                    act.wait_ge(sem("pv_done"), H * CHUNKS + (7, 12)[u] + START["pv_done"])
                    act.wait_ge(sem("ot_filled"), b * (2 * AH // HG) + hg * 2 + u + 1)
                    act.copy(ov[:, u * 512:(u + 1) * 512], banks[:, 6 + u, :]).then_inc(sem("ov_ready"), 1)

                def body(b, h, hg, j):
                    peeled = isinstance(h, int)
                    for i in range(CHUNKS):
                        exps(b, h, i)
                        if i == 1 and j == 0 and not (peeled and h == 0):
                            copy_sums(b, hg - 1, 1)
                        if i == 4 and not (peeled and h == AH - 1):
                            copy_max(b, h + 1)
                        if i == 9 and j == HG - 1:
                            copy_sums(b, hg, 0)

                for n in ("evac_act", "exp_ready", "mt_copied", "oT_ready", "ov_ready"):
                    act.sem_inc(sem(n), START[n])
                act.wait_ge(sem("loaded"), 16 * 10)
                act.copy(causal[:, :, :], causal32[:, :, :]).then_inc(sem("consts"), 1)
                with act.Fori(0, B) as b:
                    for t in range(LAST):
                        if t < Q_TILES:
                            if t == 0:
                                norm.copy_out(act, b * 2)
                            if t == GT - 1:
                                norm.copy_out(act, b * 2 + 1, sem("qkv_filled"), b * Q_TILES + GT)
                        if 1 <= t <= Q_TILES:
                            first_part(b, t - 1)
                        if t >= 2:
                            evac(b, t - 2, 0)
                        if 1 <= t <= Q_TILES:
                            second_part(b, t - 1)
                        if t >= 2:
                            evac(b, t - 2, 2)
                            evac(b, t - 2, 3)
                    copy_max(b, 0)
                    head_loop(act, lambda h, hg, j: body(b, h, hg, j))
                    copy_sums(b, AH // HG - 1, 1)
                    for u in range(2):
                        act.wait_ge(sem("oT_filled"), b * 2 + u + 1)
                        if u > 0:
                            act.wait_ge(sem("y_ready"), b * 2 + u)
                        for k in range(KD):
                            act.copy(oT[:, k, :], banks[:, k, :]).then_inc(sem("oT_ready"), 1)

            @block.vector
            def _(dve):
                def rotate(b, t):
                    T0 = b * Q_TILES + t
                    at = 2 + 2 * (t % 2)
                    dve.wait_ge(sem("qkv_filled"), T0 + 1)
                    dve.wait_ge(sem("r_ready"), T0 + 1)
                    qk = banks[:, at, :].rearrange("p (h d) -> p h d", d=AD)
                    qk2 = banks[:, at, :].rearrange("p (h d two) -> p h d two", d=AD // 2, two=2)
                    rb2 = rb[:, t % 2].rearrange("p h (d two) -> p h d two", two=2)
                    sn = rope[:, t, 1, :].rearrange("p (d two) -> p d two", two=2)
                    dve.tensor_tensor(ra[:, t % 2], qk, rope[:, t, 0, :].unsqueeze(1).to_broadcast((P, 2 * AH, AD)), ALU.mult)
                    for e in range(2):
                        last = dve.tensor_tensor(rb2[:, :, :, e], qk2[:, :, :, 1 - e],
                                                 sn[:, :, e].unsqueeze(1).to_broadcast((P, 2 * AH, AD // 2)), ALU.mult)
                    last.then_inc(sem("roped"), 1)
                    if t == 0:
                        dve.wait_ge(sem("vh_ready"), b * AH + START["vh_ready"])
                    dve.tensor_copy(v[:, t, :, :], banks[:, at + 1, 0:D].rearrange("p (h d) -> p h d", d=AD))\
                       .then_inc(sem("qp_used"), 1)

                def remainder(b, t):
                    dve.wait_ge(sem("p1_ready"), b * Q_TILES + t + 1)
                    dve.wait_ge(sem("p3_ready"), b * Q_TILES + t + 1)
                    dve.tensor_tensor(r1[:, t % 2], r[:, t % 2], stk[:, t % 4, :, 0:AD], ALU.subtract).then_inc(sem("r1_ready"), 1)

                def third_part(b, t):
                    dve.wait_ge(sem("p2_ready"), b * Q_TILES + t + 1)
                    st, rr = stk[:, t % 4], r1[:, t % 2]
                    dve.tensor_copy(st[:, AH:, 5 * AD:6 * AD], st[:, AH:, 0:AD])
                    dve.tensor_copy(st[:, 0:AH, 3 * AD:4 * AD], st[:, 0:AH, 4 * AD:5 * AD])
                    dve.tensor_copy(st[:, AH:, AD:2 * AD], st[:, AH:, 4 * AD:5 * AD])
                    dve.tensor_tensor(st[:, 0:AH, 5 * AD:6 * AD], rr[:, 0:AH], st[:, 0:AH, 4 * AD:5 * AD], ALU.subtract)
                    dve.tensor_tensor(st[:, AH:, 2 * AD:3 * AD], rr[:, AH:], st[:, AH:, 4 * AD:5 * AD], ALU.subtract)\
                       .then_inc(sem("p3_ready"), 1)

                def evac(b, t):
                    dve.wait_ge(sem("stT_filled"), (b * Q_TILES + t) * 4 + 2)
                    dve.tensor_copy(qT[0:KS, 8:16, t * P:(t + 1) * P], bf[7][0:KS, :, :]).then_inc(sem("evac_dve"), 1)

                def chunk_max(b, h, slot, i):
                    qt, half, _, size = A_CHUNKS[i]
                    dve.wait_ge(sem("sa_filled"), (b * AH + h) * CHUNKS + i + 1)
                    dve.tensor_reduce(mp[:, slot, qt, half:half + 1], banks[:, i % 2, 0:size], AX.X,
                                      ALU.max).then_inc(sem("sa_used"), 1)

                def head_max(b, h, slot):
                    H = b * AH + h
                    dve.wait_ge(sem("sa_used"), H * CHUNKS + CHUNKS + START["sa_used"])
                    dve.tensor_reduce(nm[:, slot, :], mp[:, slot, :, :], AX.X, ALU.max, negate=True).then_inc(sem("max_ready"), 1)
                    dve.wait_ge(sem("max_ready"), H + 1)
                    dve.tensor_copy(nmb[:, slot, 0, :], nm[:, slot, :]).then_inc(sem("part_ready"), 1)
                    dve.wait_ge(sem("part_ready"), H + 1)
                    dve.tensor_tensor(nmb[:, slot, 1, :], nm[:, slot, :], nmb[:, slot, 0, :], ALU.subtract).then_inc(sem("m_ready"), 1)

                def normalise(b, hg, u):
                    R = b * (2 * AH // HG) + hg * 2 + u
                    dve.wait_ge(sem("ot_filled"), R + 1 + START["ot_filled"])
                    oo = banks[:, 5, :].rearrange("p (q j d) -> p q j d", j=HG, d=VP)
                    dve.reciprocal(rec[:, u, :, :], oo[:, :, :, AD]).then_inc(sem("rec_ready"), 1)
                    dve.wait_ge(sem("rec_ready"), R + 1)
                    for n in range(GT):
                        last = dve.tensor_tensor(o[:, u * GT + n, bass.ds(hg * (HG * AD), HG * AD)].rearrange("p (j d) -> p j d", d=AD),
                                                 oo[:, n, :, 0:AD],
                                                 rec[:, u, n, :].unsqueeze(2).to_broadcast((P, HG, AD)), ALU.mult)
                    last.then_inc(sem("o_used"), 1)

                def body(b, h, hg, j):
                    peeled = isinstance(h, int)
                    for i in range(CHUNKS):
                        if not (peeled and h >= AH - 2):
                            chunk_max(b, h + 2, j % 2, i)
                        if j == 0 and not (peeled and h == 0) and i in (6, 10):
                            normalise(b, hg - 1, (i - 6) // 4)
                    if not (peeled and h >= AH - 2):
                        head_max(b, h + 2, j % 2)

                for n in ("qp_used", "p3_ready", "r1_ready", "evac_dve", "sa_used", "o_used", "y_used"):
                    dve.sem_inc(sem(n), START[n])
                dve.memset(stk[:, :, :, KS:KM], 1.0).then_inc(sem("consts"), 1)
                dve.memset(vh[:, :, :, :], 0.0).then_inc(sem("zeroed"), 1)
                dve.wait_ge(sem("zeroed"), 1)
                dve.memset(vh[:, :, :, AD:AD + 1], 1.0)
                dve.memset(mp[:, :, :, :], -3e38).then_inc(sem("consts"), 1)
                dve.wait_ge(sem("loaded"), 16 * 10)
                dve.wait_ge(sem("lora_filled"), 1)
                for i, n in ((0, 0), (1, 2)):
                    for k in range(KD):
                        dve.scalar_tensor_tensor(w[:, k, n * D:(n + 1) * D], banks[:, i, k * D:(k + 1) * D], LORA_SCALE,
                                                 w[:, k, n * D:(n + 1) * D], ALU.mult, ALU.add).then_inc(sem("w_ready"), 1)
                with dve.Fori(0, B) as b:
                    norm.moments(dve, b * 2)
                    norm.normalise(dve, b * 2, first=True)
                    norm.moments(dve, b * 2 + 1)
                    norm.normalise(dve, b * 2 + 1)
                    for t in range(LAST):
                        if t < Q_TILES:
                            rotate(b, t)
                        if t >= 2:
                            evac(b, t - 2)
                        if 1 <= t <= Q_TILES:
                            remainder(b, t - 1)
                            third_part(b, t - 1)
                    for h in range(2):
                        for i in range(CHUNKS):
                            chunk_max(b, h, h, i)
                        head_max(b, h, h)
                    head_loop(dve, lambda h, hg, j: body(b, h, hg, j))
                    for u in range(2):
                        normalise(b, AH // HG - 1, u)
                    for u in range(2):
                        dve.wait_ge(sem("y_ready"), b * 2 + u + 1)
                        at = c.x[:, bass.ds((b * 2 + u) * GT * D, GT * D)]
                        dve.tensor_tensor(at, banks[:, 2:4, :].rearrange("p a n -> p (a n)"), at, ALU.add)\
                           .then_inc(sem("y_used"), 1)


NH, HDIM = 16, 16
SEQ = B
LIN_SCALE = HDIM ** -0.5 * SEQ ** -0.5


def stage_lin(c):
    nc = c.nc
    with Local(c, "lin") as s:
        norm = Norm(c, s, tile=lambda g, j: j * G + g)
        wT = s.sb("wT", [P, KD, 3 * D])
        bias = s.sb("bias", [P, 3 * D])
        qkv = s.sb("qkv", [P, SEQ, 3, D])
        score = s.sb("score", [P, SEQ, SEQ * NH])
        qk = s.sb("qk", [P, 2, SEQ * D])
        pv = s.sb("pv", [P, SEQ, SEQ * D])
        qp = s.ps("qp", [P, 2, 1024])
        yp = s.ps("yp", [P, SEQ, D])
        loaded, qkv_filled, qkv_ready = s.sem("loaded"), s.sem("qkv_filled"), s.sem("qkv_ready")
        suffix_ready, qk_ready, score_ready = s.sem("suffix_ready"), s.sem("qk_ready"), s.sem("score_ready")
        pv_ready, y_ready, y_used = s.sem("pv_ready"), s.sem("y_ready"), s.sem("y_used")
        x4 = c.x[:, :].rearrange("p (q n) -> p q n", q=SEQ)
        with nc.Block() as block:
            @block.sync
            def _(sp):
                sp.dma_start(wT[:, :, :], c.ins["lin_wT"].rearrange("(k p) n -> p k n", p=P)).then_inc(loaded, 16)
                sp.dma_start(bias[:, :], c.ins["lin_b"].to_broadcast((P, 3 * D))).then_inc(loaded, 16)

            @block.tensor
            def _(pe):
                def project(g, first=False):
                    pe.wait_ge(norm.xT_ready, g * KD + KD)
                    for j in range(SEQ):
                        if not (first and j < 2):
                            pe.wait_ge(qkv_ready, g * SEQ + j - 1)
                        for n, size in ((0, 512), (512, 256)):
                            for k in range(KD):
                                mm = pe.matmul(qp[:, j % 2, n:n + size], norm.xT[:, k, j * P:(j + 1) * P],
                                               wT[:, k, n:n + size], start=(k == 0), stop=(k == KD - 1))
                        mm.then_inc(qkv_filled, 1)

                def sums(g, first=False):
                    for q in range(SEQ):
                        pe.wait_ge(pv_ready, g * SEQ + q + 1)
                        if q % 2 == 0 and not first:
                            pe.wait_ge(y_used, g * 2 - 1 + q // 2)
                        for t in range(SEQ):
                            mm = pe.matmul(yp[:, q, :], c.ident[:, :], pv[:, q, t * D:(t + 1) * D],
                                           start=(t == 0), stop=(t == SEQ - 1))
                        if q % 2 == 1:
                            mm.then_inc(y_ready, 1)

                norm.transposes(pe, 0, first=True)
                pe.wait_ge(loaded, 32)
                project(0, first=True)
                norm.transposes(pe, 1)
                project(1)
                sums(0, first=True)
                with pe.Fori(2, G) as g:
                    norm.transposes(pe, g)
                    project(g)
                    sums(g - 1)
                sums(G - 1)

            @block.gpsimd
            def _(pool):
                norm.pool_prologue(pool)
                norm.power(pool, 0)
                with pool.Fori(1, G) as g:
                    norm.power(pool, g)

            @block.scalar
            def _(act):
                norm.copy_out(act, 0)
                with act.Fori(1, G) as g:
                    norm.copy_out(act, g, qkv_filled, g * SEQ)

            @block.vector
            def _(dve):
                def take(g, first=False):
                    if not first:
                        dve.wait_ge(pv_ready, g * SEQ)
                    for j in range(SEQ):
                        dve.wait_ge(qkv_filled, g * SEQ + j + 1)
                        dve.tensor_tensor(qkv[:, j, :, :].rearrange("p a n -> p (a n)"), qp[:, j % 2, 0:3 * D],
                                          bias[:, :], ALU.add).then_inc(qkv_ready, 1)
                    dve.wait_ge(qkv_ready, g * SEQ + SEQ)
                    for i, t in enumerate((2, 1, 0)):
                        dve.tensor_tensor(qkv[:, t, 2, :], qkv[:, t, 2, :], qkv[:, t + 1, 2, :], ALU.add).then_inc(suffix_ready, 1)
                        dve.wait_ge(suffix_ready, g * 3 + i + 1)

                def scores(g, first=False):
                    for q in range(SEQ + 1):
                        if q < SEQ:
                            if not (first and q < 2):
                                dve.wait_ge(score_ready, g * SEQ + q - 1)
                            dve.tensor_tensor(qk[:, q % 2, :].rearrange("p (t n) -> p t n", t=SEQ),
                                              qkv[:, q, 0, :].unsqueeze(1).to_broadcast((P, SEQ, D)),
                                              qkv[:, :, 1, :], ALU.mult).then_inc(qk_ready, 1)
                        if q > 0:
                            dve.wait_ge(qk_ready, g * SEQ + q)
                            dve.tensor_reduce(score[:, q - 1, :], qk[:, (q - 1) % 2, :].rearrange("p (m d) -> p m d", d=HDIM),
                                              AX.X, ALU.add).then_inc(score_ready, 1)

                def products(g, first=False):
                    dve.wait_ge(score_ready, g * SEQ + SEQ)
                    if not first:
                        dve.wait_ge(y_ready, g * 2)
                    for q in range(SEQ):
                        for t in range(SEQ):
                            last = dve.tensor_tensor(pv[:, q, t * D:(t + 1) * D].rearrange("p (h d) -> p h d", d=HDIM),
                                                     qkv[:, t, 2, :].rearrange("p (h d) -> p h d", d=HDIM),
                                                     score[:, q, t * NH:(t + 1) * NH].unsqueeze(2).to_broadcast((P, NH, HDIM)),
                                                     ALU.mult)
                        last.then_inc(pv_ready, 1)

                def add(g):
                    for i in range(2):
                        dve.wait_ge(y_ready, g * 2 + i + 1)
                        at = x4[:, 2 * i:2 * i + 2, bass.ds(g * D, D)]
                        dve.scalar_tensor_tensor(at, yp[:, 2 * i:2 * i + 2, :], LIN_SCALE, at, ALU.mult,
                                                 ALU.add).then_inc(y_used, 1)

                norm.moments(dve, 0)
                norm.normalise(dve, 0, first=True)
                norm.moments(dve, 1)
                norm.normalise(dve, 1)
                dve.wait_ge(loaded, 32)
                take(0, first=True)
                scores(0, first=True)
                products(0, first=True)
                with dve.Fori(1, G - 1) as g:
                    norm.moments(dve, g + 1)
                    norm.normalise(dve, g + 1)
                    take(g)
                    scores(g)
                    products(g)
                    add(g - 1)
                take(G - 1)
                scores(G - 1)
                products(G - 1)
                add(G - 2)
                add(G - 1)


E = 8
EG = 4
SB_ = 2
MB = E + SB_
ROUTED_SCALE = 2.5


def prepare_moe(c):
    wg = c.keep("moe_wg", [P, KD, MB, P])
    wu = c.keep("moe_wu", [P, KD, MB, P])
    wd = c.keep("moe_wd", [P, MB, D])
    wr = c.keep("moe_router", [P, KD, E])
    bias = c.keep("moe_bias", [P, E])
    below = c.keep("moe_below", [P, E * E])
    c.prepared["moe"] = (wg, wu, wd, wr, bias, below)
    with Local(c, "moeprep") as s:
        loaded = s.sem("loaded")
        with c.nc.Block() as block:
            @block.sync
            def _(sp):
                n = 0
                for k in range(KD):
                    f = slice(k * P, (k + 1) * P)
                    for w, routed, shared in ((wg, "w_gate", "sw_gate"), (wu, "w_up", "sw_up")):
                        sp.dma_start(w[:, k, 0:E, :], c.ins[routed][:, f, :].rearrange("e p i -> p e i")).then_inc(loaded, 16)
                        sp.dma_start(w[:, k, E:, :], c.ins[shared][f, :].rearrange("p (b i) -> p b i", i=P)).then_inc(loaded, 16)
                        n += 2
                sp.dma_start(wd[:, 0:E, :], c.ins["w_down"].rearrange("e i d -> i e d")).then_inc(loaded, 16)
                sp.dma_start(wd[:, E:, :], c.ins["sw_down"].rearrange("(b i) d -> i b d", i=P)).then_inc(loaded, 16)
                sp.dma_start(wr[:, :, :], c.ins["gate_w"].rearrange("(k p) e -> p k e", p=P)).then_inc(loaded, 16)
                sp.dma_start(bias[:, :], c.ins["gate_bias"].to_broadcast((P, E))).then_inc(loaded, 16)
                sp.dma_start(below[:, :], c.ins["below"]).then_inc(loaded, 16)
                sp.wait_ge(loaded, 16 * (n + 5))


def stage_moe(c, name):
    nc = c.nc
    wg, wu, wd, wr, bias, below = c.prepared["moe"]
    with Local(c, name) as s:
        norm = Norm(c, s)
        xT, trp = norm.xT, norm.trp
        score = s.sb("score", [P, GT, E])
        sfc = s.sb("sfc", [P, GT, E])
        pair = s.sb("pair", [P, GT, EG])
        gt = s.sb("greater", [P, GT, E * E])
        eq = s.sb("equal", [P, GT, E * E])
        rank = s.sb("rank", [P, GT, E])
        tmp = s.sb("masked", [P, GT, E])
        wsum = s.sb("wsum", [P, GT])
        w = s.sb("w", [P, GT, E])
        sg = s.sb("silu", [P, 2, GN])
        prod = s.sb("prod", [P, 2, GN])
        h = s.sb("h", [P, MB, GN])
        hp = s.ps("hp", [P, 4, GN])
        yp = s.ps("yp", [P, GT, D])
        xT_ready = norm.xT_ready
        logits_ready, score_ready, gate_step = s.sem("logits_ready"), s.sem("score_ready"), s.sem("gate_step")
        w_ready, wb_ready = s.sem("w_ready"), s.sem("wb_ready")
        up_filled, silu_ready, prod_ready = s.sem("up_filled"), s.sem("silu_ready"), s.sem("prod_ready")
        h_ready, y_ready, y_used = s.sem("h_ready"), s.sem("y_ready"), s.sem("y_used")
        STEPS = 18
        with nc.Block() as block:
            @block.gpsimd
            def _(pool):
                norm.pool_prologue(pool)
                norm.power(pool, 0)
                with pool.Fori(1, G) as g:
                    norm.power(pool, g)

            @block.tensor
            def _(pe):
                def transposes(g, first=False):
                    if not first:
                        pe.wait_ge(h_ready, g * MB - SB_)
                    norm.transposes(pe, g, first)

                def logits(g, first=False):
                    pe.wait_ge(xT_ready, g * KD + KD)
                    if not first:
                        pe.wait_ge(prod_ready, g * MB)
                    for j in range(GT):
                        for k in range(KD):
                            mm = pe.matmul(hp[:, 0, j * E:(j + 1) * E], xT[:, k, j * P:(j + 1) * P], wr[:, k, :],
                                           start=(k == 0), stop=(k == KD - 1))
                    mm.then_inc(logits_ready, 1)

                def broadcast(g, e):
                    if e == 0:
                        pe.wait_ge(w_ready, g + 1)
                    if e >= 2:
                        pe.wait_ge(h_ready, g * MB + e - 1)
                    for j in range(GT):
                        mm = pe.transpose(trp[:, e % 2, j * P:(j + 1) * P], w[:, j, e:e + 1].to_broadcast((P, P)),
                                          c.ident[:, :])
                    mm.then_inc(wb_ready, 1)

                def ups(g):
                    for b in range(MB):
                        if b == 0:
                            pe.wait_ge(score_ready, g + 1)
                        if b >= 2:
                            pe.wait_ge(prod_ready, g * MB + b - 1)
                        for i, wt in enumerate((wg, wu)):
                            for k in range(KD):
                                mm = pe.matmul(hp[:, 2 * (b % 2) + i, :], wt[:, k, b, :], xT[:, k, :],
                                               start=(k == 0), stop=(k == KD - 1))
                        mm.then_inc(up_filled, 1)
                        if 1 <= b <= E:
                            broadcast(g, b - 1)

                def down(g, first=False):
                    pe.wait_ge(h_ready, g * MB + MB)
                    for j in range(GT):
                        if j % 2 == 0 and not first:
                            pe.wait_ge(y_used, g * 2 - 1 + j // 2)
                        for b in range(MB):
                            mm = pe.matmul(yp[:, j, :], h[:, b, j * P:(j + 1) * P], wd[:, b, :],
                                           start=(b == 0), stop=(b == MB - 1))
                        if j % 2 == 1:
                            mm.then_inc(y_ready, 1)

                transposes(0, first=True)
                logits(0, first=True)
                ups(0)
                transposes(1)
                down(0, first=True)
                logits(1)
                ups(1)
                with pe.Fori(2, G) as g:
                    transposes(g)
                    down(g - 1)
                    logits(g)
                    ups(g)
                down(G - 1)

            @block.scalar
            def _(act):
                def group(g, first=False):
                    if first:
                        norm.copy_out(act, g)
                    else:
                        norm.copy_out(act, g, up_filled, g * MB)
                    act.wait_ge(logits_ready, g + 1)
                    if not first:
                        act.wait_ge(gate_step, g * STEPS)
                    act.activation(score[:, :, :].rearrange("p j e -> p (j e)"), hp[:, 0, 0:GT * E],
                                   ACT.Sigmoid).then_inc(score_ready, 1)
                    for b in range(MB):
                        act.wait_ge(up_filled, g * MB + b + 1)
                        if not (first and b < 2):
                            act.wait_ge(prod_ready, g * MB + b - 1)
                        act.activation(sg[:, b % 2, :], hp[:, 2 * (b % 2), :], ACT.Silu).then_inc(silu_ready, 1)

                group(0, first=True)
                with act.Fori(1, G) as g:
                    group(g)

            @block.vector
            def _(dve):
                def ranks(g, n, values, at):
                    a_, b_ = (gt[:, :, 0:n * n].rearrange("p j (a b) -> p j a b", b=n),
                              eq[:, :, 0:n * n].rearrange("p j (a b) -> p j a b", b=n))
                    tri = below[:, :].rearrange("p (a b) -> p a b", b=E)[:, 0:n, 0:n].unsqueeze(1).to_broadcast((P, GT, n, n))
                    other = values.unsqueeze(2).to_broadcast((P, GT, n, n))
                    mine = values.unsqueeze(3).to_broadcast((P, GT, n, n))
                    dve.tensor_tensor(a_, other, mine, ALU.is_gt).then_inc(gate_step, 1)
                    dve.tensor_tensor(b_, other, mine, ALU.is_equal).then_inc(gate_step, 1)
                    dve.wait_ge(gate_step, g * STEPS + at + 2)
                    for j in range(GT):
                        last = dve.tensor_tensor(b_[:, j], b_[:, j], tri[:, j], ALU.mult)
                    last.then_inc(gate_step, 1)
                    dve.wait_ge(gate_step, g * STEPS + at + 3)
                    dve.tensor_tensor(gt[:, :, 0:n * n], gt[:, :, 0:n * n], eq[:, :, 0:n * n], ALU.add).then_inc(gate_step, 1)
                    dve.wait_ge(gate_step, g * STEPS + at + 4)
                    dve.tensor_reduce(rank[:, :, 0:n], a_, AX.X, ALU.add).then_inc(gate_step, 1)
                    dve.wait_ge(gate_step, g * STEPS + at + 5)

                def gate(g):
                    def step(ins, n):
                        ins.then_inc(gate_step, 1)
                        dve.wait_ge(gate_step, g * STEPS + n)

                    dve.wait_ge(score_ready, g + 1)
                    step(dve.tensor_tensor(sfc[:, :, :], score[:, :, :], bias[:, :].unsqueeze(1).to_broadcast((P, GT, E)),
                                           ALU.add), 1)
                    step(dve.tensor_reduce(pair[:, :, :], sfc[:, :, :].rearrange("p j (a b) -> p j a b", b=2), AX.X,
                                           ALU.add), 2)
                    ranks(g, EG, pair[:, :, :], 2)
                    step(dve.tensor_scalar(pair[:, :, :], rank[:, :, 0:EG], 1.5, None, ALU.is_lt), 8)
                    step(dve.tensor_tensor(tmp[:, :, :].rearrange("p j (a b) -> p j a b", b=2),
                                           sfc[:, :, :].rearrange("p j (a b) -> p j a b", b=2),
                                           pair[:, :, :].unsqueeze(3).to_broadcast((P, GT, EG, 2)), ALU.mult), 9)
                    ranks(g, E, tmp[:, :, :], 9)
                    step(dve.scalar_tensor_tensor(tmp[:, :, :], rank[:, :, :], 1.5, sfc[:, :, :], ALU.is_lt, ALU.mult), 15)
                    step(dve.tensor_reduce(wsum[:, :], tmp[:, :, :], AX.X, ALU.add), 16)
                    step(dve.tensor_scalar(wsum[:, :], wsum[:, :], 1e-20, None, ALU.add), 17)
                    step(dve.reciprocal(wsum[:, :], wsum[:, :]), 18)
                    for j in range(GT):
                        last = dve.tensor_scalar(w[:, j, :], tmp[:, j, :], wsum[:, j:j + 1], ROUTED_SCALE, ALU.mult, ALU.mult)
                    last.then_inc(w_ready, 1)

                def blocks(g, first=False, last=False):
                    for b in range(MB):
                        if b == 3 and not last:
                            norm.normalise(dve, g + 1)
                        dve.wait_ge(silu_ready, g * MB + b + 1)
                        if b == 0 and not first:
                            dve.wait_ge(y_ready, g * 2)
                        up = hp[:, 2 * (b % 2) + 1, :]
                        if b >= E:
                            dve.tensor_tensor(h[:, b, :], up, sg[:, b % 2, :], ALU.mult).then_inc(prod_ready, 1)
                            dve.wait_ge(prod_ready, g * MB + b + 1)
                            dve.sem_inc(h_ready, 1)
                            continue
                        if b >= 2 or not first:
                            dve.wait_ge(h_ready, g * MB + max(b - 1, 0))
                        dve.tensor_tensor(prod[:, b % 2, :], up, sg[:, b % 2, :], ALU.mult).then_inc(prod_ready, 1)
                        dve.wait_ge(prod_ready, g * MB + b + 1)
                        dve.wait_ge(wb_ready, g * E + b + 1)
                        dve.tensor_tensor(h[:, b, :], trp[:, b % 2, :], prod[:, b % 2, :], ALU.mult).then_inc(h_ready, 1)

                def add(g):
                    for i in range(2):
                        dve.wait_ge(y_ready, g * 2 + i + 1)
                        at = c.x_pair(g * 2 + i)
                        dve.tensor_tensor(at, yp[:, 2 * i:2 * i + 2, :].rearrange("p a n -> p (a n)"), at,
                                          ALU.add).then_inc(y_used, 1)

                norm.moments(dve, 0)
                norm.normalise(dve, 0, first=True)
                norm.moments(dve, 1)
                gate(0)
                blocks(0, first=True)
                with dve.Fori(1, G - 1) as g:
                    norm.moments(dve, g + 1)
                    add(g - 1)
                    gate(g)
                    blocks(g)
                add(G - 2)
                gate(G - 1)
                blocks(G - 1, last=True)
                add(G - 1)


MH, MD = 16, 16
SET = P // MH
SETS = GN // SET
QUAD = 4
STACK = P // MD


def mix_project(c, z, scr, stored):
    nc = c.nc
    with Local(c, "mixA") as s:
        norm = TwiceNorm(c, s)
        w0 = s.sb("w0", [P, KD, 3 * D])
        w = s.sb("w", [P, KD, 3 * D])
        b0 = s.sb("b0", [P, 3 * D])
        bias = s.sb("bias", [P, 3 * D])
        ln = s.sb("ln", [P, KD, 4])
        qkv = s.sb("qkv", [P, GT, 3 * D])
        low = s.sb("low", [P, GT, 2 * D])
        expo = s.sb("expo", [P, GT, 2 * D])
        qp = s.ps("qp", [P, 2, 1024])
        loaded, w_ready, biasp_ready, bias_ready = s.sem("loaded"), s.sem("w_ready"), s.sem("biasp_ready"), s.sem("bias_ready")
        qkv_filled, qkv_biased, low_ready, exp_ready, qkv_ready = (s.sem("qkv_filled"), s.sem("qkv_biased"), s.sem("low_ready"),
                                                                   s.sem("exp_ready"), s.sem("qkv_ready"))
        with nc.Block() as block:
            @block.sync
            def _(sp):
                sp.dma_start(w0[:, :, :], c.ins["mix_wT"].rearrange("(k p) n -> p k n", p=P)).then_inc(loaded, 16)
                sp.dma_start(b0[:, :], c.ins["mix_b"].to_broadcast((P, 3 * D))).then_inc(loaded, 16)
                sp.dma_start(ln[:, :, :], c.ins["mix_ln"].rearrange("(k p) n -> p k n", p=P)).then_inc(loaded, 16)
                with sp.Fori(0, G) as g:
                    sp.wait_ge(qkv_ready, g * GT + GT)
                    for i in range(3):
                        sp.dma_start(scr[i, bass.ds(g * GN, GN), :].rearrange("(j p) d -> p j d", p=P),
                                     qkv[:, :, i * D:(i + 1) * D]).then_inc(stored, 16)
                sp.wait_ge(stored, 48 * G)

            @block.tensor
            def _(pe):
                def project(g, first=False):
                    pe.wait_ge(norm.xT_ready, g * KD + KD)
                    for j in range(GT):
                        if not (first and j < 2):
                            pe.wait_ge(qkv_biased, g * GT + j - 1)
                        for n, size in ((0, 512), (512, 256)):
                            for k in range(KD):
                                mm = pe.matmul(qp[:, j % 2, n:n + size], norm.xT[:, k, j * P:(j + 1) * P],
                                               w[:, k, n:n + size], start=(k == 0), stop=(k == KD - 1))
                        mm.then_inc(qkv_filled, 1)

                pe.wait_ge(loaded, 48)
                for n, size in ((0, 512), (512, 256)):
                    for k in range(KD):
                        mm = pe.matmul(qp[:, 0, n:n + size], ln[:, k, 1:2].to_broadcast((P, P)), w0[:, k, n:n + size],
                                       start=(k == 0), stop=(k == KD - 1))
                mm.then_inc(biasp_ready, 1)
                norm.transposes(pe, 0, first=True)
                pe.wait_ge(bias_ready, 1)
                pe.wait_ge(w_ready, KD)
                project(0, first=True)
                with pe.Fori(1, G) as g:
                    norm.transposes(pe, g)
                    project(g)

            @block.gpsimd
            def _(pool):
                norm.pool_prologue(pool)
                norm.power(pool, 0)
                with pool.Fori(1, G) as g:
                    norm.power(pool, g)

            @block.scalar
            def _(act):
                def exps(g, first=False):
                    for j in range(GT):
                        act.wait_ge(low_ready, g * GT + j + 1)
                        if not first:
                            act.wait_ge(qkv_ready, g * GT - GT + j + 1)
                        act.activation(expo[:, j, :], low[:, j, :], ACT.Exp).then_inc(exp_ready, 1)

                norm.copy_out(act, 0)
                exps(0, first=True)
                with act.Fori(1, G) as g:
                    norm.copy_out(act, g, qkv_filled, g * GT)
                    exps(g)

            @block.vector
            def _(dve):
                def take(g, first=False):
                    if not first:
                        dve.wait_ge(stored, g * 48)
                        dve.wait_ge(exp_ready, g * GT)
                    for j in range(GT):
                        dve.wait_ge(qkv_filled, g * GT + j + 1)
                        dve.tensor_tensor(qkv[:, j, :], qp[:, j % 2, 0:3 * D], bias[:, :], ALU.add).then_inc(qkv_biased, 1)
                    for j in range(GT):
                        dve.wait_ge(qkv_biased, g * GT + j + 1)
                        dve.tensor_scalar(low[:, j, :], qkv[:, j, 0:2 * D], 0.0, None, ALU.min).then_inc(low_ready, 1)

                def elu(g):
                    for j in range(GT):
                        dve.wait_ge(exp_ready, g * GT + j + 1)
                        dve.scalar_tensor_tensor(qkv[:, j, 0:2 * D], qkv[:, j, 0:2 * D], 0.0, expo[:, j, :], ALU.max,
                                                 ALU.add).then_inc(qkv_ready, 1)

                def z_tiles(g):
                    return lambda j: z[:, bass.ds((g * GT + j) * D, D)]

                norm.moments(dve, 0)
                dve.wait_ge(loaded, 48)
                for k in range(KD):
                    dve.tensor_scalar(w[:, k, :], w0[:, k, :], ln[:, k, 0:1], None, ALU.mult).then_inc(w_ready, 1)
                norm.normalise(dve, 0, z_tiles(0), first=True)
                dve.wait_ge(biasp_ready, 1)
                dve.tensor_tensor(bias[:, :], qp[:, 0, 0:3 * D], b0[:, :], ALU.add).then_inc(bias_ready, 1)
                dve.wait_ge(bias_ready, 1)
                norm.moments(dve, 1)
                take(0, first=True)
                norm.normalise(dve, 1, z_tiles(1))
                elu(0)
                with dve.Fori(1, G - 1) as g:
                    norm.moments(dve, g + 1)
                    take(g)
                    norm.normalise(dve, g + 1, z_tiles(g + 1))
                    elu(g)
                take(G - 1)
                elu(G - 1)


def mix_heads(c, scr, scr_o, stored_o):
    nc = c.nc
    with Local(c, "mixB") as s:
        HALF = SETS // 2
        NHALF = T // SET // HALF
        qz = s.sb("qz", [P, 2, HALF // STACK, STACK, P])
        kh = s.sb("kh", [P, 2, HALF, MD])
        vh = s.sb("vh", [P, 2, HALF, MD])
        ve = s.sb("v_one", [P, 2, HALF, MD + 1])
        mask = s.sb("mask", [P, P])
        kT = s.sb("kT", [P, 2, HALF // STACK, P])
        qT = s.sb("qT", [P, 2, QUAD, P])
        sm = s.sb("sm", [P, 2, QUAD, P])
        rec = s.sb("rec", [P, 2, HALF])
        oh = s.sb("oh", [P, 2, HALF, MD])
        ktp = s.ps("ktp", [P, HALF // STACK, P])
        qtp = s.ps("qtp", [P, 2, QUAD, P])
        sp_ = s.ps("sp", [P, 2, QUAD, P])
        op = s.ps("op", [P, 2, 512])
        OB = 16
        QH = HALF // QUAD
        cleared, mask_loaded = s.sem("cleared"), s.sem("mask_loaded")
        loaded = [s.sem("loaded_even"), s.sem("loaded_odd")]
        v_ready, kt_filled, kt_ready = s.sem("v_ready"), s.sem("kt_filled"), s.sem("kt_ready")
        qt_filled, qt_ready, s_filled, s_ready = s.sem("qt_filled"), s.sem("qt_ready"), s.sem("s_filled"), s.sem("s_ready")
        pv_done, rec_ready, o_ready = s.sem("pv_done"), s.sem("rec_ready"), s.sem("o_ready")
        LOAD = 16 * (HALF // STACK + 2)

        def in_dram(which, n):
            return which[bass.ds(n * HALF * SET, HALF * SET), :].rearrange("(a t) (h d) -> (t h) a d", t=SET, d=MD)

        with nc.Block() as block:
            @block.sync
            def _(sp):
                def load(n, slot, first=False):
                    if not first:
                        sp.wait_ge(qt_filled, (n - 1) * QH)
                        sp.wait_ge(v_ready, n - 1)
                    for a in range(HALF // STACK):
                        src = scr[0, bass.ds(n * HALF * SET + a * STACK * SET, STACK * SET), :]
                        src = src.rearrange("(a t) (h d) -> (t h) a d", t=SET, d=MD)
                        dst = qz[:, slot, a, :, :].rearrange("p i n -> p (i n)")[:, 0:STACK * P]
                        sp.dma_start(diagonal(dst), src).then_inc(loaded[slot], 16)
                    sp.dma_start(kh[:, slot, :, :], in_dram(scr[1], n)).then_inc(loaded[slot], 16)
                    sp.dma_start(vh[:, slot, :, :], in_dram(scr[2], n)).then_inc(loaded[slot], 16)

                def diagonal(block_):
                    step = P + MD
                    whole = block_
                    ap = whole[:, 0:(STACK - 1) * step + MD]
                    return bass.AP(tensor=ap.tensor, offset=ap.offset, ap=[list(ap.ap[0]), [step, STACK], [1, MD]])

                def store(n, slot):
                    sp.wait_ge(o_ready, n * 2 + 2)
                    sp.dma_start(in_dram(scr_o, n), oh[:, slot, :, :]).then_inc(stored_o, 16)

                sp.dma_start(mask[:, :], c.ins["token_mask"]).then_inc(mask_loaded, 16)
                sp.wait_ge(cleared, 2)
                load(0, 0, first=True)
                load(1, 1, first=True)
                with sp.Fori(0, NHALF // 2 - 1) as m:
                    for slot in range(2):
                        store(m * 2 + slot, slot)
                        load(m * 2 + slot + 2, slot)
                store(NHALF - 2, 0)
                store(NHALF - 1, 1)
                sp.wait_ge(stored_o, 16 * NHALF)

            @block.gpsimd
            def _(pool):
                for slot in range(2):
                    pool.memset(qz[:, slot, :, :, :].rearrange("p a i n -> p (a i n)"), 0.0).then_inc(cleared, 1)

            @block.tensor
            def _(pe):
                def queries(n, slot, i, first=False):
                    if not (first and i < 2):
                        pe.wait_ge(qt_ready, n * QH + i - 1)
                    for m in range(QUAD):
                        at = QUAD * i + m
                        mm = pe.transpose(qtp[:, i % 2, m, :], qz[:, slot, at // STACK, at % STACK, :], c.ident[:, :])
                    mm.then_inc(qt_filled, 1)

                def half(n, slot, first=False):
                    pe.wait_ge(loaded[slot], (n - slot) * (LOAD // 2) + LOAD)
                    if not first:
                        pe.wait_ge(kt_ready, n)
                    for a in range(HALF // STACK):
                        mm = pe.transpose(ktp[:, a, :], kh[:, slot, a * STACK:(a + 1) * STACK, :].rearrange("p a d -> p (a d)"),
                                          c.ident[:, :])
                    mm.then_inc(kt_filled, 1)
                    queries(n, slot, 0, first)
                    queries(n, slot, 1, first)
                    for i in range(QH + 1):
                        if i < QH:
                            if i == 0:
                                pe.wait_ge(kt_ready, n + 1)
                            pe.wait_ge(qt_ready, n * QH + i + 1)
                            if not (first and i < 2):
                                pe.wait_ge(s_ready, n * QH + i - 1)
                            pe.matmul(sp_[:, i % 2, :, :].rearrange("p m n -> p (m n)"), kT[:, slot, i * QUAD // STACK, :],
                                      qT[:, i % 2, :, :].rearrange("p m n -> p (m n)"), start=True,
                                      stop=True).then_inc(s_filled, 1)
                            if i + 2 < QH:
                                queries(n, slot, i + 2)
                        if i > 0:
                            q = i - 1
                            pe.wait_ge(s_ready, n * QH + q + 1)
                            if q == 0:
                                pe.wait_ge(v_ready, n + 1)
                            if q % (QH // 2) == 0 and not first:
                                pe.wait_ge(o_ready, n * 2 - 1 + q // (QH // 2))
                            for m in range(QUAD):
                                at = QUAD * q + m
                                mm = pe.matmul(op[:, at // OB, (at % OB) * (MD + 1):(at % OB + 1) * (MD + 1)],
                                               sm[:, q % 2, m, :], ve[:, slot, at, :], start=True, stop=True)
                            mm.then_inc(pv_done, 1)

                half(0, 0, first=True)
                half(1, 1)
                with pe.Fori(1, NHALF // 2) as m:
                    half(m * 2, 0)
                    half(m * 2 + 1, 1)

            @block.scalar
            def _(act):
                def half(n, slot, first=False):
                    act.wait_ge(kt_filled, n + 1)
                    act.copy(kT[:, slot, :, :].rearrange("p a n -> p (a n)"),
                             ktp[:, :, :].rearrange("p a n -> p (a n)")).then_inc(kt_ready, 1)
                    for i in range(QH):
                        act.wait_ge(qt_filled, n * QH + i + 1)
                        if not (first and i < 2):
                            act.wait_ge(s_filled, n * QH + i - 1)
                        act.copy(qT[:, i % 2, :, :].rearrange("p m n -> p (m n)"),
                                 qtp[:, i % 2, :, :].rearrange("p m n -> p (m n)")).then_inc(qt_ready, 1)

                half(0, 0, first=True)
                half(1, 1)
                with act.Fori(1, NHALF // 2) as m:
                    half(m * 2, 0)
                    half(m * 2 + 1, 1)

            @block.vector
            def _(dve):
                def normalise(n, slot, i, early):
                    dve.wait_ge(pv_done, n * QH + (i + 1) * (QH // 2))
                    if i == 0 and not early:
                        dve.wait_ge(stored_o, (n - 1) * 16)
                    o = op[:, i, 0:OB * (MD + 1)].rearrange("p (a d) -> p a d", d=MD + 1)
                    dve.reciprocal(rec[:, slot, i * OB:(i + 1) * OB], o[:, :, MD]).then_inc(rec_ready, 1)
                    dve.wait_ge(rec_ready, n * 2 + i + 1)
                    dve.tensor_tensor(oh[:, slot, i * OB:(i + 1) * OB, :], o[:, :, 0:MD],
                                      rec[:, slot, i * OB:(i + 1) * OB].unsqueeze(2).to_broadcast((P, OB, MD)),
                                      ALU.mult).then_inc(o_ready, 1)

                def half(n, slot, first=False, early=False):
                    dve.wait_ge(loaded[slot], (n - slot) * (LOAD // 2) + LOAD)
                    dve.tensor_copy(ve[:, slot, :, 0:MD], vh[:, slot, :, :]).then_inc(v_ready, 1)
                    for i in range(QH):
                        dve.wait_ge(s_filled, n * QH + i + 1)
                        if i >= 2 and i - 2 == QH // 2 - 1:
                            normalise(n, slot, 0, early)
                        if not (first and i < 2):
                            dve.wait_ge(pv_done, n * QH + i - 1)
                        dve.tensor_tensor(sm[:, i % 2, :, :], sp_[:, i % 2, :, :],
                                          mask[:, :].unsqueeze(1).to_broadcast((P, QUAD, P)), ALU.mult).then_inc(s_ready, 1)
                    normalise(n, slot, 1, early)

                for slot in range(2):
                    last = dve.memset(ve[:, slot, :, MD:MD + 1], 1.0)
                dve.wait_ge(mask_loaded, 16)
                half(0, 0, first=True, early=True)
                half(1, 1, early=True)
                with dve.Fori(1, NHALF // 2) as m:
                    half(m * 2, 0)
                    half(m * 2 + 1, 1)


def mix_finish(c, z, scr_o):
    nc = c.nc
    with Local(c, "mixC") as s:
        norm = Norm(c, s)
        za, xT, trp = s.sb("za", [P, GT, D]), norm.xT, norm.trp
        ot = s.sb("ot", [P, GT, D])
        oT = s.sb("oT", [P, KD, GN])
        wo = s.sb("wo", [P, KD, D])
        ob = s.sb("ob", [P, D])
        ln = s.sb("ln", [P, KD, 4])
        fc = s.sb("fc", [P, KD, HID])
        fcb0 = s.sb("fcb0", [P, HB])
        fcb = s.sb("fcb", [P, HB])
        wp = s.sb("wp", [P, HB, D])
        pb = s.sb("pb", [P, D])
        h = s.sb("h", [P, HB, GN])
        hp = s.ps("hp", [P, 4, GN])
        yp = s.ps("yp", [P, GT, D])
        loaded, o_loaded, biasp_ready, fcb_ready, fc_ready = (s.sem("loaded"), s.sem("o_loaded"), s.sem("biasp_ready"),
                                                              s.sem("fcb_ready"), s.sem("fc_ready"))
        ot_used, oT_ready, a_ready, za_step = s.sem("ot_used"), s.sem("oT_ready"), s.sem("a_ready"), s.sem("za_step")
        xb_ready = s.sem("xb_ready")
        h_filled, h_ready, y_ready, y_used = s.sem("h_filled"), s.sem("h_ready"), s.sem("y_ready"), s.sem("y_used")
        def flat(t):
            return t.rearrange("p a n -> p (a n)")

        with nc.Block() as block:
            @block.sync
            def _(sp):
                for dst, src in ((wo[:, :, :], c.ins["mix_oT"].rearrange("(k p) n -> p k n", p=P)),
                                 (ob[:, :], c.ins["mix_ob"].to_broadcast((P, D))),
                                 (ln[:, :, :], c.ins["mix_ln"].rearrange("(k p) n -> p k n", p=P)),
                                 (fc[:, :, :], c.ins["mix_fcT"].rearrange("(k p) n -> p k n", p=P)),
                                 (fcb0[:, :], c.ins["mix_fcb"]),
                                 (wp[:, :, :], c.ins["mix_pT"].rearrange("(b p) n -> p b n", p=P)),
                                 (pb[:, :], c.ins["mix_pb"].to_broadcast((P, D)))):
                    sp.dma_start(dst, src).then_inc(loaded, 16)

                def load(g, first=False):
                    if not first:
                        sp.wait_ge(ot_used, g)
                    sp.dma_start(ot[:, :, :], scr_o[bass.ds(g * GN, GN), :].rearrange("(j p) d -> p j d", p=P)).then_inc(o_loaded, 16)

                load(0, first=True)
                with sp.Fori(1, G) as g:
                    load(g)

            @block.gpsimd
            def _(pool):
                norm.pool_prologue(pool)
                norm.power(pool, 0)
                with pool.Fori(1, G) as g:
                    norm.power(pool, g)

            @block.tensor
            def _(pe):
                def project(g, first=False):
                    pe.wait_ge(o_loaded, g * 16 + 16)
                    if not first:
                        pe.wait_ge(norm.xT_ready, g * KD)
                    for k in range(KD):
                        for j in range(GT):
                            mm = pe.transpose(trp[:, k, j * P:(j + 1) * P], ot[:, j, k * P:(k + 1) * P], c.ident[:, :])
                    mm.then_inc(ot_used, 1)
                    pe.wait_ge(oT_ready, g * KD + KD)
                    for j in range(GT):
                        if j % 2 == 0 and not first:
                            pe.wait_ge(y_used, g * 2 - 1 + j // 2)
                        for k in range(KD):
                            mm = pe.matmul(yp[:, j, :], oT[:, k, j * P:(j + 1) * P], wo[:, k, :],
                                           start=(k == 0), stop=(k == KD - 1))
                    mm.then_inc(a_ready, 1)

                def up(g, first=False):
                    pe.wait_ge(norm.xT_ready, g * KD + KD)
                    for b in range(HB):
                        if not (first and b < 4):
                            pe.wait_ge(h_ready, g * HB + b - 3)
                        for k in range(KD):
                            mm = pe.matmul(hp[:, b % 4, :], fc[:, k, b * P:(b + 1) * P], xT[:, k, :],
                                           start=(k == 0), stop=(k == KD - 1))
                        mm.then_inc(h_filled, 1)

                def down(g):
                    pe.wait_ge(h_ready, g * HB + HB)
                    for j in range(GT):
                        for b in range(HB):
                            mm = pe.matmul(yp[:, j, :], h[:, b, j * P:(j + 1) * P], wp[:, b, :],
                                           start=(b == 0), stop=(b == HB - 1))
                        if j % 2 == 1:
                            mm.then_inc(y_ready, 1)

                def group(g, first=False):
                    project(g, first)
                    pe.wait_ge(oT_ready, g * KD + KD)
                    norm.transposes(pe, g, first)
                    up(g, first)
                    down(g)

                pe.wait_ge(loaded, 112)
                for b in range(HB):
                    for k in range(KD):
                        mm = pe.matmul(hp[:, 0, b:b + 1], fc[:, k, b * P:(b + 1) * P], ln[:, k, 3:4],
                                       start=(k == 0), stop=(k == KD - 1))
                mm.then_inc(biasp_ready, 1)
                pe.wait_ge(fc_ready, KD)
                group(0, first=True)
                with pe.Fori(1, G) as g:
                    group(g)

            @block.scalar
            def _(act):
                def group(g, first=False):
                    act.wait_ge(ot_used, g + 1)
                    if not first:
                        act.wait_ge(a_ready, g)
                    for k in range(KD):
                        act.copy(oT[:, k, :], trp[:, k, :]).then_inc(oT_ready, 1)
                    if first:
                        norm.copy_out(act, g)
                    else:
                        norm.copy_out(act, g, h_filled, g * HB)
                    for b in range(HB):
                        act.wait_ge(h_filled, g * HB + b + 1)
                        if b == 0 and not first:
                            act.wait_ge(y_ready, g * 2)
                        act.activation(h[:, b, :], hp[:, b % 4, :], ACT.Gelu, bias=fcb[:, b:b + 1]).then_inc(h_ready, 1)

                act.wait_ge(fcb_ready, 1)
                group(0, first=True)
                with act.Fori(1, G) as g:
                    group(g)

            @block.vector
            def _(dve):
                ZA = 4

                def attend(g, first=False):
                    dve.wait_ge(a_ready, g + 1)
                    if not first:
                        dve.wait_ge(norm.xn_ready, g * GT)
                    for i in range(2):
                        dve.tensor_tensor(flat(za[:, 2 * i:2 * i + 2, :]), flat(yp[:, 2 * i:2 * i + 2, :]),
                                          z[:, bass.ds(g * GT * D + i * 2 * D, 2 * D)], ALU.add).then_inc(za_step, 1)
                    dve.wait_ge(za_step, g * ZA + 2)
                    dve.tensor_tensor(za[:, :, :], za[:, :, :], ob[:, :].unsqueeze(1).to_broadcast((P, GT, D)),
                                      ALU.add).then_inc(za_step, 1)
                    dve.wait_ge(za_step, g * ZA + 3)
                    for j in range(GT):
                        dve.bn_stats(norm.st[:, j, :], za[:, j, :]).then_inc(norm.stats_ready, 1)
                    dve.wait_ge(norm.stats_ready, g * GT + GT)
                    dve.sem_inc(norm.stats_seen, 1)
                    for j in range(GT):
                        dve.bn_aggr(norm.mv[:, j, :], norm.st[:, j, :]).then_inc(norm.moments_ready, 1)
                    xg = c.x[:, bass.ds(g * GT * D, GT * D)]
                    dve.tensor_tensor(xg, flat(za[:, :, :]), xg, ALU.add).then_inc(za_step, 1)
                    dve.wait_ge(norm.rstd_ready, g + 1)
                    if not first:
                        dve.wait_ge(norm.xn_used, g)
                    for j in range(GT):
                        dve.tensor_scalar(norm.xn[:, j, :], za[:, j, :], norm.mv[:, j, 0:1], norm.rstd[:, j:j + 1],
                                          ALU.subtract, ALU.mult).then_inc(norm.xn_ready, 1)

                def add(g):
                    dve.wait_ge(za_step, g * ZA + 4)
                    xg = c.x[:, bass.ds(g * GT * D, GT * D)]
                    xg3 = xg.rearrange("p (j d) -> p j d", d=D)
                    dve.tensor_tensor(xg3, xg3, pb[:, :].unsqueeze(1).to_broadcast((P, GT, D)), ALU.add).then_inc(xb_ready, 1)
                    dve.wait_ge(xb_ready, g + 1)
                    for i in range(2):
                        dve.wait_ge(y_ready, g * 2 + i + 1)
                        at = c.x_pair(g * 2 + i)
                        dve.tensor_tensor(at, flat(yp[:, 2 * i:2 * i + 2, :]), at, ALU.add).then_inc(y_used, 1)

                dve.wait_ge(biasp_ready, 1)
                for k in range(KD):
                    dve.tensor_scalar(fc[:, k, :], fc[:, k, :], ln[:, k, 2:3], None, ALU.mult).then_inc(fc_ready, 1)
                dve.tensor_tensor(fcb[:, :], hp[:, 0, 0:HB], fcb0[:, :], ALU.add).then_inc(fcb_ready, 1)
                attend(0, first=True)
                add(0)
                with dve.Fori(1, G) as g:
                    attend(g)
                    add(g)


def stage_mix(c):
    nc = c.nc
    scr = nc.dram_tensor("mix_qkv", (3, T, D), F32, kind="Internal").ap()
    scr_o = nc.dram_tensor("mix_out", (T, D), F32, kind="Internal").ap()
    with Local(c, "mix") as s:
        z = s.sb("z", [P, TILES * D])
        stored, stored_o = s.sem("stored"), s.sem("stored_o")
        mix_project(c, z, scr, stored)
        mix_heads(c, scr, scr_o, stored_o)
        mix_finish(c, z, scr_o)


def load_x(c, x_in, ident_in):
    with Local(c, "load") as s:
        loaded = s.sem("loaded")
        with c.nc.Block() as block:
            @block.sync
            def _(sp):
                sp.dma_start(c.ident[:, :], ident_in).then_inc(loaded, 16)
                for q in range(4):
                    sp.dma_start(c.x[:, q * 8 * D:(q + 1) * 8 * D].rearrange("p (n d) -> p n d", d=D),
                                 x_in[q].rearrange("(n p) d -> p n d", p=P)).then_inc(loaded, 16)
                sp.wait_ge(loaded, 80)


def store_x(c, out):
    with Local(c, "store") as s:
        stored = s.sem("stored")
        with c.nc.Block() as block:
            @block.sync
            def _(sp):
                for q in range(4):
                    sp.dma_start(out[q].rearrange("(n p) d -> p n d", p=P),
                                 c.x[:, q * 8 * D:(q + 1) * 8 * D].rearrange("p (n d) -> p n d", d=D)).then_inc(stored, 16)
                sp.wait_ge(stored, 64)


def build(nc, ins, out):
    with ExitStack() as stack:
        c = Ctx(nc, ins, stack)
        load_x(c, ins["x"], ins["ident"])
        stage_mamba(c)
        prepare_ffn(c)
        stage_ffn(c, "ffn1")
        stage_attn(c)
        stage_ffn(c, "ffn2")
        stage_lin(c)
        prepare_moe(c)
        stage_moe(c, "moe1")
        stage_mix(c)
        stage_moe(c, "moe2")
        store_x(c, out)


def host_constants():
    out = {"ident": np.eye(P, dtype=np.float32)}
    theta = (np.arange(L, dtype=np.float32)[:, None]
             / np.float32(10000.0) ** (np.arange(0, 16, 2, dtype=np.float32) / 16)[None, :]).astype(np.float32)
    cos, sin = np.cos(theta.astype(np.float64)), np.sin(theta.astype(np.float64))
    rope = np.stack([np.repeat(cos, 2, axis=1), np.stack([-sin, sin], axis=-1).reshape(L, 16)], axis=1)
    out["rope"] = rope.astype(np.float32).reshape(L // P, P, 32).transpose(1, 0, 2)
    later = np.triu(np.full((P, P), -1e9, np.float32), k=1)
    out["causal"] = np.stack([later, later.T, np.eye(P, dtype=np.float32)], axis=1)
    out["below"] = np.tile((np.arange(8)[None, :] < np.arange(8)[:, None]).astype(np.float32).reshape(1, 64), (P, 1))
    out["token_mask"] = np.kron(np.eye(8, dtype=np.float32), np.ones((16, 16), np.float32))
    return out


def host_layouts(a):
    def t(w):
        return np.ascontiguousarray(np.swapaxes(np.asarray(w), -1, -2))
    out = {"x": np.asarray(a["L0_attn_a_x"])}
    out["w_fc"] = np.asarray(a["L0_ffn_w_fc"])
    out["w_proj"] = np.asarray(a["L0_ffn_w_proj"])
    out["uT"] = t(a["L0_ffn_u"])
    out["v"] = np.asarray(a["L0_ffn_v"])
    out["fast_b"] = np.asarray(a["L0_ffn_fast_b"])
    out["gate"] = np.asarray(a["L0_ffn_gate"]).reshape(1, 1)
    m = {n: np.asarray(a["L0_attn_a_" + n]) for n in
         ("norm_w", "in_proj_w", "conv_w", "conv_b", "x_proj_w", "dt_proj_w", "dt_proj_b", "A_log", "D_param", "out_proj_w")}
    out["mb_inT"] = t(m["in_proj_w"])
    out["mb_norm"] = m["norm_w"].reshape(KD, P).T
    chan = np.concatenate([m["conv_w"].reshape(-1, 4), m["conv_b"][:, None], m["dt_proj_b"][:, None], m["D_param"][:, None]], axis=1)
    out["mb_chan"] = chan.reshape(4, P, 7).transpose(1, 0, 2)
    out["mb_alog"] = m["A_log"].reshape(4, P, 16).transpose(1, 0, 2)
    out["mb_xpT"] = t(m["x_proj_w"])
    out["mb_dtT"] = t(m["dt_proj_w"])
    out["mb_outT"] = t(m["out_proj_w"])
    for n in ("wq", "wk", "wv", "wo", "Bq", "Bv"):
        out["attn_" + n] = np.asarray(a["L0_attn_b_" + n])
    out["attn_AqT"], out["attn_AvT"] = t(a["L0_attn_b_Aq"]), t(a["L0_attn_b_Av"])
    out["lin_wT"] = t(np.asarray(a["L1_attn_a_W_qkv"]).reshape(16, 3, 16, D).transpose(1, 0, 2, 3).reshape(3 * D, D))
    out["lin_b"] = np.asarray(a["L1_attn_a_b_qkv"]).reshape(16, 3, 16).transpose(1, 0, 2).reshape(1, 3 * D)
    out["gate_w"] = np.asarray(a["L1_ffn_gate_w"])
    out["gate_bias"] = np.asarray(a["L1_ffn_gate_bias"]).reshape(1, -1)
    for n in ("w_gate", "w_up", "w_down", "sw_gate", "sw_up", "sw_down"):
        out[n] = np.asarray(a["L1_ffn_" + n])
    m = {n: np.asarray(a["L1_attn_b_" + n]) for n in
         ("ln1_w", "ln1_b", "q_w", "q_b", "k_w", "k_b", "v_w", "v_b", "o_w", "o_b", "ln2_w", "ln2_b", "fc_w", "fc_b", "proj_w", "proj_b")}
    out["mix_wT"] = t(np.concatenate([m["q_w"], m["k_w"], m["v_w"]], axis=0))
    out["mix_b"] = np.concatenate([m["q_b"], m["k_b"], m["v_b"]]).reshape(1, 3 * D)
    out["mix_ln"] = np.stack([m["ln1_w"], m["ln1_b"], m["ln2_w"], m["ln2_b"]], axis=1)
    out["mix_oT"] = t(m["o_w"])
    out["mix_ob"] = m["o_b"].reshape(1, D)
    out["mix_fcT"] = t(m["fc_w"])
    out["mix_fcb"] = t(m["fc_b"].reshape(HB, P))
    out["mix_pT"] = t(m["proj_w"])
    out["mix_pb"] = m["proj_b"].reshape(1, D)
    return out


def kernel(**inputs):
    import concourse.bacc as _bacc
    from concourse.bass_utils import run_bass_kernel_spmd as _run

    nc = _bacc.Bacc("TRN2", target_bir_lowering=False, num_devices=1)
    arrays, ins = {}, {}
    for name, a in {**host_layouts(inputs), **host_constants()}.items():
        a = np.ascontiguousarray(a)
        arrays[f"in_{name}_dram"] = a
        ins[name] = nc.dram_tensor(f"in_{name}_dram", a.shape, mybir.dt.from_np(a.dtype), kind="ExternalInput").ap()
    out = nc.dram_tensor("out_dram", (B, L, D), F32, kind="ExternalOutput").ap()
    build(nc, ins, out)
    r = _run(nc, [arrays], core_ids=[0])
    return r.results[0]["out_dram"]
```

```python
from contextlib import ExitStack

import numpy as np

import concourse.bass as bass
from concourse import mybir
from concourse.alu_op_type import AluOpType as ALU

F32 = mybir.dt.float32
BF16 = mybir.dt.bfloat16
ACT = mybir.ActivationFunctionType
AX = mybir.AxisListType

P = 128
B, L, D = 4, 1024, 256
T = B * L
TILES = T // P
GT = 4
G = TILES // GT
GN = GT * P
KD = D // P
EPS = 1e-5
HID = 1024
HB = HID // P


class Ctx:

    def __init__(self, nc, ins, stack):
        self.nc, self.ins, self.stack, self.stage = nc, ins, stack, ""
        self.x = self.keep("x", [P, TILES * D])
        self.ident = self.keep("ident", [P, P])
        self.prepared = {}
        self.x_loaded = [nc.alloc_semaphore(f"x_loaded{i}") for i in range(3)]

    def keep(self, name, shape, dt=F32):
        return self.stack.enter_context(self.nc.sbuf_tensor(name, shape, dt))

    def x_tile(self, t):
        return self.x[:, bass.ds(t * D, D)]

    def x_pair(self, t):
        return self.x[:, bass.ds(t * 2 * D, 2 * D)]


class Local:

    def __init__(self, c, stage):
        self.c, self.nc, self.stage = c, c.nc, stage

    def __enter__(self):
        self.stack = ExitStack().__enter__()
        self.sems = []
        return self

    def __exit__(self, *why):
        if why[0] is None:
            self.nc.clear_and_free_semaphores(self.sems)
            self.nc.all_engine_barrier()
        return self.stack.__exit__(*why)

    def sb(self, name, shape, dt=F32):
        return self.stack.enter_context(self.nc.sbuf_tensor(f"{self.stage}_{name}", shape, dt))

    def ps(self, name, shape, dt=F32):
        return self.stack.enter_context(self.nc.psum_tensor(f"{self.stage}_{name}", shape, dt))

    def sem(self, name):
        self.sems.append(self.nc.alloc_semaphore(f"{self.stage}_{name}"))
        return self.sems[-1]


class Norm:

    def __init__(self, c, s, tile=lambda g, j: g * GT + j, trp=None):
        self.c, self.nc, self.tile = c, c.nc, tile
        self.st = s.sb("bn_stats", [P, GT, 6])
        self.mv = s.sb("moments", [P, GT, 2])
        self.ve = s.sb("var_eps", [P, GT])
        self.rstd = s.sb("rstd", [P, GT])
        self.half = s.sb("minus_half", [P, GT])
        self.eps = s.sb("eps", [P, GT])
        self.xn = s.sb("xn", [P, GT, D])
        self.xT = s.sb("xT", [P, KD, GN])
        self.trp = s.ps("trp", [P, KD, GN]) if trp is None else trp
        self.stats_ready = s.sem("stats_ready")
        self.stats_seen = s.sem("stats_seen")
        self.moments_ready = s.sem("moments_ready")
        self.half_ready = s.sem("half_ready")
        self.eps_added = s.sem("eps_added")
        self.rstd_ready = s.sem("rstd_ready")
        self.xn_ready = s.sem("xn_ready")
        self.xn_used = s.sem("xn_used")
        self.xT_ready = s.sem("xT_ready")

    def moments(self, dve, g):
        for j in range(GT):
            dve.bn_stats(self.st[:, j, :], self.c.x_tile(self.tile(g, j))).then_inc(self.stats_ready, 1)
        dve.wait_ge(self.stats_ready, g * GT + GT)
        dve.sem_inc(self.stats_seen, 1)
        for j in range(GT):
            dve.bn_aggr(self.mv[:, j, :], self.st[:, j, :]).then_inc(self.moments_ready, 1)

    def pool_prologue(self, pool):
        pool.memset(self.half[:, :], -0.5).then_inc(self.half_ready, 1)
        pool.memset(self.eps[:, :], EPS).then_inc(self.half_ready, 1)
        pool.wait_ge(self.half_ready, 2)

    def power(self, pool, g):
        pool.wait_ge(self.moments_ready, g * GT + GT)
        pool.tensor_tensor(self.ve[:, :], self.mv[:, :, 1], self.eps[:, :], ALU.add).then_inc(self.eps_added, 1)
        pool.wait_ge(self.eps_added, g + 1)
        pool.tensor_tensor(self.rstd[:, :], self.ve[:, :], self.half[:, :], ALU.pow).then_inc(self.rstd_ready, 1)

    def normalise(self, dve, g, first=False):
        dve.wait_ge(self.rstd_ready, g + 1)
        if not first:
            dve.wait_ge(self.xn_used, g)
        for j in range(GT):
            dve.tensor_scalar(self.xn[:, j, :], self.c.x_tile(self.tile(g, j)), self.mv[:, j, 0:1],
                              self.rstd[:, j:j + 1], ALU.subtract, ALU.mult).then_inc(self.xn_ready, 1)

    def transposes(self, pe, g, first=False):
        pe.wait_ge(self.xn_ready, g * GT + GT)
        if not first:
            pe.wait_ge(self.xT_ready, g * KD)
        for k in range(KD):
            for j in range(GT):
                mm = pe.transpose(self.trp[:, k, j * P:(j + 1) * P], self.xn[:, j, k * P:(k + 1) * P],
                                  self.c.ident[:, :])
        mm.then_inc(self.xn_used, 1)

    def copy_out(self, act, g, gemms_done=None, count=None):
        act.wait_ge(self.xn_used, g + 1)
        if gemms_done is not None:
            act.wait_ge(gemms_done, count)
        for k in range(KD):
            act.copy(self.xT[:, k, :], self.trp[:, k, :]).then_inc(self.xT_ready, 1)


class TwiceNorm(Norm):

    def __init__(self, c, s, tile=lambda g, j: g * GT + j, trp=None):
        super().__init__(c, s, tile, trp)
        self.v2 = s.sb("var_z", [P, GT])
        self.v2e = s.sb("var_z_eps", [P, GT])
        self.r2 = s.sb("rstd_z", [P, GT])
        self.v1 = s.sb("std_share", [P, GT])
        self.pool_step = s.sem("pool_step")
        self.r2_ready = s.sem("r2_ready")
        self.z_ready = s.sem("z_ready")

    def power(self, pool, g):
        super().power(pool, g)
        pool.wait_ge(self.rstd_ready, g + 1)
        pool.tensor_tensor(self.v1[:, :], self.mv[:, :, 1], self.rstd[:, :], ALU.mult).then_inc(self.pool_step, 1)
        pool.wait_ge(self.pool_step, g * 3 + 1)
        pool.tensor_tensor(self.v2[:, :], self.v1[:, :], self.rstd[:, :], ALU.mult).then_inc(self.pool_step, 1)
        pool.wait_ge(self.pool_step, g * 3 + 2)
        pool.tensor_tensor(self.v2e[:, :], self.v2[:, :], self.eps[:, :], ALU.add).then_inc(self.pool_step, 1)
        pool.wait_ge(self.pool_step, g * 3 + 3)
        pool.tensor_tensor(self.r2[:, :], self.v2e[:, :], self.half[:, :], ALU.pow).then_inc(self.r2_ready, 1)

    def normalise(self, dve, g, z_of, first=False):
        dve.wait_ge(self.rstd_ready, g + 1)
        for j in range(GT):
            dve.tensor_scalar(z_of(j), self.c.x_tile(self.tile(g, j)), self.mv[:, j, 0:1],
                              self.rstd[:, j:j + 1], ALU.subtract, ALU.mult).then_inc(self.z_ready, 1)
        dve.wait_ge(self.r2_ready, g + 1)
        if not first:
            dve.wait_ge(self.xn_used, g)
        for j in range(GT):
            dve.wait_ge(self.z_ready, g * GT + j + 1)
            dve.tensor_scalar(self.xn[:, j, :], z_of(j), self.r2[:, j:j + 1], None, ALU.mult).then_inc(self.xn_ready, 1)


CB = 4
NS = 16
DTR = 16
XD = DTR + 2 * NS
TAPS = 4
PAD = TAPS - 1
N = NS * CB
AHEAD = 8
OUT_AT, BLOCK_AT, COPY_AT, CONV_AT, ADD_AT = (6, 9, 16, 19), (11, 13, 21, 24, 26, 28, 31, 33), (15, 17, 25, 28), (17, 21, 26, 30), (14, 22)
FB = (6, 7, 4, 5)


def stage_mamba(c):
    nc = c.nc
    bc = nc.dram_tensor("mamba_bc", (2 * NS, T), F32, kind="Internal").ap()
    with Local(c, "mamba") as s:
        banks = s.ps("banks", [P, 8, 512])
        norm = TwiceNorm(c, s, trp=banks[:, 6:8, :])
        zt = s.sb("z", [P, GT, D])
        win = s.sb("win", [P, KD, 2 * CB * P])
        nw = s.sb("nw", [P, KD])
        chan = s.sb("chan", [P, CB, 7])
        a_log = s.sb("a_log", [P, CB, NS])
        a_neg = s.sb("a_neg", [P, CB, NS])
        wxp = s.sb("wxp", [P, CB, XD])
        wdt = s.sb("wdt", [P, CB * P])
        wout = s.sb("wout", [P, CB, D])
        xi = s.sb("xi", [P, CB, PAD + GN])
        xd = s.sb("xd", [P, GN])
        ex = s.sb("ex", [P, CB, GN])
        u = s.sb("u", [P, 2, CB, GN])
        sz = s.sb("sz", [P, 2, CB, GN])
        delta = s.sb("delta", [P, 2, CB, GN])
        du = s.sb("du", [P, 2, CB, GN])
        bcs = s.sb("bcs", [P, 4, 2, GN])
        dA = s.sb("dA", [P, AHEAD, GN])
        dBu = s.sb("dBu", [P, CB, GN])
        h = s.sb("h", [P, AHEAD, GN])
        h_end = s.sb("h_end", [P, NS, CB])
        hc = s.sb("hc", [P, CB, GN])
        names = ("loaded consts w_ready a_ready z_added carry_ready hp_filled hp_used conv_step xc_ready u_ready xp_filled xd_ready "
                 "bc_stored dt_filled abs_ready exp_ready ln_ready relu_ready delta_ready du_ready bc_loaded0 bc_loaded1 "
                 "bc_loaded2 bc_loaded3 dA_ready dBu_ready h_ready h_end_ready hc_ready hc_used skip_ready yg_ready out_filled "
                 "out_used")
        S = {n: s.sem(n) for n in names.split()}
        START = {"z_added": 2, "relu_ready": 1, "bc_stored": 16, "h_ready": AHEAD, "hc_ready": AHEAD, "hc_used": CB,
                 "skip_ready": CB, "yg_ready": CB, "out_used": 4, "out_filled": 2, "delta_ready": CB}

        def sem(n):
            return S[n]

        def group_loop(engine, group):
            group(0, 0, False, True)
            with engine.Fori(0, B - 1) as m:
                group(m * 2 + 1, 1, True, True)
                group(m * 2 + 2, 0, True, True)
            group(G - 1, 1, True, False)

        with nc.Block() as block:
            @block.sync
            def _(sp):
                sp.sem_inc(sem("bc_stored"), START["bc_stored"])
                for dst, src in ((win[:, :, :], c.ins["mb_inT"].rearrange("(k p) n -> p k n", p=P)),
                                 (nw[:, :], c.ins["mb_norm"]), (chan[:, :, :], c.ins["mb_chan"]),
                                 (a_log[:, :, :], c.ins["mb_alog"]),
                                 (wxp[:, :, :], c.ins["mb_xpT"].rearrange("(c p) n -> p c n", p=P)),
                                 (wout[:, :, :], c.ins["mb_outT"].rearrange("(c p) n -> p c n", p=P))):
                    sp.dma_start(dst, src).then_inc(sem("loaded"), 16)
                sp.wait_ge(sem("consts"), 1)
                sp.dma_start(wdt[0:DTR, :], c.ins["mb_dtT"]).then_inc(sem("loaded"), 16)

                def store(g):
                    sp.wait_ge(sem("xd_ready"), g + 1)
                    sp.dma_start(bc[:, bass.ds(g * GN, GN)], xd[DTR:XD, :]).then_inc(sem("bc_stored"), 16)

                def loads(g, after):
                    sp.wait_ge(sem("bc_stored"), g * 16 + 16 + START["bc_stored"])
                    for st in range(NS):
                        if not (isinstance(g, int) and g == 0 and st < 4):
                            sp.wait_ge(sem("hc_ready"), g * N + (st - 4) * CB + CB + START["hc_ready"])
                        src = bc.rearrange("(k s) t -> s k t", k=2)[st:st + 1, :, bass.ds(g * GN, GN)]
                        sp.dma_start(bcs[:, st % 4, :, :], src.to_broadcast((P, 2, GN))).then_inc(sem(f"bc_loaded{st % 4}"), 16)
                        if st == NS - 2 and after:
                            store(g + 1)

                store(0)
                group_loop(sp, lambda g, v, before, after: loads(g, after))

            @block.tensor
            def _(pe):
                def front(g, n):
                    if n == 5:
                        pe.wait_ge(sem("relu_ready"), g * CB + 1)
                        norm.transposes(pe, g, first=True)
                    if n in BLOCK_AT:
                        i = BLOCK_AT.index(n)
                        if i == 0:
                            pe.wait_ge(norm.xT_ready, g * KD + KD)
                        if i in (2, 3):
                            pe.wait_ge(sem("out_used"), g * 2 + i - 1)
                        if i >= 4:
                            pe.wait_ge(sem("hp_used"), g * 8 + i - 3)
                        for k in range(KD):
                            mm = pe.matmul(banks[:, FB[i % 4], :], win[:, k, i * P:(i + 1) * P], norm.xT[:, k, :],
                                           start=(k == 0), stop=(k == KD - 1))
                        mm.then_inc(sem("hp_filled"), 1)

                def front_end(g, v, n):
                    if n == 39:
                        pe.wait_ge(sem("u_ready"), g * CB + CB)
                        for k in range(CB):
                            mm = pe.matmul(banks[0:XD, 6, :], wxp[:, k, :], u[:, v, k, :], start=(k == 0), stop=(k == CB - 1))
                        mm.then_inc(sem("xp_filled"), 1)
                    if 44 <= n < 48:
                        k = n - 44
                        if k == 0:
                            pe.wait_ge(sem("xd_ready"), g + 1)
                        pe.matmul(banks[:, FB[(k + 1) % 4], :], wdt[:, k * P:(k + 1) * P], xd[:, :],
                                  start=True, stop=True).then_inc(sem("dt_filled"), 1)

                def sums(g, n):
                    k = n % CB
                    if n < CB:
                        pe.wait_ge(sem("skip_ready"), g * CB + k + 1)
                    pe.wait_ge(sem("hc_ready"), g * N + n + 1 + START["hc_ready"])
                    pe.matmul(banks[:, k, :], c.ident[:, :], hc[:, k, :], start=(n < CB), stop=True,
                              skip_group_check=True).then_inc(sem("hc_used"), 1)

                def output(g, v, t):
                    if t == 0:
                        pe.wait_ge(sem("yg_ready"), g * CB + CB + START["yg_ready"])
                    for k in range(CB):
                        mm = pe.matmul(banks[:, 4 + t // 2, (t % 2) * D:(t % 2 + 1) * D], delta[:, v, k, t * P:(t + 1) * P],
                                       wout[:, k, :], start=(k == 0), stop=(k == CB - 1))
                    if t % 2 == 1:
                        mm.then_inc(sem("out_filled"), 1)

                def group(g, v, before, after):
                    for n in range(N):
                        sums(g, n)
                        if before and n in OUT_AT:
                            output(g - 1, 1 - v, OUT_AT.index(n))
                        if after:
                            front(g + 1, n)
                            front_end(g + 1, 1 - v, n)

                pe.sem_inc(sem("out_filled"), START["out_filled"])
                pe.wait_ge(c.x_loaded[2], 16)
                pe.wait_ge(sem("w_ready"), KD)
                pe.wait_ge(sem("loaded"), 16 * 7)
                pe.wait_ge(sem("consts"), 2)
                for n in range(N):
                    front(0, n)
                    front_end(0, 0, n)
                group_loop(pe, group)
                for t in range(GT):
                    output(G - 1, 1, t)

            @block.gpsimd
            def _(pool):
                norm.pool_prologue(pool)

                def inputs(g, v, n):
                    st, k = n // CB, n % CB
                    if n < CB:
                        pool.wait_ge(sem("delta_ready"), g * CB + k + 1 + START["delta_ready"])
                        pool.tensor_tensor(du[:, v, k, :], delta[:, v, k, :], u[:, v, k, :], ALU.mult).then_inc(sem("du_ready"), 1)
                        pool.wait_ge(sem("du_ready"), g * CB + k + 1)
                    if k == 0:
                        pool.wait_ge(sem(f"bc_loaded{st % 4}"), g * 64 + st // 4 * 16 + 16)
                    pool.wait_ge(sem("h_ready"), g * N + n + 1 + AHEAD - CB)
                    pool.tensor_tensor(dBu[:, k, :], du[:, v, k, :], bcs[:, st % 4, 0, :], ALU.mult).then_inc(sem("dBu_ready"), 1)

                def group(g, v, before, after):
                    for n in range(N):
                        inputs(g, v, n)
                        if after and n == 4:
                            norm.power(pool, g + 1)
                        if after and n in (14, 18):
                            add_z(g + 1, (n - 14) // 4)

                def add_z(g, i):
                    pool.wait_ge(norm.z_ready, g * GT + GT)
                    at = c.x_pair(g * 2 + i)
                    pool.tensor_tensor(at, at, zt[:, 2 * i:2 * i + 2, :].rearrange("p j d -> p (j d)"), ALU.add)\
                        .then_inc(sem("z_added"), 1)

                norm.power(pool, 0)
                add_z(0, 0)
                add_z(0, 1)
                group_loop(pool, group)

            @block.scalar
            def _(act):
                def front(g, v, n, first=False):
                    if n == 9:
                        norm.copy_out(act, g, *(() if first else (sem("hp_filled"), g * 8)))
                    if n in COPY_AT:
                        i = COPY_AT.index(n)
                        act.wait_ge(sem("hp_filled"), g * 8 + i + 1)
                        act.wait_ge(sem("carry_ready"), g + 1)
                        act.copy(xi[:, i, PAD:PAD + GN], banks[:, FB[i], :]).then_inc(sem("hp_used"), 1)
                    if n == 41:
                        for i in range(CB):
                            act.wait_ge(sem("hp_filled"), g * 8 + CB + i + 1)
                            if i == 0 and not first:
                                act.wait_ge(sem("yg_ready"), g * CB)
                            act.activation(sz[:, v, i, :], banks[:, FB[i], :], ACT.Silu).then_inc(sem("hp_used"), 1)
                        for k in range(CB):
                            act.wait_ge(sem("xc_ready"), g * CB + k + 1)
                            act.activation(u[:, v, k, :], u[:, v, k, :], ACT.Silu, bias=chan[:, k, 4:5]).then_inc(sem("u_ready"), 1)
                    if n == 44:
                        act.wait_ge(sem("xp_filled"), g + 1)
                        act.wait_ge(sem("bc_stored"), g * 16 + 16)
                        act.copy(xd[0:XD, :], banks[0:XD, 6, :]).then_inc(sem("xd_ready"), 1)
                    if 50 <= n < 54:
                        k = n - 50
                        act.wait_ge(sem("dt_filled"), g * CB + k + 1)
                        act.wait_ge(sem("delta_ready"), g * CB + k + 1)
                        if k == 0 and not first:
                            act.wait_ge(sem("out_filled"), g * 2)
                        act.activation(ex[:, k, :], banks[:, FB[(k + 1) % 4], :], ACT.Abs, bias=chan[:, k, 5:6])\
                           .then_inc(sem("abs_ready"), 1)
                        act.activation(delta[:, v, k, :], banks[:, FB[(k + 1) % 4], :], ACT.Relu, bias=chan[:, k, 5:6])\
                           .then_inc(sem("relu_ready"), 1)
                    if n == 54:
                        for k in range(CB):
                            act.wait_ge(sem("abs_ready"), g * CB + k + 1)
                            act.activation(ex[:, k, :], ex[:, k, :], ACT.Exp, scale=-1.0).then_inc(sem("exp_ready"), 1)
                    if n == 57:
                        for k in range(CB):
                            act.wait_ge(sem("exp_ready"), g * CB + k + 1)
                            act.activation(ex[:, k, :], ex[:, k, :], ACT.Ln, bias=1.0).then_inc(sem("ln_ready"), 1)

                def decay(g, v, n):
                    st, k = n // CB, n % CB
                    if n == 0:
                        act.wait_ge(sem("delta_ready"), g * CB + CB + START["delta_ready"])
                    act.wait_ge(sem("h_ready"), g * N + n + 1)
                    act.activation(dA[:, n % AHEAD, :], delta[:, v, k, :], ACT.Exp, scale=a_neg[:, k, st:st + 1])\
                       .then_inc(sem("dA_ready"), 1)

                def group(g, v, before, after):
                    for n in range(N):
                        decay(g, v, n)
                        if after:
                            front(g + 1, 1 - v, n)

                act.wait_ge(sem("loaded"), 16 * 7)
                act.activation(a_log[:, :, :], a_log[:, :, :], ACT.Exp).then_inc(sem("a_ready"), 1)
                act.wait_ge(sem("a_ready"), 2)
                for n in range(N):
                    front(0, 0, n, first=True)
                group_loop(act, group)

            @block.vector
            def _(dve):
                STEPS = TAPS - 1

                def front(g, v, n, first=False):
                    if n == 0:
                        norm.moments(dve, g)
                    if n == 2:
                        if not first:
                            dve.wait_ge(sem("xc_ready"), g * CB)
                        if v == 0:
                            dve.memset(xi[:, :, 0:PAD], 0.0).then_inc(sem("carry_ready"), 1)
                        else:
                            dve.tensor_copy(xi[:, :, 0:PAD], xi[:, :, GN:GN + PAD]).then_inc(sem("carry_ready"), 1)
                    if n == 3:
                        dve.wait_ge(sem("z_added"), g * 2 + 2)
                        norm.normalise(dve, g, lambda j: zt[:, j, :], first=first)
                    for k, j in ((k, n - CONV_AT[k]) for k in range(CB) if CONV_AT[k] <= n < CONV_AT[k] + TAPS):
                        src = xi[:, k, j:j + GN]
                        if j == 0:
                            dve.wait_ge(sem("hp_used"), g * 8 + k + 1)
                            dve.wait_ge(sem("carry_ready"), g + 1)
                            if k == 0 and not first:
                                dve.wait_ge(sem("skip_ready"), g * CB)
                            ins = dve.tensor_scalar(u[:, v, k, :], src, chan[:, k, 0:1], None, ALU.mult)
                        else:
                            dve.wait_ge(sem("conv_step"), (g * CB + k) * STEPS + j)
                            ins = dve.scalar_tensor_tensor(u[:, v, k, :], src, chan[:, k, j:j + 1], u[:, v, k, :],
                                                           ALU.mult, ALU.add)
                        ins.then_inc(sem("conv_step" if j < TAPS - 1 else "xc_ready"), 1)
                    if n >= 60:
                        k = n - 60
                        dve.wait_ge(sem("ln_ready"), g * CB + k + 1)
                        dve.tensor_tensor(delta[:, v, k, :], delta[:, v, k, :], ex[:, k, :], ALU.add).then_inc(sem("delta_ready"), 1)

                def scan(g, v, n):
                    st, k = n // CB, n % CB
                    dve.wait_ge(sem("dA_ready"), g * N + n + 1)
                    dve.wait_ge(sem("dBu_ready"), g * N + n + 1)
                    dve.wait_ge(sem("hc_ready"), g * N + n + 1)
                    if v == 0 and k == 0 and st >= 2:
                        dve.wait_ge(sem("h_end_ready"), g * (NS // 2) + st - 1)
                    if v == 1 and n == 0:
                        dve.wait_ge(sem("h_end_ready"), (g + 1) * (NS // 2))
                    dve.tensor_tensor_scan(h[:, n % AHEAD, :], dA[:, n % AHEAD, :], dBu[:, k, :],
                                           0.0 if v == 0 else h_end[:, st, k:k + 1], ALU.mult, ALU.add).then_inc(sem("h_ready"), 1)

                def times_c(g, n):
                    st, k = n // CB, n % CB
                    dve.wait_ge(sem("h_ready"), g * N + n + 1 + START["h_ready"])
                    dve.wait_ge(sem("hc_used"), g * N + n + 1)
                    dve.tensor_tensor(hc[:, k, :], h[:, n % AHEAD, :], bcs[:, st % 4, 1, :], ALU.mult).then_inc(sem("hc_ready"), 1)

                def keep_end(g, st):
                    dve.wait_ge(sem("h_ready"), g * N + st * CB + CB + START["h_ready"])
                    at = (st % 2) * CB
                    dve.tensor_copy(h_end[:, st, :], h[:, at:at + CB, GN - 1]).then_inc(sem("h_end_ready"), 1)

                def skip(g, v):
                    dve.wait_ge(sem("hc_used"), g * N + N + START["hc_used"])
                    for k in range(CB):
                        dve.scalar_tensor_tensor(du[:, v, k, :], u[:, v, k, :], chan[:, k, 6:7], banks[:, k, :], ALU.mult,
                                                 ALU.add).then_inc(sem("skip_ready"), 1)

                def gate(g, v, k):
                    dve.wait_ge(sem("skip_ready"), g * CB + k + 1 + START["skip_ready"])
                    dve.tensor_tensor(delta[:, v, k, :], du[:, v, k, :], sz[:, v, k, :], ALU.mult).then_inc(sem("yg_ready"), 1)

                def add(g, i):
                    dve.wait_ge(sem("out_filled"), g * 2 + i + 1 + START["out_filled"])
                    at = c.x_pair(g * 2 + i)
                    dve.tensor_tensor(at, banks[:, 4 + i, :], at, ALU.add).then_inc(sem("out_used"), 1)

                def group(g, v, before, after):
                    for n in range(N):
                        scan(g, v, n)
                        if before and n == 1:
                            skip(g - 1, 1 - v)
                        if n >= 1:
                            times_c(g, n - 1)
                        if v == 0 and n % CB == 0 and n > 0:
                            keep_end(g, n // CB - 1)
                        if before and 2 <= n < 2 + CB:
                            gate(g - 1, 1 - v, n - 2)
                        if before and n in ADD_AT:
                            add(g - 1, ADD_AT.index(n))
                        if after:
                            front(g + 1, 1 - v, n)
                    times_c(g, N - 1)
                    if v == 0:
                        keep_end(g, NS - 1)

                for n in ("z_added", "relu_ready", "h_ready", "hc_ready", "hc_used", "skip_ready", "yg_ready", "out_used",
                          "delta_ready"):
                    dve.sem_inc(sem(n), START[n])
                dve.memset(wdt[:, :], 0.0).then_inc(sem("consts"), 1)
                dve.memset(xd[:, :], 0.0).then_inc(sem("consts"), 1)
                dve.wait_ge(sem("loaded"), 16 * 7)
                for k in range(KD):
                    dve.tensor_scalar(win[:, k, :], win[:, k, :], nw[:, k:k + 1], None, ALU.mult).then_inc(sem("w_ready"), 1)
                dve.wait_ge(sem("a_ready"), 1)
                dve.tensor_scalar(a_neg[:, :, :], a_log[:, :, :], -1.0, None, ALU.mult).then_inc(sem("a_ready"), 1)
                dve.wait_ge(c.x_loaded[0], 16)
                for n in range(N):
                    front(0, 0, n, first=True)
                dve.wait_ge(c.x_loaded[1], 16 * B)
                group_loop(dve, group)
                skip(G - 1, 1)
                for k in range(CB):
                    gate(G - 1, 1, k)
                for i in range(2):
                    add(G - 1, i)


RANK = 16


def prepare_ffn(c):
    nc = c.nc
    w1T = c.keep("ffn_w1T", [P, KD, HID])
    w2T = c.keep("ffn_w2T", [P, HB, D])
    c.prepared["ffn"] = (w1T, w2T)
    with Local(c, "ffnprep") as s:
        wfc = s.sb("wfc", [P, HB, D])
        wpr = s.sb("wpr", [P, KD, HID])
        scale = s.sb("scale", [P, HB + KD])
        half = s.sb("half", [P, HB + KD])
        nhalf = s.sb("nhalf", [P, HB + KD])
        hi = s.sb("hi", [P, (HB + KD), HID])
        uT = s.sb("uT", [RANK, HID])
        fb = s.sb("fb", [RANK, RANK])
        v = s.sb("v", [RANK, D])
        gate = s.sb("gate", [RANK, 1])
        ufT = s.sb("ufT", [RANK, HID])
        pu = s.ps("pu", [RANK, 2, 512])
        pw = s.ps("pw", [P, 4, 512])
        loaded, small_loaded = s.sem("loaded"), s.sem("small_loaded")
        step, uf_ready, uf_scaled = s.sem("step"), s.sem("uf_ready"), s.sem("uf_scaled")
        tern_ready, tr_ready, tr_used = s.sem("tern_ready"), s.sem("tr_ready"), s.sem("tr_used")
        rows = [(wfc[:, b, :], hi[:, b, 0:D], D) for b in range(HB)] + \
               [(wpr[:, b, :], hi[:, HB + b, :], HID) for b in range(KD)]
        with nc.Block() as block:
            @block.sync
            def _(sp):
                sp.dma_start(wfc[:, :, :], c.ins["w_fc"].rearrange("(b p) d -> p b d", p=P)).then_inc(loaded, 16)
                sp.dma_start(wpr[:, :, :], c.ins["w_proj"].rearrange("(b p) d -> p b d", p=P)).then_inc(loaded, 16)
                sp.dma_start(uT[:, :], c.ins["uT"]).then_inc(small_loaded, 16)
                sp.dma_start(fb[:, :], c.ins["fast_b"]).then_inc(small_loaded, 16)
                sp.dma_start(v[:, :], c.ins["v"]).then_inc(small_loaded, 16)
                sp.dma_start(gate[:, :], c.ins["gate"].to_broadcast((RANK, 1))).then_inc(small_loaded, 16)

            @block.vector
            def _(dve):
                done = 0

                def matrix(first, last, n):
                    nonlocal done
                    for i in range(first, last):
                        dve.tensor_reduce(scale[:, i:i + 1], rows[i][0], AX.X, ALU.add, apply_absolute_value=True).then_inc(step, 1)
                    done += last - first
                    dve.wait_ge(step, done)
                    at = slice(first, last)
                    dve.tensor_scalar(scale[:, at], scale[:, at], 1.0 / n, EPS, ALU.mult, ALU.max).then_inc(step, 1)
                    dve.wait_ge(step, done + 1)
                    dve.tensor_scalar(half[:, at], scale[:, at], 0.5, None, ALU.mult).then_inc(step, 1)
                    dve.tensor_scalar(nhalf[:, at], scale[:, at], -0.5, None, ALU.mult).then_inc(step, 1)
                    done += 3
                    dve.wait_ge(step, done)
                    for i in range(first, last):
                        w, up, _ = rows[i]
                        dve.tensor_scalar(up, w, half[:, i:i + 1], scale[:, i:i + 1], ALU.is_gt, ALU.mult).then_inc(step, 1)
                        dve.wait_ge(step, done + 1)
                        dve.tensor_scalar(w, w, nhalf[:, i:i + 1], scale[:, i:i + 1], ALU.is_lt, ALU.mult).then_inc(step, 1)
                        dve.wait_ge(step, done + 2)
                        done += 2
                        dve.tensor_tensor(w, up, w, ALU.subtract).then_inc(tern_ready, 1)

                dve.wait_ge(loaded, 32)
                matrix(0, HB, D)
                dve.wait_ge(uf_ready, 1)
                dve.wait_ge(small_loaded, 64)
                dve.tensor_scalar(ufT[:, :], pu[:, :, :].rearrange("p a n -> p (a n)"), gate[:, 0:1], None,
                                  ALU.mult).then_inc(uf_scaled, 1)
                matrix(HB, HB + KD, HID)

            @block.tensor
            def _(pe):
                pe.wait_ge(small_loaded, 64)
                for n in range(2):
                    mm = pe.matmul(pu[:, n, :], fb[:, :], uT[:, n * 512:(n + 1) * 512], start=True, stop=True)
                mm.then_inc(uf_ready, 1)
                pe.wait_ge(uf_scaled, 1)
                pe.wait_ge(tern_ready, HB)
                for k in range(KD):
                    for n in range(2):
                        for b in range(4):
                            pe.matmul(pw[:, 2 * k + n, b * P:(b + 1) * P], wfc[:, 4 * n + b, k * P:(k + 1) * P],
                                      c.ident[:, :], start=(b == 0), stop=False, skip_group_check=True)
                        mm = pe.matmul(pw[:, 2 * k + n, :], v[:, k * P:(k + 1) * P], ufT[:, n * 512:(n + 1) * 512],
                                       start=False, stop=True, skip_group_check=True)
                        mm.then_inc(tr_ready, 1)
                pe.wait_ge(tern_ready, HB + KD)
                for b in range(0, HB, 2):
                    pe.wait_ge(tr_used, b // 2 + 1)
                    for i in range(2):
                        for k in range(KD):
                            mm = pe.transpose(pw[:, b // 2, i * D + k * P:i * D + (k + 1) * P],
                                              wpr[:, k, (b + i) * P:(b + i + 1) * P], c.ident[:, :])
                    mm.then_inc(tr_ready, 1)

            @block.scalar
            def _(act):
                for i in range(4):
                    act.wait_ge(tr_ready, i + 1)
                    act.copy(w1T[:, i // 2, (i % 2) * 512:(i % 2 + 1) * 512], pw[:, i, :]).then_inc(tr_used, 1)
                for i in range(4):
                    act.wait_ge(tr_ready, 5 + i)
                    act.copy(w2T[:, 2 * i:2 * i + 2, :].rearrange("p a n -> p (a n)"), pw[:, i, :]).then_inc(tr_used, 1)


def stage_ffn(c, name):
    nc = c.nc
    w1T, w2T = c.prepared["ffn"]
    with Local(c, name) as s:
        norm = Norm(c, s)
        r = s.sb("relu", [P, 2, GN])
        h = s.sb("h", [P, HB, GN])
        hp = s.ps("hp", [P, 4, GN])
        yp = s.ps("yp", [P, GT, D])
        h_filled, relu_ready, h_ready = s.sem("h_filled"), s.sem("relu_ready"), s.sem("h_ready")
        y_ready, y_used = s.sem("y_ready"), s.sem("y_used")
        with nc.Block() as block:
            @block.tensor
            def _(pe):
                def up(g, first=False):
                    pe.wait_ge(norm.xT_ready, g * KD + KD)
                    for b in range(HB):
                        if not (first and b < 4):
                            pe.wait_ge(h_ready, g * HB + b - 3)
                        for k in range(KD):
                            mm = pe.matmul(hp[:, b % 4, :], w1T[:, k, b * P:(b + 1) * P], norm.xT[:, k, :],
                                           start=(k == 0), stop=(k == KD - 1))
                        mm.then_inc(h_filled, 1)

                def down(g, first=False):
                    pe.wait_ge(h_ready, g * HB + HB)
                    for j in range(GT):
                        if j % 2 == 0 and not first:
                            pe.wait_ge(y_used, g * 2 - 1 + j // 2)
                        for b in range(HB):
                            mm = pe.matmul(yp[:, j, :], h[:, b, j * P:(j + 1) * P], w2T[:, b, :],
                                           start=(b == 0), stop=(b == HB - 1))
                        if j % 2 == 1:
                            mm.then_inc(y_ready, 1)

                norm.transposes(pe, 0, first=True)
                up(0, first=True)
                norm.transposes(pe, 1)
                down(0, first=True)
                up(1)
                with pe.Fori(2, G) as g:
                    norm.transposes(pe, g)
                    down(g - 1)
                    up(g)
                down(G - 1)

            @block.gpsimd
            def _(pool):
                norm.pool_prologue(pool)
                norm.power(pool, 0)
                with pool.Fori(1, G) as g:
                    norm.power(pool, g)

            @block.scalar
            def _(act):
                def relu(g, first=False):
                    for b in range(HB):
                        act.wait_ge(h_filled, g * HB + b + 1)
                        if not (first and b < 2):
                            act.wait_ge(h_ready, g * HB + b - 1)
                        act.activation(r[:, b % 2, :], hp[:, b % 4, :], ACT.Relu).then_inc(relu_ready, 1)

                norm.copy_out(act, 0)
                relu(0, first=True)
                with act.Fori(1, G) as g:
                    norm.copy_out(act, g, h_filled, g * HB)
                    relu(g)

            @block.vector
            def _(dve):
                def square(g, first=False):
                    for b in range(HB):
                        dve.wait_ge(relu_ready, g * HB + b + 1)
                        if b == 0 and not first:
                            dve.wait_ge(y_ready, g * 2)
                        dve.tensor_tensor(h[:, b, :], r[:, b % 2, :], r[:, b % 2, :], ALU.mult).then_inc(h_ready, 1)

                def add(g):
                    for i in range(2):
                        dve.wait_ge(y_ready, g * 2 + i + 1)
                        pair = c.x_pair(g * 2 + i)
                        dve.tensor_tensor(pair, yp[:, 2 * i:2 * i + 2, :].rearrange("p a n -> p (a n)"), pair,
                                          ALU.add).then_inc(y_used, 1)

                norm.moments(dve, 0)
                norm.normalise(dve, 0, first=True)
                norm.moments(dve, 1)
                norm.normalise(dve, 1)
                square(0, first=True)
                with dve.Fori(1, G - 1) as g:
                    norm.moments(dve, g + 1)
                    add(g - 1)
                    norm.normalise(dve, g + 1)
                    square(g)
                add(G - 2)
                square(G - 1)
                add(G - 1)


AH, AD = 16, 16
PARTS = 6
KS = PARTS * AD
KM = KS + 2
Q_TILES = L // P
CHUNKS = 12
HG = 4
VP = 32
ST = 3
LORA_SCALE = 4.0
LORA_R = 8


def stage_attn(c):
    nc = c.nc
    with Local(c, "attn") as s:
        banks = s.ps("banks", [P, 8, 512])
        norm = Norm(c, s, trp=banks[:, 0:2, :])
        w = s.sb("w", [P, KD, 3 * D])
        wo = s.sb("wo", [P, KD, D])
        loraA = s.sb("loraA", [LORA_R, 2, D])
        loraB = s.sb("loraB", [LORA_R, 2, D])
        rope = s.sb("rope", [P, Q_TILES, 2, AD])
        causal32 = s.sb("causal32", [P, 3, P])
        causal = s.sb("causal", [P, 3, P], BF16)
        ra = s.sb("ra", [P, 2, 2 * AH, AD])
        rb = s.sb("rb", [P, 2, 2 * AH, AD])
        r = s.sb("r", [P, 2, 2 * AH, AD])
        r1 = s.sb("r1", [P, 2, 2 * AH, AD])
        stk = s.sb("stk", [P, 4, 2 * AH, KM], BF16)
        qT = s.sb("qT", [KM, AH, L], BF16)
        kT = s.sb("kT", [KM, AH, L], BF16)
        v = s.sb("v", [P, Q_TILES, AH, AD])
        vh = s.sb("vh", [P, HG, Q_TILES, VP])
        mp = s.sb("mp", [P, 2, Q_TILES, 2])
        nm = s.sb("nm", [P, 2, Q_TILES])
        nmb = s.sb("nmb", [P, 2, 2, Q_TILES], BF16)
        nmT = s.sb("nmT", [2 * Q_TILES, P], BF16)
        probs = s.sb("probs", [P, ST, 512])
        ov = ra[:, :, :, :].rearrange("p a h d -> p (a h d)")
        rec = s.sb("rec", [P, 2, GT, HG])
        o = s.sb("o", [P, Q_TILES, D])
        oT = (s.sb("oT", [P, KD, GN]), rb[:, :, :, :].rearrange("p a h d -> p (a h d)").rearrange("p (k n) -> p k n", k=KD))
        names = ("loaded lora_filled w_ready qkv_filled qp_used roped r_ready p1_ready r1_ready p2_ready p3_ready dup_ready "
                 "stT_filled evac_act evac_dve sa_filled sa_used max_ready part_ready m_ready mt_filled mt_copied "
                 "m_loaded st_filled exp_ready pv_done vh_ready ov_ready ot_filled rec_ready o_used oT_filled oT_ready y_ready y_used consts zeroed parts_seen")
        S = {n: s.sem(n) for n in names.split()}

        def sem(n):
            return S[n]

        START = {"qp_used": 2, "p3_ready": 2, "r_ready": 2, "r1_ready": 2, "evac_act": 1, "evac_dve": 1, "sa_used": 2,
                 "exp_ready": ST + 2 * CHUNKS, "pv_done": ST + HG * CHUNKS, "vh_ready": 1, "ov_ready": 2, "ot_filled": 2,
                 "mt_copied": 1, "m_loaded": 16, "o_used": 1, "oT_ready": 1, "y_used": 1}
        bf = [banks[:, i, :].bitcast(BF16).rearrange("p (h n) -> p h n", n=P) for i in range(8)]
        LAST = Q_TILES + 2

        def chunks(qt):
            return [(0, 512), (512, (qt + 1) * P - 512)] if qt >= 4 else [(0, (qt + 1) * P)]

        STEPS = [(kt, half, max(kt * P, half * 512), (half + 1) * 512 - max(kt * P, half * 512))
                 for kt in range(Q_TILES) for half in range(kt // GT, 2)]
        A_CHUNKS = [(qt, half, at, size) for qt in reversed(range(Q_TILES)) for half, (at, size) in enumerate(chunks(qt))]

        def head_loop(engine, body):
            body(0, 0, 0)
            with engine.Fori(0, HG - 1) as hh:
                for j in range(1, HG):
                    body(hh * HG + j, hh, j)
                body(hh * HG + HG, hh + 1, 0)
            for h in range(AH - HG + 1, AH):
                body(h, h // HG, h % HG)

        with nc.Block() as block:
            @block.sync
            def _(sp):
                sp.sem_inc(sem("m_loaded"), START["m_loaded"])
                for i, n in enumerate(("attn_wq", "attn_wk", "attn_wv")):
                    sp.dma_start(w[:, :, i * D:(i + 1) * D], c.ins[n].rearrange("(k p) n -> p k n", p=P)).then_inc(sem("loaded"), 16)
                sp.dma_start(wo[:, :, :], c.ins["attn_wo"].rearrange("(k p) n -> p k n", p=P)).then_inc(sem("loaded"), 16)
                for i, n in enumerate("qv"):
                    sp.dma_start(loraA[:, i, :], c.ins[f"attn_A{n}T"]).then_inc(sem("loaded"), 16)
                    sp.dma_start(loraB[:, i, :], c.ins[f"attn_B{n}"]).then_inc(sem("loaded"), 16)
                sp.dma_start(rope[:, :, :, :].rearrange("p t a d -> p t (a d)"), c.ins["rope"]).then_inc(sem("loaded"), 16)
                sp.dma_start(causal32[:, :, :], c.ins["causal"]).then_inc(sem("loaded"), 16)
                with sp.Fori(0, B) as b:
                    with sp.Fori(0, AH) as h:
                        sp.wait_ge(sem("mt_copied"), b * AH + h + 2)
                        sp.dma_start(qT[KS:KM, bass.ds(h, 1), :], nmT[:, :]).then_inc(sem("m_loaded"), 16)

            @block.tensor
            def _(pe):
                def project(b, t):
                    at, j = 2 + 2 * (t % 2), t % GT
                    pe.wait_ge(sem("qp_used"), b * Q_TILES + t + 1)
                    for n, size, bank in ((0, 512, at), (512, 256, at + 1)):
                        for k in range(KD):
                            mm = pe.matmul(banks[:, bank, 0:size], norm.xT[:, k, j * P:(j + 1) * P], w[:, k, n:n + size],
                                           start=(k == 0), stop=(k == KD - 1))
                    mm.then_inc(sem("qkv_filled"), 1)

                def stack_transposes(b, t):
                    T0 = b * Q_TILES + t
                    pe.wait_ge(sem("p3_ready"), T0 + 3)
                    pe.wait_ge(sem("dup_ready"), T0 + 1)
                    for i in range(4):
                        if i == 0:
                            pe.wait_ge(sem("evac_act"), T0 * 3 + 1)
                        if i == 2:
                            pe.wait_ge(sem("evac_act"), T0 * 3 + 2)
                        if i == 3:
                            pe.wait_ge(sem("evac_dve"), T0 + 2)
                        for n in range(8):
                            mm = pe.transpose(bf[6 + i % 2][0:KM, n, :], stk[:, t % 4, i * 8 + n, :], causal[:, 2, :])
                        mm.then_inc(sem("stT_filled"), 1)

                def scores_q(b, h, i):
                    qt, half, at, size = A_CHUNKS[i]
                    pe.wait_ge(sem("sa_used"), (b * AH + h) * CHUNKS + i + 1)
                    diag = at + size == (qt + 1) * P
                    mm = pe.matmul(banks[:, i % 2, 0:size], qT[0:KS, bass.ds(h, 1), qt * P:(qt + 1) * P],
                                   kT[0:KS, bass.ds(h, 1), at:at + size], start=True, stop=not diag, skip_group_check=True)
                    if diag:
                        mm = pe.matmul(banks[:, i % 2, size - P:size], causal[:, 2, :], causal[:, 0, :],
                                       start=False, stop=True, skip_group_check=True)
                    mm.then_inc(sem("sa_filled"), 1)

                def scores_k(b, h, i):
                    H = b * AH + h
                    kt, _, at, size = STEPS[i]
                    if i == 0:
                        pe.wait_ge(sem("m_loaded"), H * 16 + 32)
                    pe.wait_ge(sem("exp_ready"), (H + 2) * CHUNKS + i + 1)
                    diag = at == kt * P
                    mm = pe.matmul(banks[:, 2 + i % ST, 0:size], kT[:, bass.ds(h, 1), kt * P:(kt + 1) * P],
                                   qT[:, bass.ds(h, 1), at:at + size], start=True, stop=not diag, skip_group_check=True)
                    if diag:
                        mm = pe.matmul(banks[:, 2 + i % ST, 0:P], causal[:, 2, :], causal[:, 1, :],
                                       start=False, stop=True, skip_group_check=True)
                    mm.then_inc(sem("st_filled"), 1)

                def values(b, h, hg, j, i, before=0):
                    kt, half, at, size = STEPS[i]
                    H = b * AH + h - before
                    pe.wait_ge(sem("exp_ready"), (H + 2) * CHUNKS + i + 1 + ST)
                    if i == 0:
                        pe.wait_ge(sem("vh_ready"), H + 2)
                    if kt == 0 and j == 0:
                        pe.wait_ge(sem("ov_ready"), b * (2 * AH // HG) + hg * 2 + half + 1)
                    pe.matmul(banks[j * VP:(j + 1) * VP, 6 + half, at - half * 512:at - half * 512 + size], vh[:, j, kt, :],
                              probs[:, i % ST, 0:size], start=(kt == 0), stop=(at == kt * P and (kt + 1) % GT == 0),
                              skip_group_check=True).then_inc(sem("pv_done"), 1)

                def max_transpose(b, h, slot):
                    H = b * AH + h
                    pe.wait_ge(sem("m_ready"), H + 1)
                    pe.wait_ge(sem("mt_copied"), H + 1)
                    pe.transpose(bf[5][0:2 * Q_TILES, 0, :], nmb[:, slot, :, :].rearrange("p a q -> p (a q)"),
                                 causal[:, 2, :]).then_inc(sem("mt_filled"), 1)

                def turn(b, hg, u, copied):
                    R = b * (2 * AH // HG) + hg * 2 + u
                    pe.wait_ge(sem("ov_ready"), b * (2 * AH // HG) + hg * 2 + u + 3)
                    pe.wait_ge(sem("o_used"), R + 1)
                    pe.wait_ge(sem("mt_copied"), copied)
                    for n in range(GT):
                        mm = pe.transpose(banks[:, 5, n * P:(n + 1) * P], ov[:, (u * GT + n) * P:(u * GT + n + 1) * P],
                                          c.ident[:, :])
                    mm.then_inc(sem("ot_filled"), 1)

                def body(b, h, hg, j):
                    peeled = isinstance(h, int)
                    for i in range(CHUNKS):
                        scores_k(b, h, i)
                        if not (peeled and h >= AH - 2):
                            scores_q(b, h + 2, i)
                        if i >= 2:
                            values(b, h, hg, j, i - 2)
                        elif not (peeled and h == 0):
                            values(b, h, hg, (j - 1) % HG, CHUNKS - 2 + i, before=1)
                        if i == 3 and not (peeled and h == AH - 1):
                            if not (peeled and h == 0):
                                pe.wait_ge(sem("o_used"), b * (2 * AH // HG) + (hg if j else hg - 1) * 2 + 1)
                            max_transpose(b, h + 1, (j + 1) % 2)
                        if j == 0 and not (peeled and h == 0) and i in (6, 10):
                            turn(b, hg - 1, (i - 6) // 4, b * AH + h + 3)

                pe.sem_inc(sem("pv_done"), START["pv_done"])
                pe.sem_inc(sem("ot_filled"), START["ot_filled"])
                pe.wait_ge(sem("loaded"), 16 * 10)
                for i in range(2):
                    for k in range(KD):
                        mm = pe.matmul(banks[:, i, k * D:(k + 1) * D], loraA[:, i, k * P:(k + 1) * P], loraB[:, i, :],
                                       start=True, stop=True)
                mm.then_inc(sem("lora_filled"), 1)
                pe.wait_ge(sem("w_ready"), 2 * KD)
                pe.wait_ge(sem("consts"), 3)
                with pe.Fori(0, B) as b:
                    pe.wait_ge(sem("sa_used"), b * (AH * CHUNKS) + START["sa_used"])
                    pe.wait_ge(sem("ov_ready"), b * (2 * AH // HG) + START["ov_ready"])
                    pe.wait_ge(sem("mt_copied"), b * AH + 1)
                    pe.wait_ge(sem("y_used"), b * 2 + 1)
                    for t in range(-1, LAST):
                        if t + 1 < Q_TILES:
                            if (t + 1) % GT == 0:
                                g = b * 2 + (t + 1) // GT
                                if t + 1 == 0:
                                    pe.wait_ge(sem("oT_ready"), b * (2 * KD) + 1)
                                else:
                                    pe.wait_ge(norm.xT_ready, g * KD)
                                norm.transposes(pe, g, first=True)
                                pe.wait_ge(norm.xT_ready, g * KD + KD)
                            project(b, t + 1)
                        if t >= 2:
                            stack_transposes(b, t - 2)
                    pe.wait_ge(sem("qp_used"), b * Q_TILES + Q_TILES + START["qp_used"])
                    pe.wait_ge(sem("evac_act"), (b * Q_TILES + Q_TILES) * 3 + 1)
                    pe.wait_ge(sem("evac_dve"), b * Q_TILES + Q_TILES + 1)
                    for i in range(CHUNKS):
                        scores_q(b, 0, i)
                    for i in range(CHUNKS):
                        scores_q(b, 1, i)
                        if i == 5:
                            max_transpose(b, 0, 0)
                    head_loop(pe, lambda h, hg, j: body(b, h, hg, j))
                    for i in (CHUNKS - 2, CHUNKS - 1):
                        values(b, AH, 0, HG - 1, i, before=1)
                    for u in range(2):
                        turn(b, AH // HG - 1, u, b * AH + AH + 1)
                    pe.wait_ge(sem("o_used"), (b + 1) * (2 * AH // HG) + 1)
                    pe.wait_ge(sem("oT_ready"), b * (2 * KD) + 1)
                    for u in range(2):
                        for k in range(KD):
                            for j in range(GT):
                                mm = pe.transpose(banks[:, 6 * u + k, j * P:(j + 1) * P], o[:, u * GT + j, k * P:(k + 1) * P],
                                                  c.ident[:, :])
                        mm.then_inc(sem("oT_filled"), 1)
                    for u in range(2):
                        pe.wait_ge(sem("oT_ready"), (b * 2 + u) * KD + KD + 1)
                        for j in range(GT):
                            for k in range(KD):
                                mm = pe.matmul(banks[:, 2 + 2 * u + j // 2, (j % 2) * D:(j % 2 + 1) * D],
                                               oT[u][:, k, j * P:(j + 1) * P], wo[:, k, :], start=(k == 0), stop=(k == KD - 1))
                        mm.then_inc(sem("y_ready"), 1)

            @block.gpsimd
            def _(pool):
                norm.pool_prologue(pool)
                pool.sem_inc(sem("r_ready"), START["r_ready"])
                pool.sem_inc(sem("vh_ready"), START["vh_ready"])
                def sequence(b, last=False):
                    norm.power(pool, b * 2 + 1)
                    for t in range(Q_TILES + 1):
                        if t < Q_TILES:
                            T0 = b * Q_TILES + t
                            pool.wait_ge(sem("roped"), T0 + 1)
                            pool.wait_ge(sem("r1_ready"), T0 + 1)
                            pool.tensor_tensor(r[:, t % 2], ra[:, t % 2], rb[:, t % 2], ALU.add).then_inc(sem("r_ready"), 1)
                        if t >= 1:
                            m = t - 1
                            st = stk[:, m % 4, :, 0:KS].rearrange("p h (a d) -> p h a d", d=AD)
                            pool.wait_ge(sem("p1_ready"), b * Q_TILES + m + 1)
                            pool.sem_inc(sem("parts_seen"), 1)
                            pool.tensor_copy(st[:, 0:AH, 1, :], st[:, 0:AH, 0, :])
                            pool.tensor_copy(st[:, 0:AH, 2, :], st[:, 0:AH, 0, :])
                            pool.tensor_copy(st[:, AH:, 3, :], st[:, AH:, 0, :]).then_inc(sem("dup_ready"), 1)
                    pool.wait_ge(sem("qp_used"), b * Q_TILES + Q_TILES + START["qp_used"])
                    pool.sem_inc(sem("parts_seen"), 1)
                    with pool.Fori(0, AH // HG) as hg:
                        for j in range(HG):
                            H = b * AH + hg * HG + j
                            pool.wait_ge(sem("pv_done"), H * CHUNKS + ST + CHUNKS)
                            pool.sem_inc(sem("parts_seen"), 1)
                            pool.tensor_copy(vh[:, j, :, 0:AD], v[:, :, bass.ds(hg * HG + j, 1), :].rearrange("p t h d -> p t (h d)"))\
                                .then_inc(sem("vh_ready"), 1)
                    if not last:
                        norm.power(pool, b * 2 + 2)

                norm.power(pool, 0)
                with pool.Fori(0, B - 1) as b:
                    sequence(b)
                sequence(B - 1, last=True)

            @block.scalar
            def _(act):
                def evac(b, t, i):
                    act.wait_ge(sem("stT_filled"), (b * Q_TILES + t) * 4 + i + 1)
                    rows = KS if i < 2 else KM
                    dst = (qT if i < 2 else kT)[0:rows, (i % 2) * 8:(i % 2) * 8 + 8, t * P:(t + 1) * P]
                    act.copy(dst, bf[6 + i % 2][0:rows, :, :]).then_inc(sem("evac_act"), 1)

                def first_part(b, t):
                    T0 = b * Q_TILES + t
                    act.wait_ge(sem("r_ready"), T0 + 3)
                    if t >= 4:
                        act.wait_ge(sem("stT_filled"), b * (Q_TILES * 4) + (t - 3) * 4)
                    act.copy(stk[:, t % 4, :, 0:AD], r[:, t % 2]).then_inc(sem("p1_ready"), 1)

                def second_part(b, t):
                    act.wait_ge(sem("r1_ready"), b * Q_TILES + t + 3)
                    act.copy(stk[:, t % 4, :, 4 * AD:5 * AD], r1[:, t % 2]).then_inc(sem("p2_ready"), 1)

                def exps(b, h, i):
                    H = b * AH + h
                    size = STEPS[i][3]
                    act.wait_ge(sem("st_filled"), H * CHUNKS + i + 1)
                    act.wait_ge(sem("pv_done"), H * CHUNKS + i + 1 + HG * CHUNKS)
                    act.activation(probs[:, i % ST, 0:size], banks[:, 2 + i % ST, 0:size], ACT.Exp, scale=AD ** -0.5)\
                       .then_inc(sem("exp_ready"), 1)

                def copy_max(b, h):
                    H = b * AH + h
                    act.wait_ge(sem("mt_filled"), H + 1)
                    act.wait_ge(sem("m_loaded"), H * 16 + 16)
                    act.copy(nmT[:, :], bf[5][0:2 * Q_TILES, 0, :]).then_inc(sem("mt_copied"), 1)

                def copy_sums(b, hg, u):
                    H = b * AH + hg * HG + HG - 1
                    act.wait_ge(sem("pv_done"), H * CHUNKS + (7, 12)[u] + START["pv_done"])
                    act.wait_ge(sem("ot_filled"), b * (2 * AH // HG) + hg * 2 + u + 1)
                    act.copy(ov[:, u * 512:(u + 1) * 512], banks[:, 6 + u, :]).then_inc(sem("ov_ready"), 1)

                def body(b, h, hg, j):
                    peeled = isinstance(h, int)
                    for i in range(CHUNKS):
                        exps(b, h, i)
                        if i == 1 and j == 0 and not (peeled and h == 0):
                            copy_sums(b, hg - 1, 1)
                        if i == 4 and not (peeled and h == AH - 1):
                            copy_max(b, h + 1)
                        if i == 9 and j == HG - 1:
                            copy_sums(b, hg, 0)

                for n in ("evac_act", "exp_ready", "mt_copied", "oT_ready", "ov_ready"):
                    act.sem_inc(sem(n), START[n])
                act.wait_ge(sem("loaded"), 16 * 10)
                act.copy(causal[:, :, :], causal32[:, :, :]).then_inc(sem("consts"), 1)
                with act.Fori(0, B) as b:
                    for t in range(LAST):
                        if t < Q_TILES:
                            if t == 0:
                                norm.copy_out(act, b * 2)
                            if t == GT - 1:
                                norm.copy_out(act, b * 2 + 1, sem("qkv_filled"), b * Q_TILES + GT)
                        if 1 <= t <= Q_TILES:
                            first_part(b, t - 1)
                        if t >= 2:
                            evac(b, t - 2, 0)
                        if 1 <= t <= Q_TILES:
                            second_part(b, t - 1)
                        if t >= 2:
                            evac(b, t - 2, 2)
                            evac(b, t - 2, 3)
                    copy_max(b, 0)
                    head_loop(act, lambda h, hg, j: body(b, h, hg, j))
                    copy_sums(b, AH // HG - 1, 1)
                    for u in range(2):
                        act.wait_ge(sem("oT_filled"), b * 2 + u + 1)
                        for k in range(KD):
                            act.copy(oT[u][:, k, :], banks[:, 6 * u + k, :]).then_inc(sem("oT_ready"), 1)

            @block.vector
            def _(dve):
                def rotate(b, t):
                    T0 = b * Q_TILES + t
                    at = 2 + 2 * (t % 2)
                    dve.wait_ge(sem("qkv_filled"), T0 + 1)
                    dve.wait_ge(sem("r_ready"), T0 + 1)
                    qk = banks[:, at, :].rearrange("p (h d) -> p h d", d=AD)
                    qk2 = banks[:, at, :].rearrange("p (h d two) -> p h d two", d=AD // 2, two=2)
                    rb2 = rb[:, t % 2].rearrange("p h (d two) -> p h d two", two=2)
                    sn = rope[:, t, 1, :].rearrange("p (d two) -> p d two", two=2)
                    dve.tensor_tensor(ra[:, t % 2], qk, rope[:, t, 0, :].unsqueeze(1).to_broadcast((P, 2 * AH, AD)), ALU.mult)
                    for e in range(2):
                        last = dve.tensor_tensor(rb2[:, :, :, e], qk2[:, :, :, 1 - e],
                                                 sn[:, :, e].unsqueeze(1).to_broadcast((P, 2 * AH, AD // 2)), ALU.mult)
                    last.then_inc(sem("roped"), 1)
                    if t == 0:
                        dve.wait_ge(sem("vh_ready"), b * AH + START["vh_ready"])
                    dve.tensor_copy(v[:, t, :, :], banks[:, at + 1, 0:D].rearrange("p (h d) -> p h d", d=AD))\
                       .then_inc(sem("qp_used"), 1)

                def remainder(b, t):
                    dve.wait_ge(sem("p1_ready"), b * Q_TILES + t + 1)
                    dve.wait_ge(sem("p3_ready"), b * Q_TILES + t + 1)
                    dve.tensor_tensor(r1[:, t % 2], r[:, t % 2], stk[:, t % 4, :, 0:AD], ALU.subtract).then_inc(sem("r1_ready"), 1)

                def third_part(b, t):
                    dve.wait_ge(sem("p2_ready"), b * Q_TILES + t + 1)
                    st, rr = stk[:, t % 4], r1[:, t % 2]
                    dve.tensor_copy(st[:, AH:, 5 * AD:6 * AD], st[:, AH:, 0:AD])
                    dve.tensor_copy(st[:, 0:AH, 3 * AD:4 * AD], st[:, 0:AH, 4 * AD:5 * AD])
                    dve.tensor_copy(st[:, AH:, AD:2 * AD], st[:, AH:, 4 * AD:5 * AD])
                    dve.tensor_tensor(st[:, 0:AH, 5 * AD:6 * AD], rr[:, 0:AH], st[:, 0:AH, 4 * AD:5 * AD], ALU.subtract)
                    dve.tensor_tensor(st[:, AH:, 2 * AD:3 * AD], rr[:, AH:], st[:, AH:, 4 * AD:5 * AD], ALU.subtract)\
                       .then_inc(sem("p3_ready"), 1)

                def evac(b, t):
                    dve.wait_ge(sem("stT_filled"), (b * Q_TILES + t) * 4 + 2)
                    dve.tensor_copy(qT[0:KS, 8:16, t * P:(t + 1) * P], bf[7][0:KS, :, :]).then_inc(sem("evac_dve"), 1)

                def chunk_max(b, h, slot, i):
                    qt, half, _, size = A_CHUNKS[i]
                    dve.wait_ge(sem("sa_filled"), (b * AH + h) * CHUNKS + i + 1)
                    dve.tensor_reduce(mp[:, slot, qt, half:half + 1], banks[:, i % 2, 0:size], AX.X,
                                      ALU.max).then_inc(sem("sa_used"), 1)

                def head_max(b, h, slot):
                    H = b * AH + h
                    dve.wait_ge(sem("sa_used"), H * CHUNKS + CHUNKS + START["sa_used"])
                    dve.tensor_reduce(nm[:, slot, :], mp[:, slot, :, :], AX.X, ALU.max, negate=True).then_inc(sem("max_ready"), 1)
                    dve.wait_ge(sem("max_ready"), H + 1)
                    dve.tensor_copy(nmb[:, slot, 0, :], nm[:, slot, :]).then_inc(sem("part_ready"), 1)
                    dve.wait_ge(sem("part_ready"), H + 1)
                    dve.tensor_tensor(nmb[:, slot, 1, :], nm[:, slot, :], nmb[:, slot, 0, :], ALU.subtract).then_inc(sem("m_ready"), 1)

                def normalise(b, hg, u):
                    R = b * (2 * AH // HG) + hg * 2 + u
                    dve.wait_ge(sem("ot_filled"), R + 1 + START["ot_filled"])
                    oo = banks[:, 5, :].rearrange("p (q j d) -> p q j d", j=HG, d=VP)
                    dve.reciprocal(rec[:, u, :, :], oo[:, :, :, AD]).then_inc(sem("rec_ready"), 1)
                    dve.wait_ge(sem("rec_ready"), R + 1)
                    for n in range(GT):
                        last = dve.tensor_tensor(o[:, u * GT + n, bass.ds(hg * (HG * AD), HG * AD)].rearrange("p (j d) -> p j d", d=AD),
                                                 oo[:, n, :, 0:AD],
                                                 rec[:, u, n, :].unsqueeze(2).to_broadcast((P, HG, AD)), ALU.mult)
                    last.then_inc(sem("o_used"), 1)

                def body(b, h, hg, j):
                    peeled = isinstance(h, int)
                    for i in range(CHUNKS):
                        if not (peeled and h >= AH - 2):
                            chunk_max(b, h + 2, j % 2, i)
                        if j == 0 and not (peeled and h == 0) and i in (6, 10):
                            normalise(b, hg - 1, (i - 6) // 4)
                    if not (peeled and h >= AH - 2):
                        head_max(b, h + 2, j % 2)

                for n in ("qp_used", "p3_ready", "r1_ready", "evac_dve", "sa_used", "o_used", "y_used"):
                    dve.sem_inc(sem(n), START[n])
                dve.memset(stk[:, :, :, KS:KM], 1.0).then_inc(sem("consts"), 1)
                dve.memset(vh[:, :, :, :], 0.0).then_inc(sem("zeroed"), 1)
                dve.wait_ge(sem("zeroed"), 1)
                dve.memset(vh[:, :, :, AD:AD + 1], 1.0)
                dve.memset(mp[:, :, :, :], -3e38).then_inc(sem("consts"), 1)
                dve.wait_ge(sem("loaded"), 16 * 10)
                dve.wait_ge(sem("lora_filled"), 1)
                for i, n in ((0, 0), (1, 2)):
                    for k in range(KD):
                        dve.scalar_tensor_tensor(w[:, k, n * D:(n + 1) * D], banks[:, i, k * D:(k + 1) * D], LORA_SCALE,
                                                 w[:, k, n * D:(n + 1) * D], ALU.mult, ALU.add).then_inc(sem("w_ready"), 1)
                def sequence(b, last=False):
                    norm.moments(dve, b * 2 + 1)
                    norm.normalise(dve, b * 2 + 1)
                    for t in range(LAST):
                        if t < Q_TILES:
                            rotate(b, t)
                        if t >= 2:
                            evac(b, t - 2)
                        if 1 <= t <= Q_TILES:
                            remainder(b, t - 1)
                            third_part(b, t - 1)
                    for h in range(2):
                        for i in range(CHUNKS):
                            chunk_max(b, h, h, i)
                        head_max(b, h, h)
                    head_loop(dve, lambda h, hg, j: body(b, h, hg, j))
                    if not last:
                        norm.moments(dve, b * 2 + 2)
                        norm.normalise(dve, b * 2 + 2)
                    for u in range(2):
                        normalise(b, AH // HG - 1, u)
                    for u in range(2):
                        dve.wait_ge(sem("y_ready"), b * 2 + u + 1)
                        at = c.x[:, bass.ds((b * 2 + u) * GT * D, GT * D)]
                        dve.tensor_tensor(at, banks[:, 2 + 2 * u:4 + 2 * u, :].rearrange("p a n -> p (a n)"), at, ALU.add)\
                           .then_inc(sem("y_used"), 1)

                norm.moments(dve, 0)
                norm.normalise(dve, 0, first=True)
                with dve.Fori(0, B - 1) as b:
                    sequence(b)
                sequence(B - 1, last=True)


NH, HDIM = 16, 16
SEQ = B
LIN_SCALE = HDIM ** -0.5 * SEQ ** -0.5


def stage_lin(c):
    nc = c.nc
    with Local(c, "lin") as s:
        norm = Norm(c, s, tile=lambda g, j: j * G + g)
        wT = s.sb("wT", [P, KD, 3 * D])
        bias = s.sb("bias", [P, 3 * D])
        qkv = s.sb("qkv", [P, 2, SEQ, 3, D])
        score = s.sb("score", [P, SEQ, SEQ * NH])
        qk = s.sb("qk", [P, 2, SEQ * D])
        pv = s.sb("pv", [P, SEQ, SEQ * D])
        qp = s.ps("qp", [P, 2, 1024])
        yp = s.ps("yp", [P, SEQ, D])
        loaded, qkv_filled, qkv_copied, biased = s.sem("loaded"), s.sem("qkv_filled"), s.sem("qkv_copied"), s.sem("biased")
        suffix_ready, qk_ready, score_ready = s.sem("suffix_ready"), s.sem("qk_ready"), s.sem("score_ready")
        pv_ready, y_ready, y_used = s.sem("pv_ready"), s.sem("y_ready"), s.sem("y_used")
        COPIED, PV = 2, 2 * SEQ

        def walk(engine, one):
            one(0, 0, False, True, True)
            with engine.Fori(0, (G - 4) // 2) as m:
                one(m * 2 + 1, 1, True, True, True)
                one(m * 2 + 2, 0, True, True, True)
            one(G - 3, 1, True, True, True)
            one(G - 2, 0, True, True, False)
            one(G - 1, 1, True, False, False)

        x4 = c.x[:, :].rearrange("p (q n) -> p q n", q=SEQ)
        with nc.Block() as block:
            @block.sync
            def _(sp):
                sp.dma_start(wT[:, :, :], c.ins["lin_wT"].rearrange("(k p) n -> p k n", p=P)).then_inc(loaded, 16)
                sp.dma_start(bias[:, :], c.ins["lin_b"].to_broadcast((P, 3 * D))).then_inc(loaded, 16)
                load_moe_weights(c, sp)

            @block.tensor
            def _(pe):
                def project(g):
                    pe.wait_ge(norm.xT_ready, g * KD + KD)
                    for j in range(SEQ):
                        pe.wait_ge(qkv_copied, g * SEQ + j + 1)
                        for n, size in ((0, 512), (512, 256)):
                            for k in range(KD):
                                mm = pe.matmul(qp[:, j % 2, n:n + size], norm.xT[:, k, j * P:(j + 1) * P],
                                               wT[:, k, n:n + size], start=(k == 0), stop=(k == KD - 1))
                        mm.then_inc(qkv_filled, 1)

                def sums(g, first=False):
                    for q in range(SEQ):
                        pe.wait_ge(pv_ready, g * SEQ + q + 1 + PV)
                        if q % 2 == 0 and not first:
                            pe.wait_ge(y_used, g * 2 - 1 + q // 2)
                        for t in range(SEQ):
                            mm = pe.matmul(yp[:, q, :], c.ident[:, :], pv[:, q, t * D:(t + 1) * D],
                                           start=(t == 0), stop=(t == SEQ - 1))
                        if q % 2 == 1:
                            mm.then_inc(y_ready, 1)

                norm.transposes(pe, 0, first=True)
                pe.wait_ge(loaded, 32)
                project(0)

                def group(g, slot, before, after, after2):
                    if after:
                        norm.transposes(pe, g + 1)
                        project(g + 1)
                    sums(g, first=not before)

                walk(pe, group)

            @block.gpsimd
            def _(pool):
                norm.pool_prologue(pool)

                def bias_and_suffix(g, slot):
                    for j in range(SEQ):
                        pool.wait_ge(qkv_copied, g * SEQ + j + 1 + COPIED)
                        at = qkv[:, slot, j, :, :].rearrange("p a n -> p (a n)")
                        pool.tensor_tensor(at, at, bias[:, :], ALU.add).then_inc(biased, 1)
                    pool.wait_ge(biased, g * SEQ + SEQ)
                    for i, t in enumerate((2, 1, 0)):
                        pool.tensor_tensor(qkv[:, slot, t, 2, :], qkv[:, slot, t, 2, :], qkv[:, slot, t + 1, 2, :],
                                           ALU.add).then_inc(suffix_ready, 1)
                        if t > 0:
                            pool.wait_ge(suffix_ready, g * 3 + i + 1)

                def group(g, slot, before, after, after2):
                    if after2:
                        norm.power(pool, g + 2)
                    if after:
                        bias_and_suffix(g + 1, 1 - slot)

                norm.power(pool, 0)
                norm.power(pool, 1)
                pool.wait_ge(loaded, 32)
                bias_and_suffix(0, 0)
                walk(pool, group)

            @block.scalar
            def _(act):
                def group(g, slot, before, after, after2):
                    if before:
                        norm.copy_out(act, g, qkv_filled, g * SEQ)
                    else:
                        norm.copy_out(act, g)
                    act.wait_ge(pv_ready, g * SEQ + SEQ)
                    for j in range(SEQ):
                        act.wait_ge(qkv_filled, g * SEQ + j + 1)
                        act.copy(qkv[:, slot, j, :, :].rearrange("p a n -> p (a n)"), qp[:, j % 2, 0:3 * D]).then_inc(qkv_copied, 1)

                act.sem_inc(qkv_copied, COPIED)
                walk(act, group)

            @block.vector
            def _(dve):
                def scores(g, slot, first=False):
                    dve.wait_ge(suffix_ready, g * 3 + 3)
                    for q in range(SEQ + 1):
                        if q < SEQ:
                            if not (first and q < 2):
                                dve.wait_ge(score_ready, g * SEQ + q - 1)
                            dve.tensor_tensor(qk[:, q % 2, :].rearrange("p (t n) -> p t n", t=SEQ),
                                              qkv[:, slot, q, 0, :].unsqueeze(1).to_broadcast((P, SEQ, D)),
                                              qkv[:, slot, :, 1, :], ALU.mult).then_inc(qk_ready, 1)
                        if q > 0:
                            dve.wait_ge(qk_ready, g * SEQ + q)
                            dve.tensor_reduce(score[:, q - 1, :], qk[:, (q - 1) % 2, :].rearrange("p (m d) -> p m d", d=HDIM),
                                              AX.X, ALU.add).then_inc(score_ready, 1)

                def products(g, slot, first=False):
                    dve.wait_ge(score_ready, g * SEQ + SEQ)
                    if not first:
                        dve.wait_ge(y_ready, g * 2)
                    for q in range(SEQ):
                        for t in range(SEQ):
                            last = dve.tensor_tensor(pv[:, q, t * D:(t + 1) * D].rearrange("p (h d) -> p h d", d=HDIM),
                                                     qkv[:, slot, t, 2, :].rearrange("p (h d) -> p h d", d=HDIM),
                                                     score[:, q, t * NH:(t + 1) * NH].unsqueeze(2).to_broadcast((P, NH, HDIM)),
                                                     ALU.mult)
                        last.then_inc(pv_ready, 1)

                def add(g):
                    for i in range(2):
                        dve.wait_ge(y_ready, g * 2 + i + 1)
                        at = x4[:, 2 * i:2 * i + 2, bass.ds(g * D, D)]
                        dve.scalar_tensor_tensor(at, yp[:, 2 * i:2 * i + 2, :], LIN_SCALE, at, ALU.mult,
                                                 ALU.add).then_inc(y_used, 1)

                def group(g, slot, before, after, after2):
                    if after2:
                        norm.moments(dve, g + 2)
                    scores(g, slot, first=not before)
                    if after2:
                        norm.normalise(dve, g + 2)
                    products(g, slot, first=not before)
                    if before:
                        add(g - 1)

                dve.sem_inc(pv_ready, PV)
                norm.moments(dve, 0)
                norm.normalise(dve, 0, first=True)
                norm.moments(dve, 1)
                norm.normalise(dve, 1)
                walk(dve, group)
                add(G - 1)


E = 8
EG = 4
SB_ = 2
MB = E + SB_
ROUTED_SCALE = 2.5


def prepare_moe(c):
    return {"wg": c.keep("moe_wg", [P, KD, MB, P]), "wu": c.keep("moe_wu", [P, KD, MB, P]), "wd": c.keep("moe_wd", [P, MB, D]),
            "wr": c.keep("moe_router", [P, KD, E]), "bias": c.keep("moe_bias", [P, E]), "below": c.keep("moe_below", [P, E * E]),
            "loaded": c.nc.alloc_semaphore("moe_loaded")}


MOE_LOADS = 4 * KD + 5


def load_moe_weights(c, sp):
    w = c.prepared["moe"]
    for k in range(KD):
        f = slice(k * P, (k + 1) * P)
        for t, routed, shared in ((w["wg"], "w_gate", "sw_gate"), (w["wu"], "w_up", "sw_up")):
            sp.dma_start(t[:, k, 0:E, :], c.ins[routed][:, f, :].rearrange("e p i -> p e i")).then_inc(w["loaded"], 16)
            sp.dma_start(t[:, k, E:, :], c.ins[shared][f, :].rearrange("p (b i) -> p b i", i=P)).then_inc(w["loaded"], 16)
    sp.dma_start(w["wd"][:, 0:E, :], c.ins["w_down"].rearrange("e i d -> i e d")).then_inc(w["loaded"], 16)
    sp.dma_start(w["wd"][:, E:, :], c.ins["sw_down"].rearrange("(b i) d -> i b d", i=P)).then_inc(w["loaded"], 16)
    sp.dma_start(w["wr"][:, :, :], c.ins["gate_w"].rearrange("(k p) e -> p k e", p=P)).then_inc(w["loaded"], 16)
    sp.dma_start(w["bias"][:, :], c.ins["gate_bias"].to_broadcast((P, E))).then_inc(w["loaded"], 16)
    sp.dma_start(w["below"][:, :], c.ins["below"]).then_inc(w["loaded"], 16)


def stage_moe(c, name, out=None):
    nc = c.nc
    wg, wu, wd, wr, bias, below, w_loaded = (c.prepared["moe"][n] for n in ("wg", "wu", "wd", "wr", "bias", "below", "loaded"))
    with Local(c, name) as s:
        norm = Norm(c, s)
        xT, trp = norm.xT, norm.trp
        score = s.sb("score", [P, GT, E])
        sfc = s.sb("sfc", [P, GT, E])
        pair = s.sb("pair", [P, GT, EG])
        gt = s.sb("greater", [P, GT, E * E])
        eq = s.sb("equal", [P, GT, E * E])
        rank = s.sb("rank", [P, GT, E])
        tmp = s.sb("masked", [P, GT, E])
        wsum = s.sb("wsum", [P, GT])
        w = s.sb("w", [P, GT, E])
        sg = s.sb("silu", [P, 2, GN])
        prod = s.sb("prod", [P, 2, GN])
        h = s.sb("h", [P, MB, GN])
        hp = s.ps("hp", [P, 4, GN])
        yp = s.ps("yp", [P, GT, D])
        xT_ready = norm.xT_ready
        logits_ready, score_ready, gate_step = s.sem("logits_ready"), s.sem("score_ready"), s.sem("gate_step")
        w_ready, wb_ready = s.sem("w_ready"), s.sem("wb_ready")
        up_filled, silu_ready, prod_ready = s.sem("up_filled"), s.sem("silu_ready"), s.sem("prod_ready")
        h_ready, y_ready, y_used = s.sem("h_ready"), s.sem("y_ready"), s.sem("y_used")
        STEPS = 18
        stored = s.sem("stored")
        with nc.Block() as block:
            if out is not None:
                @block.sync
                def _(sp):
                    def store(g, b, v):
                        sp.wait_ge(y_used, g * 2 + 2)
                        src = c.x[:, bass.ds(g * GT * D, GT * D)].rearrange("p (n d) -> p n d", d=D)
                        dst = out[bass.ds(b, 1), v * GN:(v + 1) * GN, :].rearrange("b (n p) d -> p (b n) d", p=P)
                        sp.dma_start(dst, src).then_inc(stored, 16)

                    with sp.Fori(0, B) as b:
                        for v in range(2):
                            store(b * 2 + v, b, v)
                    sp.wait_ge(stored, 16 * G)

            @block.gpsimd
            def _(pool):
                norm.pool_prologue(pool)
                norm.power(pool, 0)
                with pool.Fori(1, G) as g:
                    norm.power(pool, g)

            @block.tensor
            def _(pe):
                def transposes(g, first=False):
                    if not first:
                        pe.wait_ge(h_ready, g * MB - SB_)
                    norm.transposes(pe, g, first)

                def logits(g, first=False):
                    pe.wait_ge(xT_ready, g * KD + KD)
                    if not first:
                        pe.wait_ge(prod_ready, g * MB)
                    for j in range(GT):
                        for k in range(KD):
                            mm = pe.matmul(hp[:, 0, j * E:(j + 1) * E], xT[:, k, j * P:(j + 1) * P], wr[:, k, :],
                                           start=(k == 0), stop=(k == KD - 1))
                    mm.then_inc(logits_ready, 1)

                def broadcast(g, e):
                    if e == 0:
                        pe.wait_ge(w_ready, g + 1)
                    if e >= 2:
                        pe.wait_ge(h_ready, g * MB + e - 1)
                    for j in range(GT):
                        mm = pe.transpose(trp[:, e % 2, j * P:(j + 1) * P], w[:, j, e:e + 1].to_broadcast((P, P)),
                                          c.ident[:, :])
                    mm.then_inc(wb_ready, 1)

                def ups(g):
                    for b in range(MB):
                        if b == 0:
                            pe.wait_ge(score_ready, g + 1)
                        if b >= 2:
                            pe.wait_ge(prod_ready, g * MB + b - 1)
                        for i, wt in enumerate((wg, wu)):
                            for k in range(KD):
                                mm = pe.matmul(hp[:, 2 * (b % 2) + i, :], wt[:, k, b, :], xT[:, k, :],
                                               start=(k == 0), stop=(k == KD - 1))
                        mm.then_inc(up_filled, 1)
                        if 1 <= b <= E:
                            broadcast(g, b - 1)

                def down(g, first=False):
                    pe.wait_ge(h_ready, g * MB + MB)
                    for j in range(GT):
                        if j % 2 == 0 and not first:
                            pe.wait_ge(y_used, g * 2 - 1 + j // 2)
                        for b in range(MB):
                            mm = pe.matmul(yp[:, j, :], h[:, b, j * P:(j + 1) * P], wd[:, b, :],
                                           start=(b == 0), stop=(b == MB - 1))
                        if j % 2 == 1:
                            mm.then_inc(y_ready, 1)

                transposes(0, first=True)
                pe.wait_ge(w_loaded, 16 * MOE_LOADS)
                logits(0, first=True)
                ups(0)
                transposes(1)
                down(0, first=True)
                logits(1)
                ups(1)
                with pe.Fori(2, G) as g:
                    transposes(g)
                    down(g - 1)
                    logits(g)
                    ups(g)
                down(G - 1)

            @block.scalar
            def _(act):
                def group(g, first=False):
                    if first:
                        norm.copy_out(act, g)
                    else:
                        norm.copy_out(act, g, up_filled, g * MB)
                    act.wait_ge(logits_ready, g + 1)
                    if not first:
                        act.wait_ge(gate_step, g * STEPS)
                    act.activation(score[:, :, :].rearrange("p j e -> p (j e)"), hp[:, 0, 0:GT * E],
                                   ACT.Sigmoid).then_inc(score_ready, 1)
                    for b in range(MB):
                        act.wait_ge(up_filled, g * MB + b + 1)
                        if not (first and b < 2):
                            act.wait_ge(prod_ready, g * MB + b - 1)
                        act.activation(sg[:, b % 2, :], hp[:, 2 * (b % 2), :], ACT.Silu).then_inc(silu_ready, 1)

                group(0, first=True)
                with act.Fori(1, G) as g:
                    group(g)

            @block.vector
            def _(dve):
                def ranks(g, n, values, at):
                    a_, b_ = (gt[:, :, 0:n * n].rearrange("p j (a b) -> p j a b", b=n),
                              eq[:, :, 0:n * n].rearrange("p j (a b) -> p j a b", b=n))
                    tri = below[:, :].rearrange("p (a b) -> p a b", b=E)[:, 0:n, 0:n].unsqueeze(1).to_broadcast((P, GT, n, n))
                    other = values.unsqueeze(2).to_broadcast((P, GT, n, n))
                    mine = values.unsqueeze(3).to_broadcast((P, GT, n, n))
                    dve.tensor_tensor(a_, other, mine, ALU.is_gt).then_inc(gate_step, 1)
                    dve.tensor_tensor(b_, other, mine, ALU.is_equal).then_inc(gate_step, 1)
                    dve.wait_ge(gate_step, g * STEPS + at + 2)
                    for j in range(GT):
                        last = dve.tensor_tensor(b_[:, j], b_[:, j], tri[:, j], ALU.mult)
                    last.then_inc(gate_step, 1)
                    dve.wait_ge(gate_step, g * STEPS + at + 3)
                    dve.tensor_tensor(gt[:, :, 0:n * n], gt[:, :, 0:n * n], eq[:, :, 0:n * n], ALU.add).then_inc(gate_step, 1)
                    dve.wait_ge(gate_step, g * STEPS + at + 4)
                    dve.tensor_reduce(rank[:, :, 0:n], a_, AX.X, ALU.add).then_inc(gate_step, 1)
                    dve.wait_ge(gate_step, g * STEPS + at + 5)

                def gate(g):
                    def step(ins, n):
                        ins.then_inc(gate_step, 1)
                        dve.wait_ge(gate_step, g * STEPS + n)

                    dve.wait_ge(score_ready, g + 1)
                    step(dve.tensor_tensor(sfc[:, :, :], score[:, :, :], bias[:, :].unsqueeze(1).to_broadcast((P, GT, E)),
                                           ALU.add), 1)
                    step(dve.tensor_reduce(pair[:, :, :], sfc[:, :, :].rearrange("p j (a b) -> p j a b", b=2), AX.X,
                                           ALU.add), 2)
                    ranks(g, EG, pair[:, :, :], 2)
                    step(dve.tensor_scalar(pair[:, :, :], rank[:, :, 0:EG], 1.5, None, ALU.is_lt), 8)
                    step(dve.tensor_tensor(tmp[:, :, :].rearrange("p j (a b) -> p j a b", b=2),
                                           sfc[:, :, :].rearrange("p j (a b) -> p j a b", b=2),
                                           pair[:, :, :].unsqueeze(3).to_broadcast((P, GT, EG, 2)), ALU.mult), 9)
                    ranks(g, E, tmp[:, :, :], 9)
                    step(dve.scalar_tensor_tensor(tmp[:, :, :], rank[:, :, :], 1.5, sfc[:, :, :], ALU.is_lt, ALU.mult), 15)
                    step(dve.tensor_reduce(wsum[:, :], tmp[:, :, :], AX.X, ALU.add), 16)
                    step(dve.tensor_scalar(wsum[:, :], wsum[:, :], 1e-20, None, ALU.add), 17)
                    step(dve.reciprocal(wsum[:, :], wsum[:, :]), 18)
                    for j in range(GT):
                        last = dve.tensor_scalar(w[:, j, :], tmp[:, j, :], wsum[:, j:j + 1], ROUTED_SCALE, ALU.mult, ALU.mult)
                    last.then_inc(w_ready, 1)

                def blocks(g, first=False, last=False):
                    for b in range(MB):
                        if b == 3 and not last:
                            norm.normalise(dve, g + 1)
                        dve.wait_ge(silu_ready, g * MB + b + 1)
                        if b == 0 and not first:
                            dve.wait_ge(y_ready, g * 2)
                        up = hp[:, 2 * (b % 2) + 1, :]
                        if b >= E:
                            dve.tensor_tensor(h[:, b, :], up, sg[:, b % 2, :], ALU.mult).then_inc(prod_ready, 1)
                            dve.wait_ge(prod_ready, g * MB + b + 1)
                            dve.sem_inc(h_ready, 1)
                            continue
                        if b >= 2 or not first:
                            dve.wait_ge(h_ready, g * MB + max(b - 1, 0))
                        dve.tensor_tensor(prod[:, b % 2, :], up, sg[:, b % 2, :], ALU.mult).then_inc(prod_ready, 1)
                        dve.wait_ge(prod_ready, g * MB + b + 1)
                        dve.wait_ge(wb_ready, g * E + b + 1)
                        dve.tensor_tensor(h[:, b, :], trp[:, b % 2, :], prod[:, b % 2, :], ALU.mult).then_inc(h_ready, 1)

                def add(g):
                    for i in range(2):
                        dve.wait_ge(y_ready, g * 2 + i + 1)
                        at = c.x_pair(g * 2 + i)
                        dve.tensor_tensor(at, yp[:, 2 * i:2 * i + 2, :].rearrange("p a n -> p (a n)"), at,
                                          ALU.add).then_inc(y_used, 1)

                norm.moments(dve, 0)
                norm.normalise(dve, 0, first=True)
                norm.moments(dve, 1)
                dve.wait_ge(w_loaded, 16 * MOE_LOADS)
                gate(0)
                blocks(0, first=True)
                with dve.Fori(1, G - 1) as g:
                    norm.moments(dve, g + 1)
                    add(g - 1)
                    gate(g)
                    blocks(g)
                add(G - 2)
                gate(G - 1)
                blocks(G - 1, last=True)
                add(G - 1)


MH, MD = 16, 16
SET = P // MH
SETS = GN // SET
QUAD = 4
STACK = P // MD
HALF = SETS // 2


def mix_project(c, z, scr, stored, qz, cleared):
    nc = c.nc
    with Local(c, "mixA") as s:
        norm = TwiceNorm(c, s)
        w0 = s.sb("w0", [P, KD, 3 * D])
        w = s.sb("w", [P, KD, 3 * D])
        b0 = s.sb("b0", [P, 3 * D])
        bias = s.sb("bias", [P, 3 * D])
        ln = s.sb("ln", [P, KD, 4])
        qkv = s.sb("qkv", [P, GT, 3 * D])
        low = s.sb("low", [P, GT, 2 * D])
        expo = s.sb("expo", [P, GT, 2 * D])
        qp = s.ps("qp", [P, 2, 1024])
        loaded, w_ready, biasp_ready, bias_ready = s.sem("loaded"), s.sem("w_ready"), s.sem("biasp_ready"), s.sem("bias_ready")
        qkv_filled, qkv_biased, low_ready, exp_ready, qkv_ready = (s.sem("qkv_filled"), s.sem("qkv_biased"), s.sem("low_ready"),
                                                                   s.sem("exp_ready"), s.sem("qkv_ready"))
        with nc.Block() as block:
            @block.sync
            def _(sp):
                sp.dma_start(w0[:, :, :], c.ins["mix_wT"].rearrange("(k p) n -> p k n", p=P)).then_inc(loaded, 16)
                sp.dma_start(b0[:, :], c.ins["mix_b"].to_broadcast((P, 3 * D))).then_inc(loaded, 16)
                sp.dma_start(ln[:, :, :], c.ins["mix_ln"].rearrange("(k p) n -> p k n", p=P)).then_inc(loaded, 16)
                with sp.Fori(0, G) as g:
                    sp.wait_ge(qkv_ready, g * GT + GT)
                    for i in range(3):
                        sp.dma_start(scr[i, bass.ds(g * GN, GN), :].rearrange("(j p) d -> p j d", p=P),
                                     qkv[:, :, i * D:(i + 1) * D]).then_inc(stored, 16)
                sp.wait_ge(stored, 48 * G)

            @block.tensor
            def _(pe):
                def project(g, first=False):
                    pe.wait_ge(norm.xT_ready, g * KD + KD)
                    for j in range(GT):
                        if not (first and j < 2):
                            pe.wait_ge(qkv_biased, g * GT + j - 1)
                        for n, size in ((0, 512), (512, 256)):
                            for k in range(KD):
                                mm = pe.matmul(qp[:, j % 2, n:n + size], norm.xT[:, k, j * P:(j + 1) * P],
                                               w[:, k, n:n + size], start=(k == 0), stop=(k == KD - 1))
                        mm.then_inc(qkv_filled, 1)

                pe.wait_ge(loaded, 48)
                for n, size in ((0, 512), (512, 256)):
                    for k in range(KD):
                        mm = pe.matmul(qp[:, 0, n:n + size], ln[:, k, 1:2].to_broadcast((P, P)), w0[:, k, n:n + size],
                                       start=(k == 0), stop=(k == KD - 1))
                mm.then_inc(biasp_ready, 1)
                norm.transposes(pe, 0, first=True)
                pe.wait_ge(bias_ready, 1)
                pe.wait_ge(w_ready, KD)
                project(0, first=True)
                with pe.Fori(1, G) as g:
                    norm.transposes(pe, g)
                    project(g)

            @block.gpsimd
            def _(pool):
                norm.pool_prologue(pool)
                norm.power(pool, 0)
                norm.power(pool, 1)
                for slot in range(2):
                    pool.memset(qz[:, slot, :, :, :].rearrange("p a i n -> p (a i n)"), 0.0).then_inc(cleared, 1)
                with pool.Fori(2, G) as g:
                    norm.power(pool, g)

            @block.scalar
            def _(act):
                def exps(g, first=False):
                    for j in range(GT):
                        act.wait_ge(low_ready, g * GT + j + 1)
                        if not first:
                            act.wait_ge(qkv_ready, g * GT - GT + j + 1)
                        act.activation(expo[:, j, :], low[:, j, :], ACT.Exp).then_inc(exp_ready, 1)

                norm.copy_out(act, 0)
                exps(0, first=True)
                with act.Fori(1, G) as g:
                    norm.copy_out(act, g, qkv_filled, g * GT)
                    exps(g)

            @block.vector
            def _(dve):
                def take(g, first=False):
                    if not first:
                        dve.wait_ge(stored, g * 48)
                        dve.wait_ge(exp_ready, g * GT)
                    for j in range(GT):
                        dve.wait_ge(qkv_filled, g * GT + j + 1)
                        dve.tensor_tensor(qkv[:, j, :], qp[:, j % 2, 0:3 * D], bias[:, :], ALU.add).then_inc(qkv_biased, 1)
                    for j in range(GT):
                        dve.wait_ge(qkv_biased, g * GT + j + 1)
                        dve.tensor_scalar(low[:, j, :], qkv[:, j, 0:2 * D], 0.0, None, ALU.min).then_inc(low_ready, 1)

                def elu(g):
                    for j in range(GT):
                        dve.wait_ge(exp_ready, g * GT + j + 1)
                        dve.scalar_tensor_tensor(qkv[:, j, 0:2 * D], qkv[:, j, 0:2 * D], 0.0, expo[:, j, :], ALU.max,
                                                 ALU.add).then_inc(qkv_ready, 1)

                def z_tiles(g):
                    return lambda j: z[:, bass.ds((g * GT + j) * D, D)]

                norm.moments(dve, 0)
                dve.wait_ge(loaded, 48)
                for k in range(KD):
                    dve.tensor_scalar(w[:, k, :], w0[:, k, :], ln[:, k, 0:1], None, ALU.mult).then_inc(w_ready, 1)
                norm.normalise(dve, 0, z_tiles(0), first=True)
                dve.wait_ge(biasp_ready, 1)
                dve.tensor_tensor(bias[:, :], qp[:, 0, 0:3 * D], b0[:, :], ALU.add).then_inc(bias_ready, 1)
                dve.wait_ge(bias_ready, 1)
                norm.moments(dve, 1)
                norm.normalise(dve, 1, z_tiles(1))
                take(0, first=True)
                elu(0)
                with dve.Fori(1, G - 1) as g:
                    norm.moments(dve, g + 1)
                    norm.normalise(dve, g + 1, z_tiles(g + 1))
                    take(g)
                    elu(g)
                take(G - 1)
                elu(G - 1)


def load_finish_weights(c, sp, fw):
    for dst, src in ((fw["wo"][:, :, :], c.ins["mix_oT"].rearrange("(k p) n -> p k n", p=P)),
                     (fw["ob"][:, :], c.ins["mix_ob"].to_broadcast((P, D))),
                     (fw["ln"][:, :, :], c.ins["mix_ln"].rearrange("(k p) n -> p k n", p=P)),
                     (fw["fc"][:, :, :], c.ins["mix_fcT"].rearrange("(k p) n -> p k n", p=P)),
                     (fw["fcb0"][:, :], c.ins["mix_fcb"]),
                     (fw["wp"][:, :, :], c.ins["mix_pT"].rearrange("(b p) n -> p b n", p=P)),
                     (fw["pb"][:, :], c.ins["mix_pb"].to_broadcast((P, D)))):
        sp.dma_start(dst, src).then_inc(fw["loaded"], 16)


def mix_heads(c, scr, scr_o, stored_o, qz, cleared, fw):
    nc = c.nc
    with Local(c, "mixB") as s:
        NHALF = T // SET // HALF
        kh = s.sb("kh", [P, 2, HALF, MD])
        vh = s.sb("vh", [P, 2, HALF, MD])
        ve = s.sb("v_one", [P, 2, HALF, MD + 1])
        mask = s.sb("mask", [P, P])
        kT = s.sb("kT", [P, 2, HALF // STACK, P])
        qT = s.sb("qT", [P, 2, QUAD, P])
        sm = s.sb("sm", [P, 2, QUAD, P])
        rec = s.sb("rec", [P, 2, HALF])
        oh = s.sb("oh", [P, 2, HALF, MD])
        ktp = s.ps("ktp", [P, HALF // STACK, P])
        qtp = s.ps("qtp", [P, 2, QUAD, P])
        sp_ = s.ps("sp", [P, 2, QUAD, P])
        op = s.ps("op", [P, 2, 512])
        OB = 16
        QH = HALF // QUAD
        mask_loaded = s.sem("mask_loaded")
        loaded = [s.sem("loaded_even"), s.sem("loaded_odd")]
        v_ready, kt_filled, kt_ready = s.sem("v_ready"), s.sem("kt_filled"), s.sem("kt_ready")
        qt_filled, qt_ready, s_filled, s_ready = s.sem("qt_filled"), s.sem("qt_ready"), s.sem("s_filled"), s.sem("s_ready")
        pv_done, rec_ready, o_ready = s.sem("pv_done"), s.sem("rec_ready"), s.sem("o_ready")
        LOAD = 16 * (HALF // STACK + 2)

        def in_dram(which, n):
            return which[bass.ds(n * HALF * SET, HALF * SET), :].rearrange("(a t) (h d) -> (t h) a d", t=SET, d=MD)

        with nc.Block() as block:
            @block.sync
            def _(sp):
                def load(n, slot, first=False):
                    if not first:
                        sp.wait_ge(qt_filled, (n - 1) * QH)
                        sp.wait_ge(v_ready, n - 1)
                    for a in range(HALF // STACK):
                        src = scr[0, bass.ds(n * HALF * SET + a * STACK * SET, STACK * SET), :]
                        src = src.rearrange("(a t) (h d) -> (t h) a d", t=SET, d=MD)
                        dst = qz[:, slot, a, :, :].rearrange("p i n -> p (i n)")[:, 0:STACK * P]
                        sp.dma_start(diagonal(dst), src).then_inc(loaded[slot], 16)
                    sp.dma_start(kh[:, slot, :, :], in_dram(scr[1], n)).then_inc(loaded[slot], 16)
                    sp.dma_start(vh[:, slot, :, :], in_dram(scr[2], n)).then_inc(loaded[slot], 16)

                def diagonal(block_):
                    step = P + MD
                    whole = block_
                    ap = whole[:, 0:(STACK - 1) * step + MD]
                    return bass.AP(tensor=ap.tensor, offset=ap.offset, ap=[list(ap.ap[0]), [step, STACK], [1, MD]])

                def store(n, slot):
                    sp.wait_ge(o_ready, n * 2 + 2)
                    sp.dma_start(in_dram(scr_o, n), oh[:, slot, :, :]).then_inc(stored_o, 16)

                sp.dma_start(mask[:, :], c.ins["token_mask"]).then_inc(mask_loaded, 16)
                sp.wait_ge(cleared, 2)
                load(0, 0, first=True)
                load(1, 1, first=True)
                load_finish_weights(c, sp, fw)
                with sp.Fori(0, NHALF // 2 - 1) as m:
                    for slot in range(2):
                        store(m * 2 + slot, slot)
                        load(m * 2 + slot + 2, slot)
                store(NHALF - 2, 0)
                store(NHALF - 1, 1)
                sp.wait_ge(stored_o, 16 * NHALF)

            @block.tensor
            def _(pe):
                def queries(n, slot, i, first=False):
                    if not (first and i < 2):
                        pe.wait_ge(qt_ready, n * QH + i - 1)
                    for m in range(QUAD):
                        at = QUAD * i + m
                        mm = pe.transpose(qtp[:, i % 2, m, :], qz[:, slot, at // STACK, at % STACK, :], c.ident[:, :])
                    mm.then_inc(qt_filled, 1)

                def half(n, slot, first=False):
                    pe.wait_ge(loaded[slot], (n - slot) * (LOAD // 2) + LOAD)
                    if not first:
                        pe.wait_ge(kt_ready, n)
                    for a in range(HALF // STACK):
                        mm = pe.transpose(ktp[:, a, :], kh[:, slot, a * STACK:(a + 1) * STACK, :].rearrange("p a d -> p (a d)"),
                                          c.ident[:, :])
                    mm.then_inc(kt_filled, 1)
                    queries(n, slot, 0, first)
                    queries(n, slot, 1, first)
                    for i in range(QH + 1):
                        if i < QH:
                            if i == 0:
                                pe.wait_ge(kt_ready, n + 1)
                            pe.wait_ge(qt_ready, n * QH + i + 1)
                            if not (first and i < 2):
                                pe.wait_ge(s_ready, n * QH + i - 1)
                            pe.matmul(sp_[:, i % 2, :, :].rearrange("p m n -> p (m n)"), kT[:, slot, i * QUAD // STACK, :],
                                      qT[:, i % 2, :, :].rearrange("p m n -> p (m n)"), start=True,
                                      stop=True).then_inc(s_filled, 1)
                            if i + 2 < QH:
                                queries(n, slot, i + 2)
                        if i > 0:
                            q = i - 1
                            pe.wait_ge(s_ready, n * QH + q + 1)
                            if q == 0:
                                pe.wait_ge(v_ready, n + 1)
                            if q % (QH // 2) == 0 and not first:
                                pe.wait_ge(o_ready, n * 2 - 1 + q // (QH // 2))
                            for m in range(QUAD):
                                at = QUAD * q + m
                                mm = pe.matmul(op[:, at // OB, (at % OB) * (MD + 1):(at % OB + 1) * (MD + 1)],
                                               sm[:, q % 2, m, :], ve[:, slot, at, :], start=True, stop=True)
                            mm.then_inc(pv_done, 1)

                half(0, 0, first=True)
                half(1, 1)
                with pe.Fori(1, NHALF // 2) as m:
                    half(m * 2, 0)
                    half(m * 2 + 1, 1)

            @block.scalar
            def _(act):
                def half(n, slot, first=False):
                    act.wait_ge(kt_filled, n + 1)
                    act.copy(kT[:, slot, :, :].rearrange("p a n -> p (a n)"),
                             ktp[:, :, :].rearrange("p a n -> p (a n)")).then_inc(kt_ready, 1)
                    for i in range(QH):
                        act.wait_ge(qt_filled, n * QH + i + 1)
                        if not (first and i < 2):
                            act.wait_ge(s_filled, n * QH + i - 1)
                        act.copy(qT[:, i % 2, :, :].rearrange("p m n -> p (m n)"),
                                 qtp[:, i % 2, :, :].rearrange("p m n -> p (m n)")).then_inc(qt_ready, 1)

                half(0, 0, first=True)
                half(1, 1)
                with act.Fori(1, NHALF // 2) as m:
                    half(m * 2, 0)
                    half(m * 2 + 1, 1)

            @block.vector
            def _(dve):
                def normalise(n, slot, i, early):
                    dve.wait_ge(pv_done, n * QH + (i + 1) * (QH // 2))
                    if i == 0 and not early:
                        dve.wait_ge(stored_o, (n - 1) * 16)
                    o = op[:, i, 0:OB * (MD + 1)].rearrange("p (a d) -> p a d", d=MD + 1)
                    dve.reciprocal(rec[:, slot, i * OB:(i + 1) * OB], o[:, :, MD]).then_inc(rec_ready, 1)
                    dve.wait_ge(rec_ready, n * 2 + i + 1)
                    dve.tensor_tensor(oh[:, slot, i * OB:(i + 1) * OB, :], o[:, :, 0:MD],
                                      rec[:, slot, i * OB:(i + 1) * OB].unsqueeze(2).to_broadcast((P, OB, MD)),
                                      ALU.mult).then_inc(o_ready, 1)

                def half(n, slot, first=False, early=False):
                    dve.wait_ge(loaded[slot], (n - slot) * (LOAD // 2) + LOAD)
                    dve.tensor_copy(ve[:, slot, :, 0:MD], vh[:, slot, :, :]).then_inc(v_ready, 1)
                    for i in range(QH):
                        dve.wait_ge(s_filled, n * QH + i + 1)
                        if i >= 2 and i - 2 == QH // 2 - 1:
                            normalise(n, slot, 0, early)
                        if not (first and i < 2):
                            dve.wait_ge(pv_done, n * QH + i - 1)
                        dve.tensor_tensor(sm[:, i % 2, :, :], sp_[:, i % 2, :, :],
                                          mask[:, :].unsqueeze(1).to_broadcast((P, QUAD, P)), ALU.mult).then_inc(s_ready, 1)
                    normalise(n, slot, 1, early)

                for slot in range(2):
                    last = dve.memset(ve[:, slot, :, MD:MD + 1], 1.0)
                dve.wait_ge(mask_loaded, 16)
                half(0, 0, first=True, early=True)
                half(1, 1, early=True)
                with dve.Fori(1, NHALF // 2) as m:
                    half(m * 2, 0)
                    half(m * 2 + 1, 1)


def mix_finish(c, z, scr_o, fw):
    nc = c.nc
    with Local(c, "mixC") as s:
        norm = Norm(c, s)
        za, xT, trp = s.sb("za", [P, GT, D]), norm.xT, norm.trp
        ot = s.sb("ot", [P, GT, D])
        oT = s.sb("oT", [P, KD, GN])
        wo, ob, ln, fc, fcb0, wp, pb, loaded = (fw[n] for n in ("wo", "ob", "ln", "fc", "fcb0", "wp", "pb", "loaded"))
        fcb = s.sb("fcb", [P, HB])
        h = s.sb("h", [P, HB, GN])
        hp = s.ps("hp", [P, 4, GN])
        yp = s.ps("yp", [P, GT, D])
        o_loaded, biasp_ready, fcb_ready, fc_ready = s.sem("o_loaded"), s.sem("biasp_ready"), s.sem("fcb_ready"), s.sem("fc_ready")
        ot_used, oT_ready, a_ready, za_step = s.sem("ot_used"), s.sem("oT_ready"), s.sem("a_ready"), s.sem("za_step")
        xb_ready = s.sem("xb_ready")
        h_filled, h_ready, y_ready, y_used = s.sem("h_filled"), s.sem("h_ready"), s.sem("y_ready"), s.sem("y_used")
        ZA = 4

        def flat(t):
            return t.rearrange("p a n -> p (a n)")

        with nc.Block() as block:
            @block.sync
            def _(sp):
                def load(g, first=False):
                    if not first:
                        sp.wait_ge(ot_used, g)
                    sp.dma_start(ot[:, :, :], scr_o[bass.ds(g * GN, GN), :].rearrange("(j p) d -> p j d", p=P)).then_inc(o_loaded, 16)

                load(0, first=True)
                with sp.Fori(1, G) as g:
                    load(g)

            @block.gpsimd
            def _(pool):
                norm.pool_prologue(pool)
                norm.power(pool, 0)
                with pool.Fori(1, G) as g:
                    norm.power(pool, g)

            @block.tensor
            def _(pe):
                def turn(g, first=False):
                    pe.wait_ge(o_loaded, g * 16 + 16)
                    if not first:
                        pe.wait_ge(norm.xT_ready, g * KD)
                    for k in range(KD):
                        for j in range(GT):
                            mm = pe.transpose(trp[:, k, j * P:(j + 1) * P], ot[:, j, k * P:(k + 1) * P], c.ident[:, :])
                    mm.then_inc(ot_used, 1)

                def project(g):
                    pe.wait_ge(oT_ready, g * KD + KD)
                    for j in range(GT):
                        if j % 2 == 0 and not (isinstance(g, int) and g < 2):
                            pe.wait_ge(y_used, g * 2 - 3 + j // 2)
                        for k in range(KD):
                            mm = pe.matmul(yp[:, j, :], oT[:, k, j * P:(j + 1) * P], wo[:, k, :],
                                           start=(k == 0), stop=(k == KD - 1))
                    mm.then_inc(a_ready, 1)

                def normed(g):
                    pe.wait_ge(oT_ready, g * KD + KD)
                    norm.transposes(pe, g, first=True)

                def group(g, first=False, last=False):
                    pe.wait_ge(norm.xT_ready, g * KD + KD)
                    for b in range(HB):
                        if b == 2 and not last:
                            turn(g + 1)
                        if b == 4 and not last:
                            project(g + 1)
                        if not (first and b < 4):
                            pe.wait_ge(h_ready, g * HB + b - 3)
                        for k in range(KD):
                            mm = pe.matmul(hp[:, b % 4, :], fc[:, k, b * P:(b + 1) * P], xT[:, k, :],
                                           start=(k == 0), stop=(k == KD - 1))
                        mm.then_inc(h_filled, 1)
                    pe.wait_ge(h_ready, g * HB + HB)
                    for j in range(GT):
                        if j % 2 == 0:
                            if last:
                                pe.wait_ge(y_used, g * 2 - 1 + j // 2)
                            else:
                                pe.wait_ge(za_step, (g + 1) * ZA + 1 + j // 2)
                        for b in range(HB):
                            mm = pe.matmul(yp[:, j, :], h[:, b, j * P:(j + 1) * P], wp[:, b, :],
                                           start=(b == 0), stop=(b == HB - 1))
                        if j % 2 == 1:
                            mm.then_inc(y_ready, 1)
                        if j == 1 and not last:
                            normed(g + 1)

                pe.wait_ge(loaded, 112)
                for b in range(HB):
                    for k in range(KD):
                        mm = pe.matmul(hp[:, 0, b:b + 1], fc[:, k, b * P:(b + 1) * P], ln[:, k, 3:4],
                                       start=(k == 0), stop=(k == KD - 1))
                mm.then_inc(biasp_ready, 1)
                turn(0, first=True)
                project(0)
                normed(0)
                pe.wait_ge(fc_ready, KD)
                pe.wait_ge(fcb_ready, 1)
                group(0, first=True)
                with pe.Fori(1, G - 1) as g:
                    group(g)
                group(G - 1, last=True)

            @block.scalar
            def _(act):
                def turned(g, first=False):
                    act.wait_ge(ot_used, g + 1)
                    if not first:
                        act.wait_ge(a_ready, g)
                    for k in range(KD):
                        act.copy(oT[:, k, :], trp[:, k, :]).then_inc(oT_ready, 1)

                def group(g, first=False, last=False):
                    if first:
                        norm.copy_out(act, g)
                    else:
                        norm.copy_out(act, g, h_filled, g * HB)
                    for b in range(HB):
                        if b == 2 and not last:
                            turned(g + 1)
                        act.wait_ge(h_filled, g * HB + b + 1)
                        if b == 0 and not first:
                            act.wait_ge(y_ready, g * 2)
                        act.activation(h[:, b, :], hp[:, b % 4, :], ACT.Gelu, bias=fcb[:, b:b + 1]).then_inc(h_ready, 1)

                turned(0, first=True)
                act.wait_ge(fcb_ready, 1)
                group(0, first=True)
                with act.Fori(1, G - 1) as g:
                    group(g)
                group(G - 1, last=True)

            @block.vector
            def _(dve):
                def attend(g, first=False):
                    dve.wait_ge(a_ready, g + 1)
                    if not first:
                        dve.wait_ge(norm.xn_ready, g * GT)
                    for i in range(2):
                        dve.tensor_tensor(flat(za[:, 2 * i:2 * i + 2, :]), flat(yp[:, 2 * i:2 * i + 2, :]),
                                          z[:, bass.ds(g * GT * D + i * 2 * D, 2 * D)], ALU.add).then_inc(za_step, 1)
                    dve.wait_ge(za_step, g * ZA + 2)
                    dve.tensor_tensor(za[:, :, :], za[:, :, :], ob[:, :].unsqueeze(1).to_broadcast((P, GT, D)),
                                      ALU.add).then_inc(za_step, 1)
                    dve.wait_ge(za_step, g * ZA + 3)
                    for j in range(GT):
                        dve.bn_stats(norm.st[:, j, :], za[:, j, :]).then_inc(norm.stats_ready, 1)
                    dve.wait_ge(norm.stats_ready, g * GT + GT)
                    dve.sem_inc(norm.stats_seen, 1)
                    for j in range(GT):
                        dve.bn_aggr(norm.mv[:, j, :], norm.st[:, j, :]).then_inc(norm.moments_ready, 1)
                    xg = c.x[:, bass.ds(g * GT * D, GT * D)]
                    dve.tensor_tensor(xg, flat(za[:, :, :]), xg, ALU.add).then_inc(za_step, 1)
                    dve.wait_ge(norm.rstd_ready, g + 1)
                    if not first:
                        dve.wait_ge(norm.xn_used, g)
                    for j in range(GT):
                        dve.tensor_scalar(norm.xn[:, j, :], za[:, j, :], norm.mv[:, j, 0:1], norm.rstd[:, j:j + 1],
                                          ALU.subtract, ALU.mult).then_inc(norm.xn_ready, 1)

                def add(g):
                    dve.wait_ge(za_step, g * ZA + 4)
                    xg = c.x[:, bass.ds(g * GT * D, GT * D)]
                    xg3 = xg.rearrange("p (j d) -> p j d", d=D)
                    dve.tensor_tensor(xg3, xg3, pb[:, :].unsqueeze(1).to_broadcast((P, GT, D)), ALU.add).then_inc(xb_ready, 1)
                    dve.wait_ge(xb_ready, g + 1)
                    for i in range(2):
                        dve.wait_ge(y_ready, g * 2 + i + 1)
                        at = c.x_pair(g * 2 + i)
                        dve.tensor_tensor(at, flat(yp[:, 2 * i:2 * i + 2, :]), at, ALU.add).then_inc(y_used, 1)

                dve.wait_ge(biasp_ready, 1)
                for k in range(KD):
                    dve.tensor_scalar(fc[:, k, :], fc[:, k, :], ln[:, k, 2:3], None, ALU.mult).then_inc(fc_ready, 1)
                dve.tensor_tensor(fcb[:, :], hp[:, 0, 0:HB], fcb0[:, :], ALU.add).then_inc(fcb_ready, 1)
                attend(0, first=True)
                attend(1)
                add(0)
                with dve.Fori(1, G - 1) as g:
                    attend(g + 1)
                    add(g)
                add(G - 1)


def stage_mix(c):
    nc = c.nc
    scr = nc.dram_tensor("mix_qkv", (3, T, D), F32, kind="Internal").ap()
    scr_o = nc.dram_tensor("mix_out", (T, D), F32, kind="Internal").ap()
    with Local(c, "mix") as s:
        z = s.sb("z", [P, TILES * D])
        stored, stored_o = s.sem("stored"), s.sem("stored_o")
        qz, cleared = s.sb("qz", [P, 2, HALF // STACK, STACK, P]), s.sem("cleared")
        mix_project(c, z, scr, stored, qz, cleared)
        with Local(c, "mixW") as s2:
            fw = {"wo": s2.sb("wo", [P, KD, D]), "ob": s2.sb("ob", [P, D]), "ln": s2.sb("ln", [P, KD, 4]),
                  "fc": s2.sb("fc", [P, KD, HID]), "fcb0": s2.sb("fcb0", [P, HB]), "wp": s2.sb("wp", [P, HB, D]),
                  "pb": s2.sb("pb", [P, D]), "loaded": s2.sem("loaded")}
            mix_heads(c, scr, scr_o, stored_o, qz, cleared, fw)
            mix_finish(c, z, scr_o, fw)


def load_x(c, x_in, ident_in):
    with c.nc.Block() as block:
        @block.sync
        def _(sp):
            def load(q, at, n):
                sp.dma_start(c.x[:, (q * 8 + at) * D:(q * 8 + at + n) * D].rearrange("p (n d) -> p n d", d=D),
                             x_in[q, at * P:(at + n) * P, :].rearrange("(n p) d -> p n d", p=P))\
                  .then_inc(c.x_loaded[0 if (q, at) == (0, 0) else 1], 16)

            load(0, 0, GT)
            sp.dma_start(c.ident[:, :], ident_in).then_inc(c.x_loaded[2], 16)
            load(0, GT, GT)
            for q in range(1, B):
                load(q, 0, 2 * GT)


def build(nc, ins, out):
    with ExitStack() as stack:
        c = Ctx(nc, ins, stack)
        load_x(c, ins["x"], ins["ident"])
        stage_mamba(c)
        prepare_ffn(c)
        stage_ffn(c, "ffn1")
        stage_attn(c)
        stage_ffn(c, "ffn2")
        c.prepared["moe"] = prepare_moe(c)
        stage_lin(c)
        stage_moe(c, "moe1")
        stage_mix(c)
        stage_moe(c, "moe2", out)


def host_constants():
    out = {"ident": np.eye(P, dtype=np.float32)}
    theta = (np.arange(L, dtype=np.float32)[:, None]
             / np.float32(10000.0) ** (np.arange(0, 16, 2, dtype=np.float32) / 16)[None, :]).astype(np.float32)
    cos, sin = np.cos(theta.astype(np.float64)), np.sin(theta.astype(np.float64))
    rope = np.stack([np.repeat(cos, 2, axis=1), np.stack([-sin, sin], axis=-1).reshape(L, 16)], axis=1)
    out["rope"] = rope.astype(np.float32).reshape(L // P, P, 32).transpose(1, 0, 2)
    later = np.triu(np.full((P, P), -1e9, np.float32), k=1)
    out["causal"] = np.stack([later, later.T, np.eye(P, dtype=np.float32)], axis=1)
    out["below"] = np.tile((np.arange(8)[None, :] < np.arange(8)[:, None]).astype(np.float32).reshape(1, 64), (P, 1))
    out["token_mask"] = np.kron(np.eye(8, dtype=np.float32), np.ones((16, 16), np.float32))
    return out


def host_layouts(a):
    def t(w):
        return np.ascontiguousarray(np.swapaxes(np.asarray(w), -1, -2))
    out = {"x": np.asarray(a["L0_attn_a_x"])}
    out["w_fc"] = np.asarray(a["L0_ffn_w_fc"])
    out["w_proj"] = np.asarray(a["L0_ffn_w_proj"])
    out["uT"] = t(a["L0_ffn_u"])
    out["v"] = np.asarray(a["L0_ffn_v"])
    out["fast_b"] = np.asarray(a["L0_ffn_fast_b"])
    out["gate"] = np.asarray(a["L0_ffn_gate"]).reshape(1, 1)
    m = {n: np.asarray(a["L0_attn_a_" + n]) for n in
         ("norm_w", "in_proj_w", "conv_w", "conv_b", "x_proj_w", "dt_proj_w", "dt_proj_b", "A_log", "D_param", "out_proj_w")}
    out["mb_inT"] = t(m["in_proj_w"])
    out["mb_norm"] = m["norm_w"].reshape(KD, P).T
    chan = np.concatenate([m["conv_w"].reshape(-1, 4), m["conv_b"][:, None], m["dt_proj_b"][:, None], m["D_param"][:, None]], axis=1)
    out["mb_chan"] = chan.reshape(4, P, 7).transpose(1, 0, 2)
    out["mb_alog"] = m["A_log"].reshape(4, P, 16).transpose(1, 0, 2)
    out["mb_xpT"] = t(m["x_proj_w"])
    out["mb_dtT"] = t(m["dt_proj_w"])
    out["mb_outT"] = t(m["out_proj_w"])
    for n in ("wq", "wk", "wv", "wo", "Bq", "Bv"):
        out["attn_" + n] = np.asarray(a["L0_attn_b_" + n])
    out["attn_AqT"], out["attn_AvT"] = t(a["L0_attn_b_Aq"]), t(a["L0_attn_b_Av"])
    out["lin_wT"] = t(np.asarray(a["L1_attn_a_W_qkv"]).reshape(16, 3, 16, D).transpose(1, 0, 2, 3).reshape(3 * D, D))
    out["lin_b"] = np.asarray(a["L1_attn_a_b_qkv"]).reshape(16, 3, 16).transpose(1, 0, 2).reshape(1, 3 * D)
    out["gate_w"] = np.asarray(a["L1_ffn_gate_w"])
    out["gate_bias"] = np.asarray(a["L1_ffn_gate_bias"]).reshape(1, -1)
    for n in ("w_gate", "w_up", "w_down", "sw_gate", "sw_up", "sw_down"):
        out[n] = np.asarray(a["L1_ffn_" + n])
    m = {n: np.asarray(a["L1_attn_b_" + n]) for n in
         ("ln1_w", "ln1_b", "q_w", "q_b", "k_w", "k_b", "v_w", "v_b", "o_w", "o_b", "ln2_w", "ln2_b", "fc_w", "fc_b", "proj_w", "proj_b")}
    out["mix_wT"] = t(np.concatenate([m["q_w"], m["k_w"], m["v_w"]], axis=0))
    out["mix_b"] = np.concatenate([m["q_b"], m["k_b"], m["v_b"]]).reshape(1, 3 * D)
    out["mix_ln"] = np.stack([m["ln1_w"], m["ln1_b"], m["ln2_w"], m["ln2_b"]], axis=1)
    out["mix_oT"] = t(m["o_w"])
    out["mix_ob"] = m["o_b"].reshape(1, D)
    out["mix_fcT"] = t(m["fc_w"])
    out["mix_fcb"] = t(m["fc_b"].reshape(HB, P))
    out["mix_pT"] = t(m["proj_w"])
    out["mix_pb"] = m["proj_b"].reshape(1, D)
    return out


def kernel(**inputs):
    import concourse.bacc as _bacc
    from concourse.bass_utils import run_bass_kernel_spmd as _run

    nc = _bacc.Bacc("TRN2", target_bir_lowering=False, num_devices=1)
    arrays, ins = {}, {}
    for name, a in {**host_layouts(inputs), **host_constants()}.items():
        a = np.ascontiguousarray(a)
        arrays[f"in_{name}_dram"] = a
        ins[name] = nc.dram_tensor(f"in_{name}_dram", a.shape, mybir.dt.from_np(a.dtype), kind="ExternalInput").ap()
    out = nc.dram_tensor("out_dram", (B, L, D), F32, kind="ExternalOutput").ap()
    build(nc, ins, out)
    r = _run(nc, [arrays], core_ids=[0])
    return r.results[0]["out_dram"]
```
